# Optimizing a Trainium2 kernel written in Bass

```python
import numpy as np
import jax
import jax.numpy as jnp

def _softmax(x, axis=-1):
    return jax.nn.softmax(x, axis=axis)

def _gelu(x):
    return jax.nn.gelu(x, approximate=True)

def _silu(x):
    return jax.nn.silu(x)

def _sigmoid(x):
    return jax.nn.sigmoid(x)

def _layernorm(x, axis=-1, eps=1e-05):
    m = jnp.mean(x, axis=axis, keepdims=True)
    v = jnp.var(x, axis=axis, keepdims=True)
    return (x - m) / jnp.sqrt(v + eps)

def _scatter_add(tgt, idx, src, axis=0):
    return tgt.at[idx].add(src)

def _segment_sum(src, seg, n):
    return jax.ops.segment_sum(src, seg, n)
kernel_name = 'mk_vit_tower_cls_d1_tok_img1024_r4_30b0de'

def setup_inputs(seed: int=0):
    np.random.seed(seed)
    _w = jnp.asarray

    def _rec_inputs():
        import jax
        import jax.numpy as jnp
        _rk = jax.random.key(seed)
        x = -0.00016672 + 0.999947 * jax.random.normal(jax.random.fold_in(_rk, 1), (64, 3, 96, 96), jnp.float32)
        cls_tok = 0.02 * jax.random.normal(jax.random.fold_in(_rk, 5), (1, 1, 256), jnp.float32)
        return (x, cls_tok)
    x, cls_tok = _rec_inputs()

    def _L0_tok_setup():
        import jax, jax.numpy as jnp
        import numpy as np
        B, C, H, W = (64, 3, 96, 96)
        P = 16
        HP, WP = (H // P, W // P)
        N = HP * WP
        F = C * P * P
        D = 256
        key = jax.random.key(seed)
        k1, k2, k3, k4, k5 = jax.random.split(key, 5)
        data = jax.random.normal(k1, (B, C, H, W), dtype=jnp.float32)
        lim = 1.0 / np.sqrt(F)
        W_lin = jax.random.uniform(k2, (D, F), minval=-lim, maxval=lim, dtype=jnp.float32)
        b_lin = jax.random.uniform(k3, (D,), minval=-lim, maxval=lim, dtype=jnp.float32)
        class_token = jax.random.normal(k4, (1, 1, D), dtype=jnp.float32)
        position_embeddings = jax.random.normal(k5, (1, N + 1, D), dtype=jnp.float32)
        return {'data': data, 'W_lin': W_lin, 'b_lin': b_lin, 'class_token': class_token, 'position_embeddings': position_embeddings}
    _L0_tok_all = _L0_tok_setup()
    _L0_tok_in = {k: v for k, v in _L0_tok_all.items() if k in ('W_lin', 'b_lin', 'class_token', 'position_embeddings')}
    del _L0_tok_all

    def _L0_attn_setup():
        import jax, jax.numpy as jnp
        import numpy as np
        B, S, E = (2, 512, 256)
        INNER = 512
        NH = 4
        K = 4
        PH, PD = (128, 4)

        def _forward(x, W_up, conv_w, conv_b, Wq, Wk, Wv, W_ig, b_ig, W_fg, b_fg, norm_w, skip, W_down):
            Bx, Sx, _ = x.shape
            x_inner = x @ W_up
            x_mlstm, z = jnp.split(x_inner, 2, axis=-1)
            Kk = conv_w.shape[0]
            x_pad = jnp.pad(x_mlstm, ((0, 0), (Kk - 1, 0), (0, 0)))
            x_conv = sum((x_pad[:, i:i + Sx, :] * conv_w[i] for i in range(Kk))) + conv_b
            x_act = jax.nn.swish(x_conv)

            def headwise(t, W):
                H, o, d = W.shape
                return jnp.einsum('bshd,hod->bsho', t.reshape(Bx, Sx, H, d), W).reshape(Bx, Sx, H * o)
            q = headwise(x_act, Wq)
            k = headwise(x_act, Wk)
            v = headwise(x_mlstm, Wv)
            Dm = q.shape[-1]
            NHn = b_ig.shape[0]
            DH = Dm // NHn
            qh = q.reshape(Bx, Sx, NHn, DH).transpose(0, 2, 1, 3)
            kh = k.reshape(Bx, Sx, NHn, DH).transpose(0, 2, 1, 3)
            vh = v.reshape(Bx, Sx, NHn, DH).transpose(0, 2, 1, 3)
            if_in = jnp.concatenate([q, k, v], axis=-1)
            ig = (if_in @ W_ig + b_ig).transpose(0, 2, 1)[..., None]
            fg = (if_in @ W_fg + b_fg).transpose(0, 2, 1)[..., None]
            log_f = jax.nn.log_sigmoid(fg)
            lfc = jnp.concatenate([jnp.zeros((Bx, NHn, 1, 1), log_f.dtype), jnp.cumsum(log_f, axis=2)], axis=2)
            lfm = lfc - jnp.swapaxes(lfc, -2, -1)
            mask = jnp.tril(jnp.ones((Sx + 1, Sx + 1), bool))
            lfm = jnp.where(mask, lfm, -jnp.inf)[:, :, 1:, 1:]
            logD = lfm + jnp.swapaxes(ig, -2, -1)
            mD = jnp.max(logD, axis=-1, keepdims=True)
            Dmat = jnp.exp(logD - mD)
            C = jnp.einsum('bnsd,bntd->bnst', qh, kh) * DH ** (-0.5) * Dmat
            norm = jnp.maximum(jnp.abs(C.sum(-1, keepdims=True)), jnp.exp(-mD))
            h = jnp.einsum('bnst,bntd->bnsd', C / (norm + 1e-06), vh)
            mu = h.mean(-1, keepdims=True)
            var = ((h - mu) ** 2).mean(-1, keepdims=True)
            hn = ((h - mu) * jax.lax.rsqrt(var + 1e-06)).transpose(0, 2, 1, 3).reshape(Bx, Sx, Dm)
            hn = hn * norm_w
            h_state = (hn + skip * x_act) * jax.nn.swish(z)
            return h_state @ W_down
        key = jax.random.key(seed)
        ks = jax.random.split(key, 10)
        f = lambda k, shape, s=0.02: jax.random.normal(k, shape, jnp.float32) * s
        return dict(x=jax.random.normal(ks[0], (B, S, E), jnp.float32), W_up=f(ks[1], (E, 2 * INNER)), conv_w=f(ks[2], (K, INNER), 0.1), conv_b=jnp.zeros((INNER,), jnp.float32), Wq=f(ks[3], (PH, PD, PD), 0.3), Wk=f(ks[4], (PH, PD, PD), 0.3), Wv=f(ks[5], (PH, PD, PD), 0.3), W_ig=f(ks[6], (3 * INNER, NH), 0.01), b_ig=jnp.zeros((NH,), jnp.float32), W_fg=f(ks[7], (3 * INNER, NH), 0.01), b_fg=jnp.linspace(3.0, 6.0, NH).astype(jnp.float32), norm_w=jnp.ones((INNER,), jnp.float32), skip=jnp.ones((INNER,), jnp.float32), W_down=f(ks[8], (INNER, E)))
    _L0_attn_all = _L0_attn_setup()
    _L0_attn_in = {k: v for k, v in _L0_attn_all.items() if k in ('W_up', 'conv_w', 'conv_b', 'Wq', 'Wk', 'Wv', 'W_ig', 'b_ig', 'W_fg', 'b_fg', 'norm_w', 'skip', 'W_down')}
    del _L0_attn_all

    def _L0_ffn_setup():
        import jax, jax.numpy as jnp
        import numpy as np
        H = 256
        I = 512
        E = 32
        B, S = (4, 512)

        def _grouped_mm(a, w, group_sizes):
            return jax.lax.ragged_dot(a, w, group_sizes)

        def _swiglu(x, gw, uw, dw):
            return jax.nn.silu(x @ gw) * (x @ uw) @ dw
        key = jax.random.key(seed)
        ks = jax.random.split(key, 8)
        scale = 0.02
        inp = {'hidden_states': jax.random.normal(ks[0], (B, S, H), dtype=jnp.float32), 'gate_w': jax.random.normal(ks[1], (H, E), dtype=jnp.float32) * scale, 'shared_gate_w': jax.random.normal(ks[2], (H, I), dtype=jnp.float32) * scale, 'shared_up_w': jax.random.normal(ks[3], (H, I), dtype=jnp.float32) * scale, 'shared_down_w': jax.random.normal(ks[4], (I, H), dtype=jnp.float32) * scale, 'routed_gate_w': jax.random.normal(ks[5], (E, H, I), dtype=jnp.float32) * scale, 'routed_up_w': jax.random.normal(ks[6], (E, H, I), dtype=jnp.float32) * scale, 'routed_down_w': jax.random.normal(ks[7], (E, I, H), dtype=jnp.float32) * scale}
        return inp
    _L0_ffn_all = _L0_ffn_setup()
    _L0_ffn_in = {k: v for k, v in _L0_ffn_all.items() if k in ('gate_w', 'shared_gate_w', 'shared_up_w', 'shared_down_w', 'routed_gate_w', 'routed_up_w', 'routed_down_w')}
    del _L0_ffn_all
    return {'x': x, 'cls_tok': cls_tok, 'L0_tok_W_lin': _L0_tok_in['W_lin'], 'L0_tok_b_lin': _L0_tok_in['b_lin'], 'L0_tok_class_token': _L0_tok_in['class_token'], 'L0_tok_position_embeddings': _L0_tok_in['position_embeddings'], 'L0_attn_W_up': _L0_attn_in['W_up'], 'L0_attn_conv_w': _L0_attn_in['conv_w'], 'L0_attn_conv_b': _L0_attn_in['conv_b'], 'L0_attn_Wq': _L0_attn_in['Wq'], 'L0_attn_Wk': _L0_attn_in['Wk'], 'L0_attn_Wv': _L0_attn_in['Wv'], 'L0_attn_W_ig': _L0_attn_in['W_ig'], 'L0_attn_b_ig': _L0_attn_in['b_ig'], 'L0_attn_W_fg': _L0_attn_in['W_fg'], 'L0_attn_b_fg': _L0_attn_in['b_fg'], 'L0_attn_norm_w': _L0_attn_in['norm_w'], 'L0_attn_skip': _L0_attn_in['skip'], 'L0_attn_W_down': _L0_attn_in['W_down'], 'L0_ffn_gate_w': _L0_ffn_in['gate_w'], 'L0_ffn_shared_gate_w': _L0_ffn_in['shared_gate_w'], 'L0_ffn_shared_up_w': _L0_ffn_in['shared_up_w'], 'L0_ffn_shared_down_w': _L0_ffn_in['shared_down_w'], 'L0_ffn_routed_gate_w': _L0_ffn_in['routed_gate_w'], 'L0_ffn_routed_up_w': _L0_ffn_in['routed_up_w'], 'L0_ffn_routed_down_w': _L0_ffn_in['routed_down_w']}

def reference(x, cls_tok, L0_tok_W_lin, L0_tok_b_lin, L0_tok_class_token, L0_tok_position_embeddings, L0_attn_W_up, L0_attn_conv_w, L0_attn_conv_b, L0_attn_Wq, L0_attn_Wk, L0_attn_Wv, L0_attn_W_ig, L0_attn_b_ig, L0_attn_W_fg, L0_attn_b_fg, L0_attn_norm_w, L0_attn_skip, L0_attn_W_down, L0_ffn_gate_w, L0_ffn_shared_gate_w, L0_ffn_shared_up_w, L0_ffn_shared_down_w, L0_ffn_routed_gate_w, L0_ffn_routed_up_w, L0_ffn_routed_down_w):
    import jax
    import jax.numpy as jnp

    def _L0_tok_ref(data, W_lin, b_lin, class_token, position_embeddings):
        import jax, jax.numpy as jnp
        import numpy as np
        B, C, H, W = (64, 3, 96, 96)
        P = 16
        HP, WP = (H // P, W // P)
        N = HP * WP
        F = C * P * P
        D = 256
        b = data.shape[0]
        x = data.reshape(b, C, HP, P, WP, P)
        x = x.transpose(0, 2, 4, 1, 3, 5).reshape(b, N, F)
        x = jnp.einsum('bnf,df->bnd', x, W_lin) + b_lin
        cls = jnp.broadcast_to(class_token, (b, 1, D))
        out = jnp.concatenate([cls, x], axis=1) + position_embeddings
        return out

    def _L0_attn_ref(x, W_up, conv_w, conv_b, Wq, Wk, Wv, W_ig, b_ig, W_fg, b_fg, norm_w, skip, W_down):
        import jax, jax.numpy as jnp
        import numpy as np
        B, S, E = (2, 512, 256)
        INNER = 512
        NH = 4
        K = 4
        PH, PD = (128, 4)

        def _forward(x, W_up, conv_w, conv_b, Wq, Wk, Wv, W_ig, b_ig, W_fg, b_fg, norm_w, skip, W_down):
            Bx, Sx, _ = x.shape
            x_inner = x @ W_up
            x_mlstm, z = jnp.split(x_inner, 2, axis=-1)
            Kk = conv_w.shape[0]
            x_pad = jnp.pad(x_mlstm, ((0, 0), (Kk - 1, 0), (0, 0)))
            x_conv = sum((x_pad[:, i:i + Sx, :] * conv_w[i] for i in range(Kk))) + conv_b
            x_act = jax.nn.swish(x_conv)

            def headwise(t, W):
                H, o, d = W.shape
                return jnp.einsum('bshd,hod->bsho', t.reshape(Bx, Sx, H, d), W).reshape(Bx, Sx, H * o)
            q = headwise(x_act, Wq)
            k = headwise(x_act, Wk)
            v = headwise(x_mlstm, Wv)
            Dm = q.shape[-1]
            NHn = b_ig.shape[0]
            DH = Dm // NHn
            qh = q.reshape(Bx, Sx, NHn, DH).transpose(0, 2, 1, 3)
            kh = k.reshape(Bx, Sx, NHn, DH).transpose(0, 2, 1, 3)
            vh = v.reshape(Bx, Sx, NHn, DH).transpose(0, 2, 1, 3)
            if_in = jnp.concatenate([q, k, v], axis=-1)
            ig = (if_in @ W_ig + b_ig).transpose(0, 2, 1)[..., None]
            fg = (if_in @ W_fg + b_fg).transpose(0, 2, 1)[..., None]
            log_f = jax.nn.log_sigmoid(fg)
            lfc = jnp.concatenate([jnp.zeros((Bx, NHn, 1, 1), log_f.dtype), jnp.cumsum(log_f, axis=2)], axis=2)
            lfm = lfc - jnp.swapaxes(lfc, -2, -1)
            mask = jnp.tril(jnp.ones((Sx + 1, Sx + 1), bool))
            lfm = jnp.where(mask, lfm, -jnp.inf)[:, :, 1:, 1:]
            logD = lfm + jnp.swapaxes(ig, -2, -1)
            mD = jnp.max(logD, axis=-1, keepdims=True)
            Dmat = jnp.exp(logD - mD)
            C = jnp.einsum('bnsd,bntd->bnst', qh, kh) * DH ** (-0.5) * Dmat
            norm = jnp.maximum(jnp.abs(C.sum(-1, keepdims=True)), jnp.exp(-mD))
            h = jnp.einsum('bnst,bntd->bnsd', C / (norm + 1e-06), vh)
            mu = h.mean(-1, keepdims=True)
            var = ((h - mu) ** 2).mean(-1, keepdims=True)
            hn = ((h - mu) * jax.lax.rsqrt(var + 1e-06)).transpose(0, 2, 1, 3).reshape(Bx, Sx, Dm)
            hn = hn * norm_w
            h_state = (hn + skip * x_act) * jax.nn.swish(z)
            return h_state @ W_down
        return _forward(x, W_up, conv_w, conv_b, Wq, Wk, Wv, W_ig, b_ig, W_fg, b_fg, norm_w, skip, W_down)

    def _L0_ffn_ref(hidden_states, gate_w, shared_gate_w, shared_up_w, shared_down_w, routed_gate_w, routed_up_w, routed_down_w):
        import jax, jax.numpy as jnp
        import numpy as np
        H = 256
        I = 512
        E = 32
        B, S = (4, 512)

        def _grouped_mm(a, w, group_sizes):
            return jax.lax.ragged_dot(a, w, group_sizes)

        def _swiglu(x, gw, uw, dw):
            return jax.nn.silu(x @ gw) * (x @ uw) @ dw
        b, s, h = hidden_states.shape
        x = hidden_states.reshape(-1, h)
        shared_out = _swiglu(x, shared_gate_w, shared_up_w, shared_down_w)
        logits = x @ gate_w
        topk_ids = jnp.argmax(logits, axis=-1)
        topk_val = jnp.max(logits, axis=-1)
        scores = jax.nn.sigmoid(topk_val)[:, None]
        xs = x * scores
        tokens_per_expert = jnp.zeros((E,), jnp.int32).at[topk_ids].add(1)
        order = jnp.argsort(topk_ids)
        sorted_x = xs[order]
        g = _grouped_mm(sorted_x, routed_gate_w, tokens_per_expert)
        u = _grouped_mm(sorted_x, routed_up_w, tokens_per_expert)
        d = _grouped_mm(jax.nn.silu(g) * u, routed_down_w, tokens_per_expert)
        inv = jnp.argsort(order)
        routed_out = d[inv]
        return (shared_out + routed_out).reshape(b, s, h)
    h = _L0_tok_ref(x, L0_tok_W_lin, L0_tok_b_lin, L0_tok_class_token, L0_tok_position_embeddings)
    h = jnp.concatenate([jnp.broadcast_to(cls_tok, (h.shape[0], 1, h.shape[2])), h], axis=1)
    h = h + _L0_attn_ref(_layernorm(h, axis=-1), L0_attn_W_up, L0_attn_conv_w, L0_attn_conv_b, L0_attn_Wq, L0_attn_Wk, L0_attn_Wv, L0_attn_W_ig, L0_attn_b_ig, L0_attn_W_fg, L0_attn_b_fg, L0_attn_norm_w, L0_attn_skip, L0_attn_W_down)
    h = h + _L0_ffn_ref(_layernorm(h, axis=-1), L0_ffn_gate_w, L0_ffn_shared_gate_w, L0_ffn_shared_up_w, L0_ffn_shared_down_w, L0_ffn_routed_gate_w, L0_ffn_routed_up_w, L0_ffn_routed_down_w)
    return h

_drawn_inputs = setup_inputs


def setup_inputs(seed=0):
    import zlib

    import numpy as np

    out = dict(_drawn_inputs(seed))
    spreads = {'L0_attn_conv_b': (0.0, 0.1),
     'L0_attn_b_ig': (0.0, 0.8),
     'L0_attn_norm_w': (1.0, 0.6),
     'L0_attn_skip': (1.0, 0.6)}
    factors = {'cls_tok': 6.158,
     'L0_tok_b_lin': 3.038,
     'L0_attn_W_ig': 8.0,
     'L0_attn_W_fg': 64.0,
     'L0_attn_b_fg': 64.0,
     'L0_ffn_gate_w': 6.473,
     'L0_ffn_shared_gate_w': 2.753,
     'L0_ffn_shared_up_w': 2.707,
     'L0_ffn_shared_down_w': 2.692,
     'L0_ffn_routed_gate_w': 6.397,
     'L0_ffn_routed_up_w': 6.341,
     'L0_ffn_routed_down_w': 6.405}
    for name, (base, spread) in spreads.items():
        noise = np.random.default_rng([zlib.crc32(name.encode()), seed]).standard_normal(out[name].shape)
        drawn = base * np.exp(spread * noise) if base else spread * noise
        out[name] = jnp.asarray(drawn.astype(out[name].dtype))
    for name, factor in factors.items():
        out[name] = (out[name] * factor).astype(out[name].dtype)
    return out
```

```python
from contextlib import ExitStack
from collections import namedtuple

import numpy as np
import concourse.bass as bass
from concourse import mybir

B, C, HW, P = 64, 3, 96, 16
HP = HW // P
N = HP * HP
S = N + 2
F = C * P * P
D = 256
INNER, NH, PH, PD = 512, 4, 128, 4
TAPS = 4
I = 512
E = 32
T = B * S

GS = 8
G = B // GS
GT = GS * S
TS = 2
R = TS * S
NT = GS // TS
TILES = B // TS
KF, KD, KI = F // 128, D // 128, INNER // 128
SLOT = 128
SLOTS = (T + E * (SLOT - 1)) // SLOT
SLOTS += -SLOTS % 4
LEVELS = T // SLOT
WCOLS = 2 * KD * I + KI * D
MASKED = -1.0e30
NOWHERE = 1.0e6

Group = namedtuple("Group", "n p")


def groups_phase(nc, patches, w_lin, pos, cols, w_up, conv, chan, wq, wk, wv, wvt, w_gates, b_gates,
                 w_down, w_route, w_sgu, w_sd, xs_dram, base_dram, hot, banks):
    f32, bf16, u32 = mybir.dt.float32, mybir.dt.bfloat16, mybir.dt.uint32
    ALU, ACT, AX = mybir.AluOpType, mybir.ActivationFunctionType, mybir.AxisListType
    fb, ab, mb = banks[0:2], banks[2:6], banks[6:8]

    with ExitStack() as ctx:
        def sb(name, shape, dt=f32):
            return ctx.enter_context(nc.sbuf_tensor(name, shape, dt))

        def sem(name):
            return ctx.enter_context(nc.semaphore(name))

        ident = sb("ident", [128, 128])
        ones = sb("ones", [128, 128])
        tri = sb("tri", [R, R])
        mask = sb("mask", [R, R])
        iota_e = sb("iota_e", [R, E])
        minus_half = sb("minus_half", [R, NT * NH])
        lin_w = sb("lin_w", [128, KF, D])
        up_w = sb("up_w", [128, KD, 2 * INNER])
        down_w = sb("down_w", [128, KI, D])
        sgu_w = sb("sgu_w", [128, KD, 2 * I])
        sd_w = sb("sd_w", [128, KI, D])
        route_w = sb("route_w", [128, KD, E])
        pos_t = sb("pos_t", [128, KD, N + 1])
        col_t = sb("col_t", [128, KD, 3])
        posb = sb("posb", [128, KD, N])
        conv_t = sb("conv_t", [128, KI, TAPS + 1])
        chan_t = sb("chan_t", [128, KI, 2])
        gates_b = sb("gates_b", [R, 2 * NH])
        q_raw = sb("q_raw", [128, KI, 128])
        k_raw = sb("k_raw", [128, KI, 128])
        v_raw = sb("v_raw", [128, KI, 128])
        g_raw = sb("g_raw", [128, 3, KI, 2 * NH])
        score_w = sb("score_w", [128, KI, 128])
        v_w = sb("v_w", [128, KI, 128])
        gx_w = sb("gx_w", [128, KI, 2 * NH])
        gm_w = sb("gm_w", [128, KI, 2 * NH])

        patch = sb("patch", [128, 2, KF, GS * N])
        h_t = sb("h_t", [128, KD, GS, S])
        h_rows = sb("h_rows", [R, 2, NT, D])
        stats1 = sb("stats1", [R, NT, 6])
        mv1 = sb("mv1", [R, NT, 2])
        rstd1 = sb("rstd1", [R, NT])
        xn = sb("xn", [R, NT, D])
        xn_t = sb("xn_t", [128, KD, GT])
        xm = sb("xm", [128, 2, KI, GS, S])
        tanh_z = sb("tanh_z", [128, KI, GT])
        silu_z = sb("silu_z", [128, 2, KI, GT])
        y = sb("y", [128, KI, GS, S])
        tanh_y = sb("tanh_y", [128, KI, GT])
        x_act = sb("x_act", [128, 2, KI, GT])
        q_t = sb("q_t", [128, KI, GT])
        v = sb("v", [R, NT, INNER])
        gl = sb("gl", [R, NT, 2 * NH])
        fabs = sb("fabs", [R, NT, NH])
        fexp = sb("fexp", [R, NT, NH])
        fln = sb("fln", [R, NT, NH])
        logf = sb("logf", [R, NT, NH])
        fsum = sb("fsum", [R, NT, NH])
        a_gate = sb("a_gate", [R, NT, NH])
        diag = sb("diag", [R, NT, NH, R])
        lg = sb("lg", [R, NT, NH, R])
        row_max = sb("row_max", [R, NT, NH])
        cw = sb("cw", [R, NT, NH, R])
        row_sum = sb("row_sum", [R, NT, NH])
        m_d = sb("m_d", [R, NT, NH])
        exp_md = sb("exp_md", [R, NT, NH])
        norm = sb("norm", [R, NT, NH])
        norm2 = sb("norm2", [R, NT, NH])
        cw_t = sb("cw_t", [R, NT, NH * R])
        o = sb("o", [R, NT, NH, 128])
        stats_h = sb("stats_h", [R, NT, NH, 6])
        mv_h = sb("mv_h", [R, NT, NH, 2])
        var_h = sb("var_h", [R, NT, NH])
        rstd_h = sb("rstd_h", [R, NT, NH])
        hst = sb("hst", [128, KI, GT])
        att_t = sb("att_t", [128, KD, GT])
        h2 = sb("h2", [R, 2, NT, D])
        stats2 = sb("stats2", [R, NT, 6])
        mv2 = sb("mv2", [R, NT, 2])
        rstd2 = sb("rstd2", [R, NT])
        xn2 = sb("xn2", [R, NT, D])
        xn2_t = sb("xn2_t", [128, KD, GT])
        logits = sb("logits", [R, NT, E])
        top = sb("top", [R, NT, 8])
        top_i = sb("top_i", [R, NT, 8], u32)
        top_f = sb("top_f", [R, NT])
        tanh_s = sb("tanh_s", [R, NT])
        score = sb("score", [R, NT])
        xs_rows = sb("xs_rows", [R, NT, D])
        tanh_g = sb("tanh_g", [128, 2, GT])
        silu_g = sb("silu_g", [128, 2, GT])
        act_t = sb("act_t", [128, KI, GT])
        ffn_t = sb("ffn_t", [128, KD, GT])
        base_rows = sb("base_rows", [R, NT, D])
        s_w_front = sem("s_w_front")
        s_w_att = sem("s_w_att")
        s_w_ffn = sem("s_w_ffn")
        s_passed = sem("s_passed")
        s_const = sem("s_const")
        s_prep_mm = sem("s_prep_mm")
        s_prep = sem("s_prep")
        s_patch = [sem(f"s_patch{i}") for i in range(2)]
        s_emb_mm = sem("s_emb_mm")
        s_ht = sem("s_ht")
        s_h_mm = sem("s_h_mm")
        s_hrows = sem("s_hrows")
        s_st1 = sem("s_st1")
        s_mv1 = sem("s_mv1")
        s_ve1 = sem("s_ve1")
        s_rstd1 = sem("s_rstd1")
        s_xn = sem("s_xn")
        s_xnt_mm = sem("s_xnt_mm")
        s_xnt = sem("s_xnt")
        s_up_mm = sem("s_up_mm")
        s_xm = sem("s_xm")
        s_tz = sem("s_tz")
        s_sz = sem("s_sz")
        s_conv = sem("s_conv")
        s_ty = sem("s_ty")
        s_xact = sem("s_xact")
        s_q_mm = sem("s_q_mm")
        s_q = sem("s_q")
        s_v_mm = sem("s_v_mm")
        s_v = sem("s_v")
        s_g_mm = sem("s_g_mm")
        s_gl = sem("s_gl")
        s_fabs = sem("s_fabs")
        s_fexp = sem("s_fexp")
        s_fln = sem("s_fln")
        s_logf = sem("s_logf")
        s_f_mm = sem("s_f_mm")
        s_fsum = sem("s_fsum")
        s_a = sem("s_a")
        s_diag = sem("s_diag")
        s_b_mm = sem("s_b_mm")
        s_c_mm = sem("s_c_mm")
        s_lg = sem("s_lg")
        s_max = sem("s_max")
        s_lgm = sem("s_lgm")
        s_dmat = sem("s_dmat")
        s_cw = sem("s_cw")
        s_sum = sem("s_sum")
        s_md = sem("s_md")
        s_expmd = sem("s_expmd")
        s_norm = sem("s_norm")
        s_ct_mm = sem("s_ct_mm")
        s_ct = sem("s_ct")
        s_pv_mm = sem("s_pv_mm")
        s_o = sem("s_o")
        s_sth = sem("s_sth")
        s_mvh = sem("s_mvh")
        s_varh = sem("s_varh")
        s_rstdh = sem("s_rstdh")
        s_hn = sem("s_hn")
        s_skip = sem("s_skip")
        s_hnt_mm = sem("s_hnt_mm")
        s_hmix = sem("s_hmix")
        s_hst = sem("s_hst")
        s_wd_mm = sem("s_wd_mm")
        s_att = sem("s_att")
        s_at_mm = sem("s_at_mm")
        s_h2 = sem("s_h2")
        s_st2 = sem("s_st2")
        s_mv2 = sem("s_mv2")
        s_ve2 = sem("s_ve2")
        s_rstd2 = sem("s_rstd2")
        s_xn2 = sem("s_xn2")
        s_xn2t_mm = sem("s_xn2t_mm")
        s_xn2t = sem("s_xn2t")
        s_rt_mm = sem("s_rt_mm")
        s_lgt = sem("s_lgt")
        s_top = sem("s_top")
        s_topi = sem("s_topi")
        s_topf = sem("s_topf")
        s_hot = sem("s_hot")
        s_ts = sem("s_ts")
        s_score = sem("s_score")
        s_xs = sem("s_xs")
        s_xs_out = sem("s_xs_out")
        s_gu_mm = sem("s_gu_mm")
        s_tg = sem("s_tg")
        s_sg = sem("s_sg")
        s_act = sem("s_act")
        s_sd_mm = sem("s_sd_mm")
        s_ffn = sem("s_ffn")
        s_ft_mm = sem("s_ft_mm")
        s_base = sem("s_base")
        s_base_out = sem("s_base_out")

        def wait(eng, semaphore, value):
            if not isinstance(value, int) or value > 0:
                eng.wait_ge(semaphore, value)

        def wait_apart(eng, semaphore, value):
            eng.wait_ge(semaphore, value)
            if not isinstance(value, int):
                eng.sem_inc(s_passed, 1)

        def pipeline(eng, step):
            step(Group(0, 0), None, None)
            step(Group(1, 1), Group(0, 0), None)
            with eng.Fori(0, (G - 2) // 2) as j:
                step(Group(2 * j + 2, 0), Group(2 * j + 1, 1), Group(2 * j, 0))
                step(Group(2 * j + 3, 1), Group(2 * j + 2, 0), Group(2 * j + 1, 1))
            step(None, Group(G - 1, 1), Group(G - 2, 0))
            step(None, None, Group(G - 1, 1))

        with nc.Block() as block:

            @block.sync
            def _(sp):
                for dst, src in [(lin_w, w_lin), (pos_t, pos), (col_t, cols)]:
                    sp.dma_start(dst[:], src).then_inc(s_w_front, 16)

                def load_patches(f):
                    wait(sp, s_emb_mm, KD * (f.n - 1))
                    src = patches[bass.ds(f.n, 1)].rearrange("g p (k n) -> p (g k) n", k=KF)
                    sp.dma_start(patch[:, f.p], src).then_inc(s_patch[f.p], 16)

                load_patches(Group(0, 0))
                for dst, src in [(up_w, w_up), (conv_t, conv), (chan_t, chan)]:
                    sp.dma_start(dst[:], src).then_inc(s_w_front, 16)

                def step(f, a, m):
                    if f is not None and not (isinstance(f.n, int) and f.n == 0):
                        load_patches(f)
                    if m is not None:
                        sp.wait_ge(s_xs, NT * m.n + NT)
                        dst = xs_dram[bass.ds(m.n * GT, GT), :].rearrange("(j p) d -> p j d", p=R)
                        sp.dma_start(dst, xs_rows[:]).then_inc(s_xs_out, 16)
                        sp.wait_ge(s_base, 2 * m.n + 2)
                        dst = base_dram[bass.ds(m.n * GT, GT), :].rearrange("(j p) d -> p j d", p=R)
                        sp.dma_start(dst, base_rows[:]).then_inc(s_base_out, 16)

                pipeline(sp, step)
                sp.wait_ge(s_xs_out, 16 * G + 16)
                sp.wait_ge(s_base_out, 16 * G + 16)

            @block.gpsimd
            def _(pool):
                pool.sem_inc(s_xs_out, 16)
                pool.sem_inc(s_base_out, 16)
                pool.memset(ident[:], 0.0).then_inc(s_const, 1)
                pool.memset(tri[:], 1.0).then_inc(s_const, 1)
                pool.memset(mask[:], 0.0).then_inc(s_const, 1)
                pool.memset(ones[:], 1.0).then_inc(s_const, 1)
                pool.memset(minus_half[:], -0.5).then_inc(s_const, 1)
                pool.iota(iota_e[:], pattern=[[1, E]], base=0, channel_multiplier=0,
                          allow_small_or_imprecise_dtypes=True).then_inc(s_const, 1)
                pool.wait_ge(s_const, 6)
                pool.affine_select(out=ident[:], in_=ident[:], compare_op=ALU.not_equal, fill=1.0,
                                   base=0, pattern=[[-1, 128]], channel_multiplier=1).then_inc(s_const, 1)
                pool.affine_select(out=tri[:], in_=tri[:], compare_op=ALU.is_ge, fill=0.0,
                                   base=0, pattern=[[1, R]], channel_multiplier=-1).then_inc(s_const, 1)
                pool.affine_select(out=mask[:], in_=mask[:], compare_op=ALU.is_ge, fill=MASKED,
                                   base=0, pattern=[[-1, R]], channel_multiplier=1).then_inc(s_const, 1)
                pool.wait_ge(s_const, 9)
                pool.affine_select(out=tri[:, S:R], in_=tri[:, S:R], compare_op=ALU.is_ge, fill=0.0,
                                   base=-S, pattern=[[0, S]], channel_multiplier=1).then_inc(s_const, 1)
                pool.affine_select(out=mask[:, 0:S], in_=mask[:, 0:S], compare_op=ALU.is_ge, fill=MASKED,
                                   base=S - 1, pattern=[[0, S]], channel_multiplier=-1).then_inc(s_const, 1)

                def rstd1_of(f):
                    wait_apart(pool, s_mv1, NT * f.n + NT)
                    pool.tensor_scalar(rstd1[:], mv1[:, :, 1], 1e-5, None, ALU.add).then_inc(s_ve1, 1)
                    pool.wait_ge(s_ve1, f.n + 1)
                    pool.tensor_tensor(rstd1[:], rstd1[:], minus_half[:, 0:NT], ALU.pow).then_inc(s_rstd1, 1)

                def rstd2_of(m):
                    wait_apart(pool, s_mv2, NT * m.n + NT)
                    pool.tensor_scalar(rstd2[:], mv2[:, :, 1], 1e-5, None, ALU.add).then_inc(s_ve2, 1)
                    pool.wait_ge(s_ve2, m.n + 1)
                    pool.tensor_tensor(rstd2[:], rstd2[:], minus_half[:, 0:NT], ALU.pow).then_inc(s_rstd2, 1)

                def rstd_h_of(a):
                    pool.wait_ge(s_varh, a.n + 1)
                    pool.tensor_tensor(rstd_h[:].rearrange("p j h -> p (j h)"),
                                       var_h[:].rearrange("p j h -> p (j h)"),
                                       minus_half[:], ALU.pow).then_inc(s_rstdh, 1)

                def step(f, a, m):
                    if m is not None:
                        rstd2_of(m)
                    if f is not None:
                        rstd1_of(f)
                    if a is not None:
                        rstd_h_of(a)

                pipeline(pool, step)

            @block.scalar
            def _(act):
                bias = b_gates.partition_broadcast(R)
                for dst, src in [(q_raw, wq), (k_raw, wk), (v_raw, wv), (v_w, wvt), (g_raw, w_gates),
                                 (gates_b, bias)]:
                    act.dma_start(dst[:], src).then_inc(s_w_att, 16)
                for dst, src in [(down_w, w_down), (route_w, w_route), (sgu_w, w_sgu), (sd_w, w_sd)]:
                    act.dma_start(dst[:], src).then_inc(s_w_ffn, 16)

                def copy(dst, src):
                    return act.activation(dst, src, ACT.Copy)

                def h_rows_of(f):
                    for b in range(2):
                        act.wait_ge(s_h_mm, 2 * f.n + b + 1)
                        copy(h_rows[:, f.p, 2 * b:2 * b + 2, :].rearrange("p j d -> p (j d)"),
                             fb[b][0:R, :]).then_inc(s_hrows, 1)

                def xn_t_of(f):
                    for c in range(KD):
                        act.wait_ge(s_xnt_mm, KD * f.n + c + 1)
                        copy(xn_t[:, c, :], fb[c][:, 0:GT]).then_inc(s_xnt, 1)

                def xm_of(f, k):
                    act.wait_ge(s_up_mm, 2 * KI * f.n + k + 1)
                    copy(xm[:, f.p, k].rearrange("p s t -> p (s t)"), fb[k % 2][:, 0:GT]).then_inc(s_xm, 1)

                def tanh_z_of(f, k):
                    act.wait_ge(s_up_mm, 2 * KI * f.n + KI + k + 1)
                    act.activation(tanh_z[:, k, :], fb[k % 2][:, 0:GT], ACT.Tanh).then_inc(s_tz, 1)

                def tanh_y_of(f, pair):
                    act.wait_ge(s_conv, 16 * f.n + 8 * pair + 8)
                    for k in (2 * pair, 2 * pair + 1):
                        act.activation(tanh_y[:, k, :], y[:, k].rearrange("p s t -> p (s t)"),
                                       ACT.Tanh).then_inc(s_ty, 1)

                def q_of(a):
                    for h in range(NH):
                        act.wait_ge(s_q_mm, NH * a.n + h + 1)
                        act.activation(q_t[:, h, :], ab[h][:, 0:GT], ACT.Copy,
                                       scale=float(INNER // NH) ** -0.5).then_inc(s_q, 1)

                def v_of(a):
                    for j in range(NT):
                        act.wait_ge(s_v_mm, NT * a.n + j + 1)
                        copy(v[:, j, :], ab[j][0:R, :]).then_inc(s_v, 1)

                def log_f(a):
                    act.wait_ge(s_fabs, a.n + 1)
                    act.activation(fexp[:], fabs[:], ACT.Exp, scale=-1.0).then_inc(s_fexp, 1)
                    act.wait_ge(s_fexp, a.n + 1)
                    act.activation(fln[:], fexp[:], ACT.Ln, bias=1.0).then_inc(s_fln, 1)

                def decay(a, j):
                    act.wait_ge(s_lgm, NT * a.n + j + 1)
                    act.activation(lg[:, j], lg[:, j], ACT.Exp).then_inc(s_dmat, 1)

                def exp_m_d(a):
                    act.wait_ge(s_md, a.n + 1)
                    act.activation(exp_md[:], m_d[:], ACT.Exp, scale=-1.0).then_inc(s_expmd, 1)

                def cw_t_of(a, j):
                    act.wait_ge(s_ct_mm, NT * a.n + j + 1)
                    copy(cw_t[:, j, :], ab[j][0:R, 0:GT]).then_inc(s_ct, 1)

                def o_of(a, j):
                    act.wait_ge(s_pv_mm, NT * a.n + j + 1)
                    copy(o[:, j].rearrange("p h d -> p (h d)"), ab[j][0:R, :]).then_inc(s_o, 1)

                def att_t_of(a):
                    for c in range(KD):
                        act.wait_ge(s_wd_mm, KD * a.n + c + 1)
                        copy(att_t[:, c, :], ab[c][:, 0:GT]).then_inc(s_att, 1)

                def xn2_t_of(m):
                    for c in range(KD):
                        act.wait_ge(s_xn2t_mm, KD * m.n + c + 1)
                        copy(xn2_t[:, c, :], mb[c][:, 0:GT]).then_inc(s_xn2t, 1)

                def tanh_score(m):
                    act.wait_ge(s_top, NT * m.n + NT)
                    act.activation(tanh_s[:], top[:, :, 0], ACT.Tanh, scale=0.5).then_inc(s_ts, 1)

                def tanh_g_of(m, k):
                    act.wait_ge(s_gu_mm, 2 * KI * m.n + 2 * k + 1)
                    act.activation(tanh_g[:, k % 2, :], mb[0][:, 0:GT], ACT.Tanh).then_inc(s_tg, 1)

                def ffn_t_of(m):
                    for c in range(KD):
                        act.wait_ge(s_sd_mm, KD * m.n + c + 1)
                        copy(ffn_t[:, c, :], mb[c][:, 0:GT]).then_inc(s_ffn, 1)

                def step(f, a, m):
                    if a: q_of(a)
                    if m: xn2_t_of(m)
                    if f: h_rows_of(f)
                    if a: v_of(a)
                    if m: tanh_score(m)
                    if a: log_f(a)
                    if f: xn_t_of(f)
                    if m: tanh_g_of(m, 0)
                    if f: xm_of(f, 0)
                    if m: tanh_g_of(m, 1)
                    if f: xm_of(f, 1)
                    if m: tanh_g_of(m, 2)
                    if f: xm_of(f, 2)
                    if a: decay(a, 0)
                    if m: tanh_g_of(m, 3)
                    if f: xm_of(f, 3)
                    if a: decay(a, 1)
                    if f: tanh_y_of(f, 0)
                    if m: ffn_t_of(m)
                    if f: tanh_z_of(f, 0)
                    if a: decay(a, 2)
                    if f: tanh_z_of(f, 1)
                    if a: decay(a, 3)
                    if a:
                        exp_m_d(a)
                        for j in range(NT):
                            cw_t_of(a, j)
                    if f: tanh_z_of(f, 2)
                    if a:
                        o_of(a, 0)
                        o_of(a, 1)
                    if f: tanh_z_of(f, 3)
                    if a:
                        o_of(a, 2)
                        o_of(a, 3)
                    if f: tanh_y_of(f, 1)
                    if a: att_t_of(a)

                pipeline(act, step)

            @block.vector
            def _(dve):
                dve.wait_ge(s_w_front, 6 * 16)
                for c in range(KD):
                    dve.tensor_scalar(posb[:, c, :], pos_t[:, c, 1:], col_t[:, c, 0:1], None,
                                      ALU.add).then_inc(s_prep, 1)
                    dve.tensor_copy(h_t[:, c, :, 0], col_t[:, c, 2:3].broadcast_to([128, GS])).then_inc(s_prep, 1)
                    dve.tensor_scalar(h_t[:, c, :, 1], pos_t[:, c, 0:1].broadcast_to([128, GS]),
                                      col_t[:, c, 1:2], None, ALU.add).then_inc(s_prep, 1)
                dve.tensor_scalar(conv_t[:], conv_t[:], 0.5, None, ALU.mult).then_inc(s_prep, 1)
                dve.tensor_scalar(up_w[:, :, INNER:], up_w[:, :, INNER:], 0.5, None, ALU.mult).then_inc(s_prep, 1)
                dve.wait_ge(s_prep, 8)

                def merge_weights():
                    dve.wait_ge(s_prep_mm, 1)
                    dve.tensor_copy(score_w[:].rearrange("p h d -> p (h d)"), ab[0][:, :]).then_inc(s_prep, 1)
                    dve.wait_ge(s_prep_mm, 2)
                    dve.tensor_copy(gx_w[:].rearrange("p h g -> p (h g)"), ab[1][:, 0:32]).then_inc(s_prep, 1)
                    dve.tensor_copy(gm_w[:].rearrange("p h g -> p (h g)"), ab[1][:, 32:64]).then_inc(s_prep, 1)
                    dve.wait_ge(s_w_ffn, 4 * 16)
                    dve.tensor_scalar(sgu_w[:, :, 0:I], sgu_w[:, :, 0:I], 0.5, None, ALU.mult).then_inc(s_prep, 1)

                def embed(f):
                    for c in range(KD):
                        dve.wait_ge(s_emb_mm, KD * f.n + c + 1)
                        dve.tensor_tensor(h_t[:, c, :, 2:],
                                          fb[c][:, 0:GS * N].rearrange("p (s n) -> p s n", n=N),
                                          posb[:, c].unsqueeze(1).broadcast_to([128, GS, N]),
                                          ALU.add).then_inc(s_ht, 1)

                def ln1_stats(f):
                    for j in range(NT):
                        if j % 2 == 0:
                            dve.wait_ge(s_hrows, 2 * f.n + j // 2 + 1)
                        dve.bn_stats(stats1[:, j, :], h_rows[:, f.p, j, :]).then_inc(s_st1, 1)
                    for j in range(NT):
                        wait_apart(dve, s_st1, NT * f.n + j + 1)
                        dve.bn_aggr(mv1[:, j, :], stats1[:, j, :]).then_inc(s_mv1, 1)

                def xn_of(f):
                    dve.wait_ge(s_rstd1, f.n + 1)
                    for j in range(NT):
                        dve.tensor_scalar(xn[:, j, :], h_rows[:, f.p, j, :], mv1[:, j, 0:1], rstd1[:, j:j + 1],
                                          ALU.subtract, ALU.mult).then_inc(s_xn, 1)

                def conv_of(f, pair):
                    for lag in range(TAPS):
                        for e in range(2):
                            k = 2 * pair + e
                            w = conv_t[:, k, TAPS - 1 - lag:TAPS - lag]
                            if lag == 0:
                                dve.wait_ge(s_xm, KI * f.n + k + 1)
                                last = dve.tensor_scalar(y[:, k], xm[:, f.p, k], w, conv_t[:, k, TAPS:TAPS + 1],
                                                         ALU.mult, ALU.add)
                            else:
                                dve.wait_ge(s_conv, 16 * f.n + 8 * pair + 2 * (lag - 1) + e + 1)
                                last = dve.scalar_tensor_tensor(y[:, k, :, lag:], xm[:, f.p, k, :, 0:S - lag], w,
                                                                y[:, k, :, lag:], ALU.mult, ALU.add)
                            last.then_inc(s_conv, 1)

                def x_act_of(f, pair):
                    for k in (2 * pair, 2 * pair + 1):
                        dve.wait_ge(s_ty, KI * f.n + k + 1)
                        dve.scalar_tensor_tensor(x_act[:, f.p, k, :], tanh_y[:, k, :], 1.0,
                                                 y[:, k].rearrange("p s t -> p (s t)"),
                                                 ALU.add, ALU.mult).then_inc(s_xact, 1)

                def silu_z_of(f, k):
                    dve.wait_ge(s_tz, KI * f.n + k + 1)
                    dve.scalar_tensor_tensor(silu_z[:, f.p, k, :], tanh_z[:, k, :], 1.0, fb[k % 2][:, 0:GT],
                                             ALU.add, ALU.mult).then_inc(s_sz, 1)

                def gates_of(a):
                    dve.wait_ge(s_g_mm, a.n + 1)
                    dve.tensor_tensor(gl[:], ab[0][0:R, 0:32].rearrange("p (j g) -> p j g", j=NT),
                                      gates_b[:].unsqueeze(1).broadcast_to([R, NT, 2 * NH]), ALU.add).then_inc(s_gl, 1)
                    dve.wait_ge(s_gl, a.n + 1)
                    dve.scalar_tensor_tensor(fabs[:], gl[:, :, NH:], -1.0, gl[:, :, NH:], ALU.mult,
                                             ALU.max).then_inc(s_fabs, 1)

                def log_f(a):
                    dve.wait_ge(s_fln, a.n + 1)
                    dve.scalar_tensor_tensor(logf[:], gl[:, :, NH:], 0.0, fln[:], ALU.min,
                                             ALU.subtract).then_inc(s_logf, 1)

                def a_of(a):
                    dve.wait_ge(s_f_mm, a.n + 1)
                    sums = ab[1][0:R, 0:NT * NH].rearrange("p (j h) -> p j h", j=NT)
                    dve.tensor_tensor(a_gate[:], gl[:, :, 0:NH], sums, ALU.subtract).then_inc(s_a, 1)
                    dve.tensor_copy(fsum[:], sums).then_inc(s_fsum, 1)

                def diag_of(a, j):
                    dve.wait_ge(s_a, a.n + 1)
                    dve.tensor_tensor(diag[:, j], ident[0:R, 0:R].unsqueeze(1).broadcast_to([R, NH, R]),
                                      a_gate[:, j].unsqueeze(2).broadcast_to([R, NH, R]), ALU.mult).then_inc(s_diag, 1)

                def decay(a, j):
                    n = NT * a.n + j + 1
                    dve.wait_ge(s_b_mm, n)
                    dve.tensor_tensor(lg[:, j], ab[2 * (j % 2)][0:R, 0:GT].rearrange("p (h t) -> p h t", h=NH),
                                      mask[:].unsqueeze(1).broadcast_to([R, NH, R]), ALU.add).then_inc(s_lg, 1)
                    dve.wait_ge(s_lg, n)
                    dve.tensor_reduce(row_max[:, j, :], lg[:, j], AX.X, ALU.max).then_inc(s_max, 1)
                    dve.wait_ge(s_max, n)
                    dve.tensor_tensor(lg[:, j], lg[:, j], row_max[:, j].unsqueeze(2).broadcast_to([R, NH, R]),
                                      ALU.subtract).then_inc(s_lgm, 1)

                def weigh(a, j):
                    n = NT * a.n + j + 1
                    dve.wait_ge(s_dmat, n)
                    dve.wait_ge(s_c_mm, n)
                    dve.tensor_tensor(cw[:, j], ab[2 * (j % 2) + 1][0:R, 0:GT].rearrange("p (h t) -> p h t", h=NH),
                                      lg[:, j], ALU.mult).then_inc(s_cw, 1)
                    dve.wait_ge(s_cw, n)
                    dve.tensor_reduce(row_sum[:, j, :], cw[:, j], AX.X, ALU.add).then_inc(s_sum, 1)

                def norm_1(a):
                    dve.wait_ge(s_max, NT * a.n + NT)
                    dve.tensor_tensor(m_d[:], fsum[:], row_max[:], ALU.add).then_inc(s_md, 1)

                def norm_2(a):
                    dve.wait_ge(s_sum, NT * a.n + NT)
                    dve.wait_ge(s_expmd, a.n + 1)
                    dve.scalar_tensor_tensor(norm[:], row_sum[:], -1.0, row_sum[:], ALU.mult,
                                             ALU.max).then_inc(s_norm, 1)
                    dve.wait_ge(s_norm, 4 * a.n + 1)
                    dve.tensor_tensor(norm[:], norm[:], exp_md[:], ALU.max).then_inc(s_norm, 1)
                    dve.wait_ge(s_norm, 4 * a.n + 2)
                    dve.tensor_scalar(norm[:], norm[:], 1e-6, None, ALU.add).then_inc(s_norm, 1)
                    dve.wait_ge(s_norm, 4 * a.n + 3)
                    dve.tensor_tensor(norm2[:], norm[:], norm[:], ALU.mult).then_inc(s_norm, 1)

                def head_stats(a, j):
                    dve.wait_ge(s_o, NT * a.n + j + 1)
                    for h in range(NH):
                        dve.bn_stats(stats_h[:, j, h, :], o[:, j, h, :]).then_inc(s_sth, 1)
                    for h in range(NH):
                        wait_apart(dve, s_sth, NT * NH * a.n + NH * j + h + 1)
                        dve.bn_aggr(mv_h[:, j, h, :], stats_h[:, j, h, :]).then_inc(s_mvh, 1)

                def head_var(a):
                    dve.wait_ge(s_mvh, NT * NH * a.n + NT * NH)
                    dve.wait_ge(s_norm, 4 * a.n + 4)
                    dve.scalar_tensor_tensor(var_h[:], norm2[:], 1e-6, mv_h[:, :, :, 1], ALU.mult,
                                             ALU.add).then_inc(s_varh, 1)

                def skip_of(a):
                    wait(dve, s_wd_mm, KD * a.n)
                    for h in range(NH):
                        dve.tensor_scalar(hst[:, h, :], x_act[:, a.p, h, :], chan_t[:, h, 1:2], None,
                                          ALU.mult).then_inc(s_skip, 1)

                def head_norm(a):
                    dve.wait_ge(s_rstdh, a.n + 1)
                    for j in range(NT):
                        for h in range(NH):
                            dve.tensor_scalar(o[:, j, h, :], o[:, j, h, :], mv_h[:, j, h, 0:1],
                                              rstd_h[:, j, h:h + 1], ALU.subtract, ALU.mult).then_inc(s_hn, 1)

                def state(a):
                    dve.wait_ge(s_skip, NH * a.n + NH)
                    for h in range(NH):
                        dve.wait_ge(s_hnt_mm, NH * a.n + h + 1)
                        dve.scalar_tensor_tensor(hst[:, h, :], ab[h][:, 0:GT], chan_t[:, h, 0:1], hst[:, h, :],
                                                 ALU.mult, ALU.add).then_inc(s_hmix, 1)
                        dve.wait_ge(s_hmix, NH * a.n + h + 1)
                        dve.tensor_tensor(hst[:, h, :], hst[:, h, :], silu_z[:, a.p, h, :],
                                          ALU.mult).then_inc(s_hst, 1)

                def h2_of(a):
                    for b in range(2):
                        dve.wait_ge(s_at_mm, 2 * a.n + b + 1)
                        dve.tensor_tensor(h2[:, a.p, 2 * b:2 * b + 2, :],
                                          ab[2 + b][0:R, :].rearrange("p (j d) -> p j d", j=2),
                                          h_rows[:, a.p, 2 * b:2 * b + 2, :], ALU.add).then_inc(s_h2, 1)

                def ln2_stats(m):
                    for j in range(NT):
                        if j % 2 == 0:
                            dve.wait_ge(s_h2, 2 * m.n + j // 2 + 1)
                        dve.bn_stats(stats2[:, j, :], h2[:, m.p, j, :]).then_inc(s_st2, 1)
                    for j in range(NT):
                        wait_apart(dve, s_st2, NT * m.n + j + 1)
                        dve.bn_aggr(mv2[:, j, :], stats2[:, j, :]).then_inc(s_mv2, 1)

                def xn2_of(m):
                    dve.wait_ge(s_rstd2, m.n + 1)
                    for j in range(NT):
                        dve.tensor_scalar(xn2[:, j, :], h2[:, m.p, j, :], mv2[:, j, 0:1], rstd2[:, j:j + 1],
                                          ALU.subtract, ALU.mult).then_inc(s_xn2, 1)

                def route(m):
                    dve.wait_ge(s_rt_mm, m.n + 1)
                    dve.tensor_copy(logits[:].rearrange("p j e -> p (j e)"), mb[0][0:R, 0:NT * E]).then_inc(s_lgt, 1)
                    wait_apart(dve, s_lgt, m.n + 1)
                    for j in range(NT):
                        dve.max(top[:, j, :], logits[:, j, :]).then_inc(s_top, 1)
                    for j in range(NT):
                        wait_apart(dve, s_top, NT * m.n + j + 1)
                        dve.max_index(top_i[:, j, :], top[:, j, :], logits[:, j, :]).then_inc(s_topi, 1)
                    dve.wait_ge(s_topi, NT * m.n + NT)
                    dve.tensor_copy(top_f[:], top_i[:, :, 0]).then_inc(s_topf, 1)
                    dve.wait_ge(s_topf, m.n + 1)
                    for j in range(NT):
                        dve.tensor_scalar(hot[:, bass.ds(NT * m.n + j, 1), :], iota_e[:].unsqueeze(1),
                                          top_f[:, j:j + 1], None, ALU.is_equal).then_inc(s_hot, 1)

                def score_rows(m):
                    dve.wait_ge(s_ts, m.n + 1)
                    dve.tensor_scalar(score[:], tanh_s[:], 1.0, 0.5, ALU.add, ALU.mult).then_inc(s_score, 1)
                    dve.wait_ge(s_score, m.n + 1)
                    dve.wait_ge(s_xs_out, 16 * m.n + 16)
                    for j in range(NT):
                        dve.tensor_scalar(xs_rows[:, j, :], xn2[:, j, :], score[:, j:j + 1], None,
                                          ALU.mult).then_inc(s_xs, 1)

                def expert_act(m, k):
                    dve.wait_ge(s_tg, KI * m.n + k + 1)
                    dve.scalar_tensor_tensor(silu_g[:, k % 2, :], tanh_g[:, k % 2, :], 1.0, mb[0][:, 0:GT],
                                             ALU.add, ALU.mult).then_inc(s_sg, 1)
                    dve.wait_ge(s_sg, KI * m.n + k + 1)
                    dve.wait_ge(s_gu_mm, 2 * KI * m.n + 2 * k + 2)
                    dve.tensor_tensor(act_t[:, k, :], silu_g[:, k % 2, :], mb[1][:, 0:GT], ALU.mult).then_inc(s_act, 1)

                def base_of(m):
                    dve.wait_ge(s_base_out, 16 * m.n + 16)
                    for b in range(2):
                        dve.wait_ge(s_ft_mm, 2 * m.n + b + 1)
                        dve.tensor_tensor(base_rows[:, 2 * b:2 * b + 2, :],
                                          mb[b][0:R, :].rearrange("p (j d) -> p j d", j=2),
                                          h2[:, m.p, 2 * b:2 * b + 2, :], ALU.add).then_inc(s_base, 1)

                def step(f, a, m):
                    if isinstance(f, Group) and isinstance(f.n, int) and f.n == 1:
                        merge_weights()
                    if m: ln2_stats(m)
                    if f: embed(f)
                    if m: xn2_of(m)
                    if f: ln1_stats(f)
                    if m: route(m)
                    if a: gates_of(a)
                    if f: xn_of(f)
                    if a: log_f(a)
                    if m: expert_act(m, 0)
                    if m: expert_act(m, 1)
                    if a:
                        a_of(a)
                        diag_of(a, 0)
                        diag_of(a, 1)
                    if m: expert_act(m, 2)
                    if f: conv_of(f, 0)
                    if a: decay(a, 0)
                    if m: expert_act(m, 3)
                    if a:
                        diag_of(a, 2)
                        decay(a, 1)
                        weigh(a, 0)
                    if f: x_act_of(f, 0)
                    if f: silu_z_of(f, 0)
                    if a:
                        diag_of(a, 3)
                        decay(a, 2)
                        weigh(a, 1)
                    if f: silu_z_of(f, 1)
                    if m:
                        base_of(m)
                        score_rows(m)
                    if a:
                        decay(a, 3)
                        norm_1(a)
                        weigh(a, 2)
                        weigh(a, 3)
                    if f: conv_of(f, 1)
                    if f: silu_z_of(f, 2)
                    if a:
                        norm_2(a)
                        head_stats(a, 0)
                        head_stats(a, 1)
                    if f: silu_z_of(f, 3)
                    if a:
                        head_stats(a, 2)
                        head_stats(a, 3)
                        head_var(a)
                        skip_of(a)
                    if f: x_act_of(f, 1)
                    if a:
                        head_norm(a)
                        state(a)
                        h2_of(a)

                pipeline(dve, step)

            @block.tensor
            def _(pe):
                pe.wait_ge(s_const, 11)
                pe.wait_ge(s_w_front, 6 * 16)
                pe.wait_ge(s_prep, 8)

                def merge_weights():
                    pe.wait_ge(s_w_att, 6 * 16)
                    for h in range(NH):
                        last = pe.matmul(ab[0][:, h * 128:(h + 1) * 128], q_raw[:, h], k_raw[:, h],
                                         start=True, stop=True)
                    last.then_inc(s_prep_mm, 1)
                    for h in range(NH):
                        pe.matmul(ab[1][:, 8 * h:8 * h + 8], q_raw[:, h], g_raw[:, 0, h], start=True, stop=False)
                        pe.matmul(ab[1][:, 8 * h:8 * h + 8], k_raw[:, h], g_raw[:, 1, h], start=False, stop=True)
                    for h in range(NH):
                        last = pe.matmul(ab[1][:, 32 + 8 * h:40 + 8 * h], v_raw[:, h], g_raw[:, 2, h],
                                         start=True, stop=True)
                    last.then_inc(s_prep_mm, 1)
                    pe.wait_ge(s_prep, 12)

                def embed(f):
                    pe.wait_ge(s_patch[f.p], 8 * f.n + 16 - 8 * f.p)
                    for c in range(KD):
                        wait(pe, s_sz, KI * f.n - 1 + c)
                        for k in range(KF):
                            last = pe.matmul(fb[c][:, 0:GS * N], lin_w[:, k, c * 128:(c + 1) * 128],
                                             patch[:, f.p, k, :], start=(k == 0), stop=(k == KF - 1))
                        last.then_inc(s_emb_mm, 1)

                def to_rows(dst, src, done):
                    for b in range(2):
                        for j in (2 * b, 2 * b + 1):
                            for c in range(KD):
                                last = pe.transpose(dst[b][0:R, (j % 2) * D + c * 128:(j % 2) * D + (c + 1) * 128],
                                                    src[:, c, j * R:(j + 1) * R], ident[:])
                        last.then_inc(done, 1)

                def h_rows_of(f):
                    pe.wait_ge(s_ht, KD * f.n + KD)
                    to_rows(fb, h_t[:].rearrange("p c s t -> p c (s t)"), s_h_mm)

                def to_columns(dst, src, ready, n, done):
                    for c in range(KD):
                        for j in range(NT):
                            if c == 0:
                                pe.wait_ge(ready, NT * n + j + 1)
                            last = pe.transpose(dst[c][:, j * R:(j + 1) * R], src[:, j, c * 128:(c + 1) * 128],
                                                ident[0:R, 0:R])
                        last.then_inc(done, 1)

                def up(f, k):
                    if k < 2:
                        pe.wait_ge(s_xnt, KD * f.n + KD)
                    elif k < 2 + KI:
                        pe.wait_ge(s_xm, KI * f.n + k - 1)
                    else:
                        pe.wait_ge(s_sz, KI * f.n + k - KI - 1)
                    for c in range(KD):
                        last = pe.matmul(fb[k % 2][:, 0:GT], up_w[:, c, k * 128:(k + 1) * 128], xn_t[:, c, :],
                                         start=(c == 0), stop=(c == KD - 1))
                    last.then_inc(s_up_mm, 1)

                def q_of(a):
                    pe.wait_ge(s_xact, KI * a.n + KI)
                    for h in range(NH):
                        if h < 2:
                            wait(pe, s_att, KD * a.n)
                        else:
                            wait(pe, s_h2, 2 * a.n)
                        pe.matmul(ab[h][:, 0:GT], score_w[:, h], x_act[:, a.p, h, :],
                                  start=True, stop=True).then_inc(s_q_mm, 1)

                def xm_tile(a, h, j):
                    return xm[:, a.p, h, TS * j:TS * j + TS, :].rearrange("p s t -> p (s t)")

                def v_of(a):
                    for j in range(NT):
                        pe.wait_ge(s_q, NH * a.n + j + 1)
                        for h in range(NH):
                            last = pe.matmul(ab[j][0:R, h * 128:(h + 1) * 128], xm_tile(a, h, j), v_w[:, h],
                                             start=True, stop=True)
                        last.then_inc(s_v_mm, 1)

                def gates_of(a):
                    pe.wait_ge(s_v, NT * a.n + 1)
                    for j in range(NT):
                        dst = ab[0][0:R, 8 * j:8 * j + 8]
                        for h in range(NH):
                            pe.matmul(dst, x_act[:, a.p, h, j * R:(j + 1) * R], gx_w[:, h],
                                      start=(h == 0), stop=False)
                        for h in range(NH):
                            last = pe.matmul(dst, xm_tile(a, h, j), gm_w[:, h], start=False, stop=(h == NH - 1))
                    last.then_inc(s_g_mm, 1)

                def f_sums(a):
                    pe.wait_ge(s_v, NT * a.n + 2)
                    pe.wait_ge(s_logf, a.n + 1)
                    pe.matmul(ab[1][0:R, 0:NT * NH], tri[:], logf[:].rearrange("p j h -> p (j h)"),
                              start=True, stop=True).then_inc(s_f_mm, 1)

                def scores(a, j):
                    pe.wait_ge(s_diag, NT * a.n + j + 1)
                    if j == 0:
                        pe.wait_ge(s_fsum, a.n + 1)
                    elif j == 1:
                        pe.wait_ge(s_v, NT * a.n + NT)
                    else:
                        pe.wait_ge(s_cw, NT * a.n + j - 1)
                    b = 2 * (j % 2)
                    pe.matmul(ab[b][0:R, 0:GT], ones[0:R, 0:R], diag[:, j].rearrange("p h t -> p (h t)"),
                              start=True, stop=True).then_inc(s_b_mm, 1)
                    for h in range(NH):
                        last = pe.matmul(ab[b + 1][0:R, h * R:(h + 1) * R], q_t[:, h, j * R:(j + 1) * R],
                                         x_act[:, a.p, h, j * R:(j + 1) * R], start=True, stop=True)
                    last.then_inc(s_c_mm, 1)

                def cw_t_of(a, j):
                    pe.wait_ge(s_cw, NT * a.n + (NT if j > 1 else NT - 1))
                    for h in range(NH):
                        last = pe.transpose(ab[j][0:R, h * R:(h + 1) * R], cw[:, j, h, :], ident[0:R, 0:R])
                    last.then_inc(s_ct_mm, 1)

                def heads(a, j):
                    pe.wait_ge(s_ct, NT * a.n + j + 1)
                    for h in range(NH):
                        last = pe.matmul(ab[j][0:R, h * 128:(h + 1) * 128], cw_t[:, j, h * R:(h + 1) * R],
                                         v[:, j, h * 128:(h + 1) * 128], start=True, stop=True)
                    last.then_inc(s_pv_mm, 1)

                def heads_t(a):
                    for h in range(NH):
                        for j in range(NT):
                            if h == 0:
                                pe.wait_ge(s_hn, NT * NH * a.n + NH * (j + 1))
                            last = pe.transpose(ab[h][:, j * R:(j + 1) * R], o[:, j, h, :], ident[0:R, 0:R])
                        last.then_inc(s_hnt_mm, 1)

                def down(a):
                    pe.wait_ge(s_hst, NH * a.n + NH)
                    for c in range(KD):
                        for k in range(KI):
                            last = pe.matmul(ab[c][:, 0:GT], down_w[:, k, c * 128:(c + 1) * 128], hst[:, k, :],
                                             start=(k == 0), stop=(k == KI - 1))
                        last.then_inc(s_wd_mm, 1)

                def att_rows(a):
                    pe.wait_ge(s_att, KD * a.n + KD)
                    to_rows(ab[2:4], att_t, s_at_mm)

                def route(m):
                    pe.wait_ge(s_xn2t, KD * m.n + KD)
                    for j in range(NT):
                        for c in range(KD):
                            last = pe.matmul(mb[0][0:R, j * E:(j + 1) * E], xn2_t[:, c, j * R:(j + 1) * R],
                                             route_w[:, c], start=(c == 0), stop=(c == KD - 1))
                    last.then_inc(s_rt_mm, 1)

                def gate_up(m, k):
                    if k == 0:
                        pe.wait_ge(s_lgt, m.n + 1)
                    else:
                        pe.wait_ge(s_sg, KI * m.n + k)
                    for u in range(2):
                        if u and k:
                            pe.wait_ge(s_act, KI * m.n + k)
                        at = u * I + k * 128
                        for c in range(KD):
                            last = pe.matmul(mb[u][:, 0:GT], sgu_w[:, c, at:at + 128], xn2_t[:, c, :],
                                             start=(c == 0), stop=(c == KD - 1))
                        last.then_inc(s_gu_mm, 1)

                def shared_down(m):
                    pe.wait_ge(s_act, KI * m.n + KI)
                    for c in range(KD):
                        for k in range(KI):
                            last = pe.matmul(mb[c][:, 0:GT], sd_w[:, k, c * 128:(c + 1) * 128], act_t[:, k, :],
                                             start=(k == 0), stop=(k == KI - 1))
                        last.then_inc(s_sd_mm, 1)

                def ffn_rows(m):
                    pe.wait_ge(s_ffn, KD * m.n + KD)
                    to_rows(mb, ffn_t, s_ft_mm)

                def step(f, a, m):
                    if f is not None and isinstance(f.n, int) and f.n == 1:
                        merge_weights()
                    if f: embed(f)
                    if a: q_of(a)
                    if m: to_columns(mb, xn2, s_xn2, m.n, s_xn2t_mm)
                    if f: h_rows_of(f)
                    if a: v_of(a)
                    if m: route(m)
                    if a: gates_of(a)
                    if f: to_columns(fb, xn, s_xn, f.n, s_xnt_mm)
                    if m: gate_up(m, 0)
                    if f: up(f, 0)
                    if m: gate_up(m, 1)
                    if f: up(f, 1)
                    if a: f_sums(a)
                    if m: gate_up(m, 2)
                    if f: up(f, 2)
                    if a: scores(a, 0)
                    if m: gate_up(m, 3)
                    if f: up(f, 3)
                    if a: scores(a, 1)
                    if m: shared_down(m)
                    if f: up(f, 4)
                    if a: scores(a, 2)
                    if m: ffn_rows(m)
                    if f: up(f, 5)
                    if a: scores(a, 3)
                    if a:
                        for j in range(NT):
                            cw_t_of(a, j)
                    if f: up(f, 6)
                    if a:
                        heads(a, 0)
                        heads(a, 1)
                    if f: up(f, 7)
                    if a:
                        heads(a, 2)
                        heads(a, 3)
                        heads_t(a)
                        down(a)
                        att_rows(a)

                pipeline(pe, step)


def experts_phase(nc, w_exp, xs_dram, base_dram, out, hot, banks):
    f32, i32, u32, bf16 = (mybir.dt.float32, mybir.dt.int32, mybir.dt.uint32, mybir.dt.bfloat16)
    ALU, ACT, AX = mybir.AluOpType, mybir.ActivationFunctionType, mybir.AxisListType
    HALF = TILES // 2
    PART = 8

    with ExitStack() as ctx:
        def sb(name, shape, dt=f32):
            return ctx.enter_context(nc.sbuf_tensor(name, shape, dt))

        def sem(name):
            return ctx.enter_context(nc.semaphore(name))

        ident2 = sb("ident2", [128, 128])
        before = sb("before", [R, R], bf16)
        ones_bf = sb("ones_bf", [R, R], bf16)
        ones_e = sb("ones_e", [R, E])
        restart = sb("restart", [R, E, TILES])
        levels = sb("levels", [R, LEVELS])
        iota_r = sb("iota_r", [R, SLOT])
        token1 = sb("token1", [R, TILES])
        total = sb("total", [R, E, TILES])
        upto = sb("upto", [R, E, TILES])
        above = sb("above", [R, E, LEVELS])
        n_slots = sb("n_slots", [R, E])
        end_slot = sb("end_slot", [R, E])
        start_slot = sb("start_slot", [R, E])
        start_row = sb("start_row", [R, E, TILES])
        ended = sb("ended", [R, SLOTS, E])
        slot_e = sb("slot_e", [R, SLOTS])
        table = sb("table", [R, SLOTS + 1], i32)
        place = sb("place", [R, TILES, E])
        pos_f = sb("pos_f", [R, TILES])
        pos_i = sb("pos_i", [R, TILES], i32)
        slot_i = sb("slot_i", [R, TILES], i32)
        row_i = sb("row_i", [R, TILES], i32)
        slot_f = sb("slot_f", [R, TILES])
        row_f = sb("row_f", [R, TILES])
        in_slot = sb("in_slot", [R, TILES, SLOTS])
        in_row = sb("in_row", [R, TILES, SLOT])
        empty = sb("empty", [128, SLOTS])
        take_f = sb("take_f", [128, SLOTS])
        put_f = sb("put_f", [128, SLOTS])
        take = sb("take", [128, SLOTS + 4], u32)
        put = sb("put", [128, SLOTS + 4], u32)
        wts = sb("wts", [128, 4, WCOLS])
        take_i = sb("take_i", [128, 4], u32)
        put_i = sb("put_i", [128, 4], u32)
        xg = sb("xg", [128, 4, D])
        bg = sb("bg", [128, 4, D])
        xg_t = sb("xg_t", [128, 2, KD, SLOT])
        tanh_e = sb("tanh_e", [128, 2, I])
        silu_e = sb("silu_e", [128, 2, I])
        act_e = sb("act_e", [128, 2, I])
        act_et = sb("act_et", [128, 2, KI, SLOT])
        rows = sb("rows", [128, 4, D])
        iota_s = sb("iota_s", [R, SLOTS])

        s_passed2 = sem("s_passed2")
        s_const2 = sem("s_const2")
        s_rank_mm = sem("s_rank_mm")
        s_tot_mm = sem("s_tot_mm")
        s_seq = sem("s_seq")
        s_table = sem("s_table")
        s_in = sem("s_in")
        s_list_mm = sem("s_list_mm")
        s_list = sem("s_list")
        s_wts = [sem(f"s_wts{i}") for i in range(4)]
        s_take = sem("s_take")
        s_put = sem("s_put")
        s_rows_in = [sem(f"s_rows_in{i}") for i in range(4)]
        s_xgt_mm = sem("s_xgt_mm")
        s_xgt = sem("s_xgt")
        s_ge_mm = sem("s_ge_mm")
        s_te = sem("s_te")
        s_se = sem("s_se")
        s_ae = sem("s_ae")
        s_aet_mm = sem("s_aet_mm")
        s_aet = sem("s_aet")
        s_y_mm = sem("s_y_mm")
        s_y = sem("s_y")
        s_out = sem("s_out")
        s_stored = sem("s_stored")
        CREDIT = 4

        def wait_apart(eng, semaphore, value):
            eng.wait_ge(semaphore, value)
            if not isinstance(value, int):
                eng.sem_inc(s_passed2, 1)

        def slots_in_use(eng):
            eng.wait_ge(s_table, 1)
            return eng.value_load(table[0:1, SLOTS:SLOTS + 1], min_val=1, max_val=SLOTS)

        def pairs(eng, pair):
            used = slots_in_use(eng)
            with eng.Fori(0, SLOTS // 4) as t:
                for first in (0, 2):
                    with eng.If(used > 4 * t + first):
                        pair(t, first)

        with nc.Block() as block:

            @block.sync
            def _(sp):
                used = slots_in_use(sp)
                with sp.Fori(0, SLOTS // 4) as t:
                    for i in range(4):
                        with sp.If(used > 4 * t + (i - i % 2)):
                            sp.wait_ge(s_y_mm, 4 * t + i + 1)
                            e = sp.value_load(table[0:1, bass.ds(4 * t + i, 1)], min_val=0, max_val=E - 1)
                            sp.dma_start(wts[:, i, :].rearrange("p (a n) -> p a n", a=1),
                                         w_exp[bass.ds(e, 1)].rearrange("e p n -> p e n")).then_inc(s_wts[i], 16)

            @block.gpsimd
            def _(pool):
                pool.memset(ident2[:], 0.0).then_inc(s_const2, 1)
                pool.memset(before[:], 1.0).then_inc(s_const2, 1)
                pool.wait_ge(s_const2, 2)
                pool.affine_select(out=before[:], in_=before[:], compare_op=ALU.is_ge, fill=0.0,
                                   base=-1, pattern=[[1, R]], channel_multiplier=-1).then_inc(s_const2, 1)
                pool.memset(ones_bf[:], 1.0).then_inc(s_const2, 1)
                pool.memset(restart[:], 1.0).then_inc(s_const2, 1)
                pool.wait_ge(s_const2, 5)
                pool.memset(restart[:, :, 0:1], 0.0).then_inc(s_const2, 1)
                pool.memset(ones_e[:], 1.0).then_inc(s_const2, 1)
                for dst, pattern, base, cm in [(levels, [[SLOT, LEVELS]], 0, 0), (iota_s, [[1, SLOTS]], 0, 0),
                                               (iota_r, [[1, SLOT]], 0, 0), (token1, [[R, TILES]], 1, 1)]:
                    pool.iota(dst[:], pattern=pattern, base=base, channel_multiplier=cm,
                              allow_small_or_imprecise_dtypes=True).then_inc(s_const2, 1)
                pool.affine_select(out=ident2[:], in_=ident2[:], compare_op=ALU.not_equal, fill=1.0,
                                   base=0, pattern=[[-1, 128]], channel_multiplier=1).then_inc(s_const2, 1)
                pool.sem_inc(s_stored, CREDIT)

                used = slots_in_use(pool)
                pool.wait_ge(s_list, 2)

                def gather(t, i):
                    k = 4 * t + i
                    pool.tensor_copy(take_i[:, i:i + 1], take[:, bass.ds(k, 1)]).then_inc(s_take, 1)
                    wait_apart(pool, s_take, k + 1)
                    pool.indirect_dma_start(xg[:, i, :], None, xs_dram,
                                            bass.IndirectOffsetOnAxis(ap=take_i[:, i:i + 1], axis=0)
                                            ).then_inc(s_rows_in[i], 16)
                    pool.indirect_dma_start(bg[:, i, :], None, base_dram,
                                            bass.IndirectOffsetOnAxis(ap=take_i[:, i:i + 1], axis=0)
                                            ).then_inc(s_rows_in[i], 16)

                def scatter(t, i):
                    k = 4 * t + i
                    pool.wait_ge(s_y, k + 3)
                    pool.tensor_copy(put_i[:, i:i + 1], put[:, bass.ds(k, 1)]).then_inc(s_put, 1)
                    wait_apart(pool, s_put, k + 1)
                    pool.indirect_dma_start(out, bass.IndirectOffsetOnAxis(ap=put_i[:, i:i + 1], axis=0),
                                            rows[:, i, :], None, bounds_check=T - 1,
                                            oob_is_err=False).then_inc(s_out, 16)

                def stored(t, i):
                    pool.wait_ge(s_out, 16 * (4 * t + i + 1))
                    pool.sem_inc(s_stored, 1)

                for i in range(2):
                    gather(0, i)
                with pool.Fori(0, SLOTS // 4) as t:
                    with pool.If(used > 4 * t + 2):
                        gather(t, 2)
                        gather(t, 3)
                    with pool.If(used > 4 * t):
                        scatter(t, 0)
                        stored(t, 0)
                        scatter(t, 1)
                    with pool.If(used > 4 * t + 4):
                        gather(t + 1, 0)
                        gather(t + 1, 1)
                    with pool.If(used > 4 * t):
                        stored(t, 1)
                    with pool.If(used > 4 * t + 2):
                        scatter(t, 2)
                        stored(t, 2)
                        scatter(t, 3)
                        stored(t, 3)

            @block.vector
            def _(dve):
                step = [0]

                def seq(op):
                    step[0] += 1
                    op.then_inc(s_seq, 1)
                    dve.wait_ge(s_seq, step[0])

                dve.sem_inc(s_y, 2)
                dve.wait_ge(s_const2, 12)
                dve.wait_ge(s_tot_mm, 1)
                for i in range(2):
                    op = dve.tensor_copy(total[:, :, i * HALF:(i + 1) * HALF],
                                         banks[2 + i][0:R, :].rearrange("p (t e) -> p e t", e=E))
                    op.then_inc(s_seq, 1)
                step[0] = 2
                dve.wait_ge(s_seq, 2)
                seq(dve.tensor_tensor_scan(upto[:].rearrange("p e t -> p (e t)"),
                                           restart[:].rearrange("p e t -> p (e t)"),
                                           total[:].rearrange("p e t -> p (e t)"), 0.0, ALU.mult, ALU.add))
                seq(dve.tensor_tensor(above[:], upto[:, :, TILES - 1:TILES].broadcast_to([R, E, LEVELS]),
                                      levels[:].unsqueeze(1).broadcast_to([R, E, LEVELS]), ALU.is_gt))
                seq(dve.tensor_reduce(n_slots[:], above[:], AX.X, ALU.add))
                seq(dve.tensor_tensor_scan(end_slot[:], ones_e[:], n_slots[:], 0.0, ALU.mult, ALU.add))
                seq(dve.tensor_tensor(ended[:], end_slot[:].unsqueeze(1).broadcast_to([R, SLOTS, E]),
                                      iota_s[:].unsqueeze(2).broadcast_to([R, SLOTS, E]), ALU.is_le))
                seq(dve.tensor_reduce(slot_e[:], ended[:], AX.X, ALU.add))
                seq(dve.tensor_scalar(table[:, 0:SLOTS], slot_e[:], float(E - 1), None, ALU.min))
                seq(dve.tensor_copy(table[:, SLOTS:SLOTS + 1], end_slot[:, E - 1:E]))
                dve.tensor_tensor(start_slot[:], end_slot[:], n_slots[:], ALU.subtract).then_inc(s_table, 1)
                dve.wait_ge(s_table, 1)
                seq(dve.tensor_tensor(upto[:], upto[:], total[:], ALU.subtract))
                seq(dve.scalar_tensor_tensor(start_row[:], start_slot[:].unsqueeze(2).broadcast_to([R, E, TILES]),
                                             float(SLOT), upto[:], ALU.mult, ALU.add))
                dve.wait_ge(s_rank_mm, 1)
                for i in range(2):
                    half = slice(i * HALF, (i + 1) * HALF)
                    seq(dve.tensor_tensor(place[:, half, :], banks[i][0:R, :].rearrange("p (t e) -> p t e", e=E),
                                          start_row[:, :, half].rearrange("p e t -> p t e"), ALU.add))
                seq(dve.tensor_tensor(place[:], place[:], hot[:], ALU.mult))
                seq(dve.tensor_reduce(pos_f[:], place[:], AX.X, ALU.add))
                seq(dve.tensor_copy(pos_i[:], pos_f[:]))
                seq(dve.tensor_scalar(slot_i[:], pos_i[:], SLOT.bit_length() - 1, None, ALU.arith_shift_right))
                seq(dve.tensor_scalar(row_i[:], pos_i[:], SLOT - 1, None, ALU.bitwise_and))
                seq(dve.tensor_copy(slot_f[:], slot_i[:]))
                seq(dve.tensor_copy(row_f[:], row_i[:]))
                for t in range(0, TILES, PART):
                    part = slice(t, t + PART)
                    seq(dve.tensor_tensor(in_slot[:, part, :], iota_s[:].unsqueeze(1).broadcast_to([R, PART, SLOTS]),
                                          slot_f[:, part].unsqueeze(2).broadcast_to([R, PART, SLOTS]), ALU.is_equal))
                    seq(dve.tensor_tensor(in_slot[:, part, :], in_slot[:, part, :],
                                          token1[:, part].unsqueeze(2).broadcast_to([R, PART, SLOTS]), ALU.mult))
                    dve.tensor_tensor(in_row[:, part, :], iota_r[:].unsqueeze(1).broadcast_to([R, PART, SLOT]),
                                      row_f[:, part].unsqueeze(2).broadcast_to([R, PART, SLOT]),
                                      ALU.is_equal).then_inc(s_in, 1)
                dve.wait_ge(s_list_mm, 1)
                seq(dve.tensor_scalar(empty[:], banks[4][:, 0:SLOTS], 0.5, NOWHERE, ALU.is_lt, ALU.mult))
                seq(dve.tensor_scalar(take_f[:], banks[4][:, 0:SLOTS], -1.0, 0.0, ALU.add, ALU.max))
                seq(dve.tensor_tensor(put_f[:], take_f[:], empty[:], ALU.add))
                dve.tensor_copy(take[:, 0:SLOTS], take_f[:]).then_inc(s_list, 1)
                dve.tensor_copy(put[:, 0:SLOTS], put_f[:]).then_inc(s_list, 1)

                def pair(t, first):
                    for i in (first, first + 1):
                        k, e = 4 * t + i, i % 2
                        dve.wait_ge(s_te, k + 1)
                        dve.scalar_tensor_tensor(silu_e[:, e, :], tanh_e[:, e, :], 1.0, banks[2 + 2 * e][:, :],
                                                 ALU.add, ALU.mult).then_inc(s_se, 1)
                        dve.wait_ge(s_se, k + 1)
                        dve.wait_ge(s_ge_mm, 2 * k + 2)
                        dve.tensor_tensor(act_e[:, e, :], silu_e[:, e, :], banks[3 + 2 * e][:, :],
                                          ALU.mult).then_inc(s_ae, 1)
                    for i in (first, first + 1):
                        k, e = 4 * t + i, i % 2
                        dve.wait_ge(s_y_mm, k + 1 + CREDIT)
                        dve.wait_ge(s_rows_in[i], 32 * t + 32)
                        dve.wait_ge(s_stored, k + 1)
                        dve.scalar_tensor_tensor(rows[:, i, :], banks[e][:, 0:D], 0.5, bg[:, i, :],
                                                 ALU.mult, ALU.add).then_inc(s_y, 1)

                pairs(dve, pair)

            @block.scalar
            def _(act):
                def pair(t, first):
                    for i in (first, first + 1):
                        k, e = 4 * t + i, i % 2
                        act.wait_ge(s_xgt_mm, k + 1)
                        act.activation(xg_t[:, e].rearrange("p c n -> p (c n)"), banks[e][:, 0:D],
                                       ACT.Copy).then_inc(s_xgt, 1)
                        act.wait_ge(s_ge_mm, 2 * k + 1)
                        act.activation(tanh_e[:, e, :], banks[2 + 2 * e][:, :], ACT.Tanh, scale=0.5).then_inc(s_te, 1)
                    for i in (first, first + 1):
                        k, e = 4 * t + i, i % 2
                        act.wait_ge(s_aet_mm, k + 1)
                        act.activation(act_et[:, e].rearrange("p c n -> p (c n)"), banks[6 + e][:, :],
                                       ACT.Copy).then_inc(s_aet, 1)

                pairs(act, pair)

            @block.tensor
            def _(pe):
                pe.sem_inc(s_y_mm, CREDIT)
                pe.wait_ge(s_const2, 12)
                for i in range(2):
                    last = pe.matmul(banks[2 + i][0:R, :], ones_bf[:], hot[:, i * HALF:(i + 1) * HALF, :],
                                     start=True, stop=True)
                last.then_inc(s_tot_mm, 1)
                for i in range(2):
                    last = pe.matmul(banks[i][0:R, :], before[:], hot[:, i * HALF:(i + 1) * HALF, :],
                                     start=True, stop=True)
                last.then_inc(s_rank_mm, 1)
                for t in range(TILES):
                    if t % PART == 0:
                        pe.wait_ge(s_in, t // PART + 1)
                    last = pe.matmul(banks[4][:, 0:SLOTS], in_row[:, t, :], in_slot[:, t, :],
                                     start=(t == 0), stop=(t == TILES - 1))
                last.then_inc(s_list_mm, 1)
                pe.wait_ge(s_list, 2)

                def pair(t, first):
                    for i in (first, first + 1):
                        k, e = 4 * t + i, i % 2
                        pe.wait_ge(s_rows_in[i], 32 * t + 32)
                        pe.wait_ge(s_y, k + 1)
                        for c in range(KD):
                            last = pe.transpose(banks[e][:, c * 128:(c + 1) * 128],
                                                xg[:, i, c * 128:(c + 1) * 128], ident2[:])
                        last.then_inc(s_xgt_mm, 1)
                        pe.wait_ge(s_wts[i], 16 * t + 16)
                        pe.wait_ge(s_xgt, k + 1)
                        for u in range(2):
                            for c in range(KD):
                                at = (u * KD + c) * I
                                last = pe.matmul(banks[2 + 2 * e + u][:, :], xg_t[:, e, c, :], wts[:, i, at:at + I],
                                                 start=(c == 0), stop=(c == KD - 1))
                            last.then_inc(s_ge_mm, 1)
                    for i in (first, first + 1):
                        k, e = 4 * t + i, i % 2
                        pe.wait_ge(s_ae, k + 1)
                        for c in range(KI):
                            last = pe.transpose(banks[6 + e][:, c * 128:(c + 1) * 128],
                                                act_e[:, e, c * 128:(c + 1) * 128], ident2[:])
                        last.then_inc(s_aet_mm, 1)
                        pe.wait_ge(s_aet, k + 1)
                        for c in range(KI):
                            at = 2 * KD * I + c * D
                            last = pe.matmul(banks[e][:, 0:D], act_et[:, e, c, :], wts[:, i, at:at + D],
                                             start=(c == 0), stop=(c == KI - 1))
                        last.then_inc(s_y_mm, 1)

                pairs(pe, pair)


def vit_tower(nc, patches, w_lin, pos, cols, w_up, conv, chan, wq, wk, wv, wvt, w_gates, b_gates,
              w_down, w_route, w_sgu, w_sd, w_exp, out):
    xs_dram = nc.dram_tensor("xs_rows_dram", (T, D), mybir.dt.float32).ap()
    base_dram = nc.dram_tensor("base_rows_dram", (T, D), mybir.dt.float32).ap()
    with ExitStack() as ctx:
        hot = ctx.enter_context(nc.sbuf_tensor("hot", [R, TILES, E], mybir.dt.bfloat16))
        banks = [ctx.enter_context(nc.psum_tensor(f"bank{i}", [128, 512], mybir.dt.float32)) for i in range(8)]
        groups_phase(nc, patches, w_lin, pos, cols, w_up, conv, chan, wq, wk, wv, wvt, w_gates, b_gates,
                     w_down, w_route, w_sgu, w_sd, xs_dram, base_dram, hot, banks)
        experts_phase(nc, w_exp, xs_dram, base_dram, out, hot, banks)


def _block_diagonal(w, transposed=False):
    d = np.zeros((KI, 128, 128), w.dtype)
    for c in range(KI):
        for i in range(128 // PD):
            d[c, PD * i:PD * i + PD, PD * i:PD * i + PD] = w[(128 // PD) * c + i]
    return d.transpose(2, 0, 1) if transposed else d.transpose(1, 0, 2)


def _chunks(w):
    return w.reshape(-1, 128, w.shape[-1]).transpose(1, 0, 2)


def kernel(**inputs):
    import concourse.bacc as bacc
    from concourse.bass_utils import run_bass_kernel_spmd

    a = {k: np.asarray(v) for k, v in inputs.items()}
    L = "L0_"
    x = a["x"].reshape(G, GS, C, HP, P, HP, P).transpose(0, 2, 4, 6, 1, 3, 5).reshape(G, KF, 128, GS * N)
    ig, fg = a[L + "attn_W_ig"], a[L + "attn_W_fg"]
    gates = np.concatenate([ig, fg], 1).reshape(3, KI, 128, 2 * NH)
    laid = {
        "patches": x.transpose(0, 2, 1, 3).reshape(G, 128, KF * GS * N),
        "w_lin": _chunks(a[L + "tok_W_lin"].T),
        "pos": _chunks(a[L + "tok_position_embeddings"][0].T),
        "cols": _chunks(np.stack([a[L + "tok_b_lin"], a[L + "tok_class_token"][0, 0], a["cls_tok"][0, 0]], 1)),
        "w_up": _chunks(a[L + "attn_W_up"]),
        "conv": _chunks(np.concatenate([a[L + "attn_conv_w"], a[L + "attn_conv_b"][None]], 0).T),
        "chan": _chunks(np.stack([a[L + "attn_norm_w"], a[L + "attn_skip"]], 1)),
        "wq": _block_diagonal(a[L + "attn_Wq"]),
        "wk": _block_diagonal(a[L + "attn_Wk"]),
        "wv": _block_diagonal(a[L + "attn_Wv"]),
        "wvt": _block_diagonal(a[L + "attn_Wv"], True),
        "w_gates": gates.transpose(2, 0, 1, 3),
        "b_gates": np.concatenate([a[L + "attn_b_ig"], a[L + "attn_b_fg"]])[None],
        "w_down": _chunks(a[L + "attn_W_down"]),
        "w_route": _chunks(a[L + "ffn_gate_w"]),
        "w_sgu": _chunks(np.concatenate([a[L + "ffn_shared_gate_w"], a[L + "ffn_shared_up_w"]], 1)),
        "w_sd": _chunks(a[L + "ffn_shared_down_w"]),
        "w_exp": np.concatenate(
            [a[L + "ffn_routed_gate_w"].reshape(E, KD, 128, I).transpose(0, 2, 1, 3).reshape(E, 128, KD * I),
             a[L + "ffn_routed_up_w"].reshape(E, KD, 128, I).transpose(0, 2, 1, 3).reshape(E, 128, KD * I),
             a[L + "ffn_routed_down_w"].reshape(E, KI, 128, D).transpose(0, 2, 1, 3).reshape(E, 128, KI * D)], 2),
    }
    laid = {k: np.ascontiguousarray(v) for k, v in laid.items()}
    nc = bacc.Bacc("TRN2", target_bir_lowering=False, num_devices=1)
    args = [nc.dram_tensor(k, v.shape, mybir.dt.from_np(v.dtype), kind="ExternalInput").ap()
            for k, v in laid.items()]
    out = nc.dram_tensor("out", (T, D), mybir.dt.float32, kind="ExternalOutput").ap()
    vit_tower(nc, *args, out)
    r = run_bass_kernel_spmd(nc, [laid], core_ids=[0])
    return r.results[0]["out"].reshape(B, S, D)
```

```python
from contextlib import ExitStack
from collections import namedtuple

import numpy as np
import concourse.bass as bass
from concourse import mybir

B, C, HW, P = 64, 3, 96, 16
HP = HW // P
N = HP * HP
S = N + 2
F = C * P * P
D = 256
INNER, NH, PH, PD = 512, 4, 128, 4
TAPS = 4
I = 512
E = 32
T = B * S

GS = 8
G = B // GS
GT = GS * S
TS = 2
R = TS * S
NT = GS // TS
TILES = B // TS
KF, KD, KI = F // 128, D // 128, INNER // 128
SLOT = 128
SLOTS = (T + E * (SLOT - 1)) // SLOT
SLOTS += -SLOTS % 4
LEVELS = T // SLOT
WCOLS = 2 * KD * I + KI * D
MASKED = -1.0e30
NOWHERE = 1.0e6

Group = namedtuple("Group", "n p")


def groups_phase(nc, patches, w_lin, pos, cols, w_up, conv, chan, wq, wk, wv, wvt, w_gates, b_gates,
                 w_down, w_route, w_sgu, w_sd, xs_dram, base_dram, hot, banks):
    f32, bf16, u32, f32r = mybir.dt.float32, mybir.dt.bfloat16, mybir.dt.uint32, mybir.dt.float32r
    ALU, ACT, AX = mybir.AluOpType, mybir.ActivationFunctionType, mybir.AxisListType
    fb, ab, mb = banks[0:2], banks[2:6], banks[6:8]

    with ExitStack() as ctx:
        def sb(name, shape, dt=f32):
            return ctx.enter_context(nc.sbuf_tensor(name, shape, dt))

        def sem(name):
            return ctx.enter_context(nc.semaphore(name))

        ident = sb("ident", [128, 128])
        ones = sb("ones", [128, 128])
        tri = sb("tri", [R, R])
        mask = sb("mask", [R, R])
        mask_bf = sb("mask_bf", [R, R], bf16)
        ident_bf = sb("ident_bf", [R, R], bf16)
        iota_e = sb("iota_e", [R, E])
        minus_half = sb("minus_half", [R, NH])
        lin_w = sb("lin_w", [128, KF, D])
        up_hi = sb("up_hi", [128, KD, 2 * INNER], f32r)
        up_lo = sb("up_lo", [128, KD, 2 * INNER], f32r)
        down_w = sb("down_w", [128, KI, D])
        sgu_hi = sb("sgu_hi", [128, KD, 2 * I], f32r)
        sgu_lo = sb("sgu_lo", [128, KD, 2 * I], f32r)
        sd_w = sb("sd_w", [128, KI, D])
        route_w = sb("route_w", [128, KD, E])
        pos_t = sb("pos_t", [128, KD, N + 1])
        col_t = sb("col_t", [128, KD, 3])
        posb = sb("posb", [128, KD, N])
        conv_t = sb("conv_t", [128, KI, TAPS + 1])
        chan_t = sb("chan_t", [128, KI, 2])
        gates_b = sb("gates_b", [R, 2 * NH])
        score_w = sb("score_w", [128, KI, 128])
        v_w = sb("v_w", [128, KI, 128])
        gx_w = sb("gx_w", [128, KI, 2 * NH])
        gm_w = sb("gm_w", [128, KI, 2 * NH])

        patch = sb("patch", [128, KF, GS * N])
        h_t = sb("h_t", [128, KD, GS, S])
        h_rows = sb("h_rows", [R, 2, NT, D])
        stats1 = sb("stats1", [R, NT, 6])
        mv1 = sb("mv1", [R, NT, 2])
        rstd1 = sb("rstd1", [R, NT])
        xn = sb("xn", [R, NT, D])
        xn_hi = sb("xn_hi", [128, KD, GT], f32r)
        xn_lo = sb("xn_lo", [128, KD, GT], f32r)
        xm = sb("xm", [128, 2, KI, GS, S])
        tanh_z = sb("tanh_z", [128, KI, GT])
        silu_z = sb("silu_z", [128, 2, KI, GT])
        y = sb("y", [128, KI, GS, S])
        tanh_y = sb("tanh_y", [128, KI, GT])
        x_act = sb("x_act", [128, 2, KI, GT])
        q_t = sb("q_t", [128, KI, GT])
        v = sb("v", [R, NT, INNER])
        gl = sb("gl", [R, NT, 2 * NH])
        fabs = sb("fabs", [R, NT, NH])
        fexp = sb("fexp", [R, NT, NH])
        fln = sb("fln", [R, NT, NH])
        logf = sb("logf", [R, NT, NH])
        fsum = sb("fsum", [R, NT, NH])
        a_gate = sb("a_gate", [R, NT, NH])
        diag = sb("diag", [R, NT, NH, R])
        cw = sb("cw", [R, NT, NH, R])
        minus_max = sb("minus_max", [R, NT, NH])
        row_sum = sb("row_sum", [R, NT, NH])
        m_d = sb("m_d", [R, NT, NH])
        exp_md = sb("exp_md", [R, NT, NH])
        norm = sb("norm", [R, NT, NH])
        norm2 = sb("norm2", [R, NT, NH])
        cw_t = sb("cw_t", [R, NT, NH * R])
        o = sb("o", [R, NT, NH, 128])
        stats_h = sb("stats_h", [R, NT, NH, 6])
        mv_h = sb("mv_h", [R, NT, NH, 2])
        var_h = sb("var_h", [R, NT, NH])
        rstd_h = sb("rstd_h", [R, NT, NH])
        shift_h = sb("shift_h", [R, NT, NH])
        hst = sb("hst", [128, KI, GT])
        att_t = sb("att_t", [128, KD, GT])
        h2 = sb("h2", [R, 2, NT, D])
        stats2 = sb("stats2", [R, NT, 6])
        mv2 = sb("mv2", [R, NT, 2])
        rstd2 = sb("rstd2", [R, NT])
        xn2 = sb("xn2", [R, NT, D])
        xn2_hi = sb("xn2_hi", [128, KD, GT], f32r)
        xn2_lo = sb("xn2_lo", [128, KD, GT], f32r)
        logits = sb("logits", [R, NT, E])
        top = sb("top", [R, NT, 8])
        top_i = sb("top_i", [R, NT, 8], u32)
        top_f = sb("top_f", [R, NT])
        tanh_s = sb("tanh_s", [R, NT])
        score = sb("score", [R, NT])
        xs_rows = sb("xs_rows", [R, NT, D])
        tanh_g = sb("tanh_g", [128, 2, GT])
        silu_g = sb("silu_g", [128, 2, GT])
        act_t = sb("act_t", [128, KI, GT])
        ffn_t = sb("ffn_t", [128, KD, GT])
        base_rows = sb("base_rows", [R, NT, D])
        def within(buffer, pattern, at, shape):
            flat = buffer[:].rearrange(pattern)
            names = "abc"[:len(shape)]
            sizes = {c: n for c, n in zip(names[:-1], shape[:-1])}
            size = int(np.prod(shape))
            return flat[:, at:at + size].rearrange(f"p ({' '.join(names)}) -> p {' '.join(names)}", **sizes)

        up_raw = within(xm, "p a k s t -> p (a k s t)", 0, [KD, 2 * INNER])
        sgu_raw = within(silu_z, "p a k n -> p (a k n)", 0, [KD, 2 * I])
        q_raw = within(tanh_y, "p k n -> p (k n)", 0, [KI, 128])
        k_raw = within(tanh_y, "p k n -> p (k n)", KI * 128, [KI, 128])
        v_raw = within(tanh_z, "p k n -> p (k n)", 0, [KI, 128])
        g_raw = within(tanh_z, "p k n -> p (k n)", KI * 128, [3, KI, 2 * NH])

        s_w_emb = sem("s_w_emb")
        s_w_front = sem("s_w_front")
        s_w_att = sem("s_w_att")
        s_w_ffn = sem("s_w_ffn")
        s_passed = sem("s_passed")
        s_const = sem("s_const")
        s_prep_mm = sem("s_prep_mm")
        s_prep = sem("s_prep")
        s_patch = sem("s_patch")
        s_emb_mm = sem("s_emb_mm")
        s_ht = sem("s_ht")
        s_h_mm = sem("s_h_mm")
        s_hrows = sem("s_hrows")
        s_st1 = sem("s_st1")
        s_mv1 = sem("s_mv1")
        s_ve1 = sem("s_ve1")
        s_rstd1 = sem("s_rstd1")
        s_xn = sem("s_xn")
        s_xnt_mm = sem("s_xnt_mm")
        s_xnt = sem("s_xnt")
        s_xnl = sem("s_xnl")
        s_split = sem("s_split")
        s_up_mm = sem("s_up_mm")
        s_xm = sem("s_xm")
        s_tz = sem("s_tz")
        s_sz = sem("s_sz")
        s_conv = sem("s_conv")
        s_ty = sem("s_ty")
        s_tyy = sem("s_tyy")
        s_xact = sem("s_xact")
        s_q_mm = sem("s_q_mm")
        s_q = sem("s_q")
        s_v_mm = sem("s_v_mm")
        s_v = sem("s_v")
        s_g_mm = sem("s_g_mm")
        s_gl = sem("s_gl")
        s_fabs = sem("s_fabs")
        s_fexp = sem("s_fexp")
        s_fln = sem("s_fln")
        s_logf = sem("s_logf")
        s_f_mm = sem("s_f_mm")
        s_fsum = sem("s_fsum")
        s_a = sem("s_a")
        s_diag = sem("s_diag")
        s_b_mm = sem("s_b_mm")
        s_c_mm = sem("s_c_mm")
        s_max = sem("s_max")
        s_dmat = sem("s_dmat")
        s_cw = sem("s_cw")
        s_sum = sem("s_sum")
        s_md = sem("s_md")
        s_expmd = sem("s_expmd")
        s_norm = sem("s_norm")
        s_ct_mm = sem("s_ct_mm")
        s_ct = sem("s_ct")
        s_pv_mm = sem("s_pv_mm")
        s_o = sem("s_o")
        s_sth = sem("s_sth")
        s_mvh = sem("s_mvh")
        s_varh = sem("s_varh")
        s_rstdh = sem("s_rstdh")
        s_shift = sem("s_shift")
        s_hn = sem("s_hn")
        s_hn_act = sem("s_hn_act")
        s_skip = sem("s_skip")
        s_hnt_mm = sem("s_hnt_mm")
        s_hmix = sem("s_hmix")
        s_hst = sem("s_hst")
        s_wd_mm = sem("s_wd_mm")
        s_att = sem("s_att")
        s_at_mm = sem("s_at_mm")
        s_h2 = sem("s_h2")
        s_st2 = sem("s_st2")
        s_mv2 = sem("s_mv2")
        s_ve2 = sem("s_ve2")
        s_rstd2 = sem("s_rstd2")
        s_xn2 = sem("s_xn2")
        s_xn2t_mm = sem("s_xn2t_mm")
        s_xn2t = sem("s_xn2t")
        s_xn2l = sem("s_xn2l")
        s_rt_mm = sem("s_rt_mm")
        s_lgt = sem("s_lgt")
        s_top = sem("s_top")
        s_topi = sem("s_topi")
        s_topf = sem("s_topf")
        s_hot = sem("s_hot")
        s_ts = sem("s_ts")
        s_score = sem("s_score")
        s_xs = sem("s_xs")
        s_xs_out = sem("s_xs_out")
        s_gu_mm = sem("s_gu_mm")
        s_tg = sem("s_tg")
        s_sg = sem("s_sg")
        s_act = sem("s_act")
        s_sd_mm = sem("s_sd_mm")
        s_ffn = sem("s_ffn")
        s_ft_mm = sem("s_ft_mm")
        s_base = sem("s_base")
        s_base_out = sem("s_base_out")

        CONV = KI * (TAPS - 1)

        def wait(eng, semaphore, value):
            if not isinstance(value, int) or value > 0:
                eng.wait_ge(semaphore, value)

        def wait_apart(eng, semaphore, value):
            eng.wait_ge(semaphore, value)
            if not isinstance(value, int):
                eng.sem_inc(s_passed, 1)

        def pipeline(eng, step):
            step(Group(0, 0), None, None, None)
            step(Group(1, 1), Group(0, 0), None, None)
            step(Group(2, 0), Group(1, 1), Group(0, 0), None)
            with eng.Fori(0, (G - 4) // 2) as j:
                step(Group(2 * j + 3, 1), Group(2 * j + 2, 0), Group(2 * j + 1, 1), Group(2 * j, 0))
                step(Group(2 * j + 4, 0), Group(2 * j + 3, 1), Group(2 * j + 2, 0), Group(2 * j + 1, 1))
            step(Group(G - 1, 1), Group(G - 2, 0), Group(G - 3, 1), Group(G - 4, 0))
            step(None, Group(G - 1, 1), Group(G - 2, 0), Group(G - 3, 1))
            step(None, None, Group(G - 1, 1), Group(G - 2, 0))
            step(None, None, None, Group(G - 1, 1))

        with nc.Block() as block:

            @block.sync
            def _(sp):
                sp.dma_start(lin_w[:], w_lin).then_inc(s_w_emb, 16)

                def load_patches(f):
                    wait(sp, s_emb_mm, KD * f.n)
                    src = patches[bass.ds(f.n, 1)].rearrange("g p (k n) -> p (g k) n", k=KF)
                    sp.dma_start(patch[:], src).then_inc(s_patch, 16)

                load_patches(Group(0, 0))
                for dst, src in [(pos_t, pos), (col_t, cols)]:
                    sp.dma_start(dst[:], src).then_inc(s_w_emb, 16)
                for dst, src in [(up_raw, w_up), (conv_t[:], conv), (chan_t[:], chan)]:
                    sp.dma_start(dst, src).then_inc(s_w_front, 16)

                def step(e, f, a, m):
                    if m is not None:
                        sp.wait_ge(s_xs, NT * m.n + NT)
                        dst = xs_dram[bass.ds(m.n * GT, GT), :].rearrange("(j p) d -> p j d", p=R)
                        sp.dma_start(dst, xs_rows[:]).then_inc(s_xs_out, 16)
                        sp.wait_ge(s_base, 2 * m.n + 2)
                        dst = base_dram[bass.ds(m.n * GT, GT), :].rearrange("(j p) d -> p j d", p=R)
                        sp.dma_start(dst, base_rows[:]).then_inc(s_base_out, 16)
                    if e is not None and not (isinstance(e.n, int) and e.n == G - 1):
                        load_patches(Group(e.n + 1, 1 - e.p))

                pipeline(sp, step)
                sp.wait_ge(s_xs_out, 16 * G + 16)
                sp.wait_ge(s_base_out, 16 * G + 16)

            @block.gpsimd
            def _(pool):
                pool.sem_inc(s_xs_out, 16)
                pool.sem_inc(s_base_out, 16)
                pool.memset(ident[:], 0.0).then_inc(s_const, 1)
                pool.memset(tri[:], 1.0).then_inc(s_const, 1)
                pool.memset(mask[:], 0.0).then_inc(s_const, 1)
                pool.memset(ones[:], 1.0).then_inc(s_const, 1)
                pool.memset(minus_half[:], -0.5).then_inc(s_const, 1)
                pool.iota(iota_e[:], pattern=[[1, E]], base=0, channel_multiplier=0,
                          allow_small_or_imprecise_dtypes=True).then_inc(s_const, 1)
                pool.wait_ge(s_const, 6)
                pool.affine_select(out=ident[:], in_=ident[:], compare_op=ALU.not_equal, fill=1.0,
                                   base=0, pattern=[[-1, 128]], channel_multiplier=1).then_inc(s_const, 1)
                pool.affine_select(out=tri[:], in_=tri[:], compare_op=ALU.is_ge, fill=0.0,
                                   base=0, pattern=[[1, R]], channel_multiplier=-1).then_inc(s_const, 1)
                pool.affine_select(out=mask[:], in_=mask[:], compare_op=ALU.is_ge, fill=MASKED,
                                   base=0, pattern=[[-1, R]], channel_multiplier=1).then_inc(s_const, 1)
                pool.wait_ge(s_const, 9)
                pool.affine_select(out=tri[:, S:R], in_=tri[:, S:R], compare_op=ALU.is_ge, fill=0.0,
                                   base=-S, pattern=[[0, S]], channel_multiplier=1).then_inc(s_const, 1)
                pool.affine_select(out=mask[:, 0:S], in_=mask[:, 0:S], compare_op=ALU.is_ge, fill=MASKED,
                                   base=S - 1, pattern=[[0, S]], channel_multiplier=-1).then_inc(s_const, 1)
                pool.wait_ge(s_const, 11)
                pool.tensor_copy(mask_bf[:], mask[:]).then_inc(s_const, 1)
                pool.tensor_copy(ident_bf[:], ident[0:R, 0:R]).then_inc(s_const, 1)

                def rstd1_of(f):
                    wait_apart(pool, s_mv1, NT * f.n + NT)
                    pool.tensor_scalar(rstd1[:], mv1[:, :, 1], 1e-5, None, ALU.add).then_inc(s_ve1, 1)
                    pool.wait_ge(s_ve1, f.n + 1)
                    pool.tensor_tensor(rstd1[:], rstd1[:], minus_half[:], ALU.pow).then_inc(s_rstd1, 1)

                def rstd2_of(m):
                    wait_apart(pool, s_mv2, NT * m.n + NT)
                    pool.tensor_scalar(rstd2[:], mv2[:, :, 1], 1e-5, None, ALU.add).then_inc(s_ve2, 1)
                    pool.wait_ge(s_ve2, m.n + 1)
                    pool.tensor_tensor(rstd2[:], rstd2[:], minus_half[:], ALU.pow).then_inc(s_rstd2, 1)

                def skip_of(a):
                    wait(pool, s_wd_mm, KD * a.n)
                    wait_apart(pool, s_xact, KI * a.n + KI)
                    for h in range(NH):
                        pool.tensor_scalar(hst[:, h, :], x_act[:, a.p, h, :], chan_t[:, h, 1:2], None,
                                           ALU.mult).then_inc(s_skip, 1)

                def x_act_of(f, pair):
                    for k in (2 * pair, 2 * pair + 1):
                        pool.wait_ge(s_ty, KI * f.n + k + 1)
                        half = y[:, k].rearrange("p s t -> p (s t)")
                        pool.tensor_tensor(tanh_y[:, k, :], tanh_y[:, k, :], half, ALU.mult).then_inc(s_tyy, 1)
                        pool.wait_ge(s_tyy, KI * f.n + k + 1)
                        pool.tensor_tensor(x_act[:, f.p, k, :], tanh_y[:, k, :], half, ALU.add).then_inc(s_xact, 1)

                def rstd_h_of(a, j):
                    pool.wait_ge(s_varh, NT * a.n + j + 1)
                    pool.tensor_tensor(rstd_h[:, j, :], var_h[:, j, :], minus_half[:],
                                       ALU.pow).then_inc(s_rstdh, 1)

                def step(e, f, a, m):
                    if m: rstd2_of(m)
                    if f: rstd1_of(f)
                    if a: skip_of(a)
                    if f: x_act_of(f, 0)
                    if a:
                        rstd_h_of(a, 0)
                        rstd_h_of(a, 1)
                        rstd_h_of(a, 2)
                        rstd_h_of(a, 3)
                    if f: x_act_of(f, 1)

                pipeline(pool, step)

            @block.scalar
            def _(act):
                bias = b_gates.partition_broadcast(R)
                act.wait_ge(s_w_emb, 3 * 16)
                for dst, src in [(q_raw, wq), (k_raw, wk), (v_raw, wv), (v_w[:], wvt), (g_raw, w_gates),
                                 (gates_b[:], bias)]:
                    act.dma_start(dst, src).then_inc(s_w_att, 16)
                for dst, src in [(down_w[:], w_down), (route_w[:], w_route), (sgu_raw, w_sgu), (sd_w[:], w_sd)]:
                    act.dma_start(dst, src).then_inc(s_w_ffn, 16)

                def copy(dst, src):
                    return act.activation(dst, src, ACT.Copy)

                def split_weights():
                    act.wait_ge(s_prep, 8)
                    copy(up_hi[:], up_raw).then_inc(s_split, 1)
                    act.wait_ge(s_prep, 9)
                    copy(sgu_hi[:], sgu_raw).then_inc(s_split, 1)
                    act.wait_ge(s_prep_mm, 2)

                def h_rows_of(f):
                    for b in range(2):
                        act.wait_ge(s_h_mm, 2 * f.n + b + 1)
                        copy(h_rows[:, f.p, 2 * b:2 * b + 2, :].rearrange("p j d -> p (j d)"),
                             fb[b][0:R, :]).then_inc(s_hrows, 1)

                def xn_t_of(f):
                    for c in range(KD):
                        act.wait_ge(s_xnt_mm, KD * f.n + c + 1)
                        copy(xn_hi[:, c, :], fb[c][:, 0:GT]).then_inc(s_xnt, 1)

                def xm_of(f, k):
                    act.wait_ge(s_up_mm, 2 * KI * f.n + k + 1)
                    if k == 0:
                        wait(act, s_xact, KI * f.n)
                    act.activation(y[:, k].rearrange("p s t -> p (s t)"), fb[k % 2][:, 0:GT], ACT.Identity,
                                   bias=conv_t[:, k, TAPS:TAPS + 1], scale=conv_t[:, k, TAPS - 1:TAPS])
                    copy(xm[:, f.p, k].rearrange("p s t -> p (s t)"), fb[k % 2][:, 0:GT]).then_inc(s_xm, 1)

                def tanh_z_of(f, k):
                    act.wait_ge(s_up_mm, 2 * KI * f.n + KI + k + 1)
                    act.activation(tanh_z[:, k, :], fb[k % 2][:, 0:GT], ACT.Tanh).then_inc(s_tz, 1)

                def tanh_y_of(f, pair):
                    act.wait_ge(s_conv, CONV * f.n + CONV // 2 * (pair + 1))
                    for k in (2 * pair, 2 * pair + 1):
                        act.activation(tanh_y[:, k, :], y[:, k].rearrange("p s t -> p (s t)"),
                                       ACT.Tanh).then_inc(s_ty, 1)

                def q_of(a):
                    for h in range(NH):
                        act.wait_ge(s_q_mm, NH * a.n + h + 1)
                        act.activation(q_t[:, h, :], ab[h][:, 0:GT], ACT.Copy,
                                       scale=float(INNER // NH) ** -0.5).then_inc(s_q, 1)

                def v_of(a, j):
                    act.wait_ge(s_v_mm, NT * a.n + j + 1)
                    copy(v[:, j, :], ab[j][0:R, :]).then_inc(s_v, 1)

                def log_f(a):
                    act.wait_ge(s_fabs, a.n + 1)
                    act.activation(fexp[:], fabs[:], ACT.Exp, scale=-1.0).then_inc(s_fexp, 1)
                    act.wait_ge(s_fexp, a.n + 1)
                    act.activation(fln[:], fexp[:], ACT.Ln, bias=1.0).then_inc(s_fln, 1)

                def decay(a, j):
                    act.wait_ge(s_max, NT * a.n + j + 1)
                    for h in range(NH):
                        act.activation(cw[:, j, h, :], ab[2 * (j % 2)][0:R, h * R:(h + 1) * R], ACT.Exp,
                                       bias=minus_max[:, j, h:h + 1]).then_inc(s_dmat, 1)

                def exp_m_d(a):
                    act.wait_ge(s_md, a.n + 1)
                    act.activation(exp_md[:], m_d[:], ACT.Exp).then_inc(s_expmd, 1)

                def cw_t_of(a, j):
                    act.wait_ge(s_ct_mm, NT * a.n + j + 1)
                    copy(cw_t[:, j, :], ab[j][0:R, 0:GT]).then_inc(s_ct, 1)

                def o_of(a, j):
                    act.wait_ge(s_pv_mm, NT * a.n + j + 1)
                    copy(o[:, j].rearrange("p h d -> p (h d)"), ab[j][0:R, :]).then_inc(s_o, 1)

                def head_norm(a, j):
                    act.wait_ge(s_shift, 2 * a.n + j + 1)
                    for h in range(NH):
                        act.activation(o[:, j, h, :], o[:, j, h, :], ACT.Identity, bias=shift_h[:, j, h:h + 1],
                                       scale=rstd_h[:, j, h:h + 1]).then_inc(s_hn_act, 1)

                def att_t_of(a):
                    for c in range(KD):
                        act.wait_ge(s_wd_mm, KD * a.n + c + 1)
                        copy(att_t[:, c, :], ab[c][:, 0:GT]).then_inc(s_att, 1)

                def xn2_t_of(m):
                    for c in range(KD):
                        act.wait_ge(s_xn2t_mm, KD * m.n + c + 1)
                        copy(xn2_hi[:, c, :], mb[c][:, 0:GT]).then_inc(s_xn2t, 1)

                def tanh_score(m):
                    act.wait_ge(s_top, NT * m.n + NT)
                    act.activation(tanh_s[:], top[:, :, 0], ACT.Tanh, scale=0.5).then_inc(s_ts, 1)

                def score_rows(m):
                    act.wait_ge(s_score, m.n + 1)
                    act.wait_ge(s_xs_out, 16 * m.n + 16)
                    for j in range(NT):
                        act.activation(xs_rows[:, j, :], xn2[:, j, :], ACT.Copy,
                                       scale=score[:, j:j + 1]).then_inc(s_xs, 1)

                def tanh_g_of(m, k):
                    act.wait_ge(s_gu_mm, 2 * KI * m.n + 2 * k + 1)
                    act.activation(tanh_g[:, k % 2, :], mb[0][:, 0:GT], ACT.Tanh).then_inc(s_tg, 1)

                def ffn_t_of(m):
                    for c in range(KD):
                        act.wait_ge(s_sd_mm, KD * m.n + c + 1)
                        copy(ffn_t[:, c, :], mb[c][:, 0:GT]).then_inc(s_ffn, 1)

                def step(e, f, a, m):
                    if f and isinstance(f.n, int) and f.n == 0:
                        split_weights()
                    if a: q_of(a)
                    if f: h_rows_of(f)
                    if a:
                        v_of(a, 0)
                        v_of(a, 1)
                        log_f(a)
                        v_of(a, 2)
                        v_of(a, 3)
                    if f: xn_t_of(f)
                    if m: xn2_t_of(m)
                    if f:
                        xm_of(f, 0)
                        xm_of(f, 1)
                        xm_of(f, 2)
                    if a:
                        decay(a, 0)
                        decay(a, 1)
                    if f: xm_of(f, 3)
                    if a: decay(a, 2)
                    if m:
                        tanh_score(m)
                        tanh_g_of(m, 0)
                    if a: decay(a, 3)
                    if m: tanh_g_of(m, 1)
                    if a:
                        exp_m_d(a)
                        cw_t_of(a, 0)
                        cw_t_of(a, 1)
                    if f:
                        tanh_y_of(f, 0)
                        tanh_z_of(f, 0)
                    if a:
                        o_of(a, 0)
                        o_of(a, 1)
                    if m: tanh_g_of(m, 2)
                    if a:
                        cw_t_of(a, 2)
                        cw_t_of(a, 3)
                    if f:
                        tanh_y_of(f, 1)
                        tanh_z_of(f, 1)
                    if a:
                        o_of(a, 2)
                        o_of(a, 3)
                    if m: tanh_g_of(m, 3)
                    if a: head_norm(a, 0)
                    if f: tanh_z_of(f, 2)
                    if a: head_norm(a, 1)
                    if f: tanh_z_of(f, 3)
                    if m:
                        ffn_t_of(m)
                        score_rows(m)
                    if a: att_t_of(a)

                pipeline(act, step)

            @block.vector
            def _(dve):
                dve.wait_ge(s_w_emb, 3 * 16)
                for c in range(KD):
                    dve.tensor_scalar(posb[:, c, :], pos_t[:, c, 1:], col_t[:, c, 0:1], None,
                                      ALU.add).then_inc(s_prep, 1)
                    dve.tensor_copy(h_t[:, c, :, 0], col_t[:, c, 2:3].broadcast_to([128, GS])).then_inc(s_prep, 1)
                    dve.tensor_scalar(h_t[:, c, :, 1], pos_t[:, c, 0:1].broadcast_to([128, GS]),
                                      col_t[:, c, 1:2], None, ALU.add).then_inc(s_prep, 1)
                dve.wait_ge(s_prep, 6)

                def halve_front():
                    dve.wait_ge(s_w_front, 3 * 16)
                    dve.tensor_scalar(conv_t[:], conv_t[:], 0.5, None, ALU.mult).then_inc(s_prep, 1)
                    dve.tensor_scalar(up_raw[:, :, INNER:], up_raw[:, :, INNER:], 0.5, None, ALU.mult).then_inc(s_prep, 1)
                    dve.wait_ge(s_w_ffn, 4 * 16)
                    dve.tensor_scalar(sgu_raw[:, :, 0:I], sgu_raw[:, :, 0:I], 0.5, None, ALU.mult).then_inc(s_prep, 1)
                    dve.wait_ge(s_split, 1)
                    dve.tensor_tensor(up_lo[:], up_raw, up_hi[:].bitcast(f32), ALU.subtract).then_inc(s_prep, 1)
                    dve.wait_ge(s_split, 2)
                    dve.tensor_tensor(sgu_lo[:], sgu_raw, sgu_hi[:].bitcast(f32), ALU.subtract).then_inc(s_prep, 1)

                def merge_weights():
                    dve.wait_ge(s_prep_mm, 1)
                    dve.tensor_copy(score_w[:].rearrange("p h d -> p (h d)"), ab[0][:, :]).then_inc(s_prep, 1)
                    dve.wait_ge(s_prep_mm, 2)
                    dve.tensor_copy(gx_w[:].rearrange("p h g -> p (h g)"), ab[1][:, 0:32]).then_inc(s_prep, 1)
                    dve.tensor_copy(gm_w[:].rearrange("p h g -> p (h g)"), ab[1][:, 32:64]).then_inc(s_prep, 1)

                def embed(f):
                    for c in range(KD):
                        dve.wait_ge(s_emb_mm, KD * f.n + c + 1)
                        dve.tensor_tensor(h_t[:, c, :, 2:],
                                          fb[c][:, 0:GS * N].rearrange("p (s n) -> p s n", n=N),
                                          posb[:, c].unsqueeze(1).broadcast_to([128, GS, N]),
                                          ALU.add).then_inc(s_ht, 1)

                def ln1_stats(f):
                    for j in range(NT):
                        if j % 2 == 0:
                            dve.wait_ge(s_hrows, 2 * f.n + j // 2 + 1)
                        dve.bn_stats(stats1[:, j, :], h_rows[:, f.p, j, :]).then_inc(s_st1, 1)
                    for j in range(NT):
                        wait_apart(dve, s_st1, NT * f.n + j + 1)
                        dve.bn_aggr(mv1[:, j, :], stats1[:, j, :]).then_inc(s_mv1, 1)

                def xn_of(f):
                    dve.wait_ge(s_rstd1, f.n + 1)
                    for j in range(NT):
                        dve.tensor_scalar(xn[:, j, :], h_rows[:, f.p, j, :], mv1[:, j, 0:1], rstd1[:, j:j + 1],
                                          ALU.subtract, ALU.mult).then_inc(s_xn, 1)

                def xn_lo_of(f):
                    for c in range(KD):
                        dve.wait_ge(s_xnt, KD * f.n + c + 1)
                        dve.tensor_tensor(xn_lo[:, c, :], fb[c][:, 0:GT], xn_hi[:, c, :].bitcast(f32),
                                          ALU.subtract).then_inc(s_xnl, 1)

                def conv_of(f, pair, lags):
                    for lag in lags:
                        for e in range(2):
                            k = 2 * pair + e
                            w = conv_t[:, k, TAPS - 1 - lag:TAPS - lag]
                            if lag == 1:
                                dve.wait_ge(s_xm, KI * f.n + k + 1)
                            else:
                                dve.wait_ge(s_conv, CONV * f.n + CONV // 2 * pair + 2 * (lag - 2) + e + 1)
                            dve.scalar_tensor_tensor(y[:, k, :, lag:], xm[:, f.p, k, :, 0:S - lag], w,
                                                     y[:, k, :, lag:], ALU.mult, ALU.add).then_inc(s_conv, 1)

                def silu_z_of(f, k):
                    dve.wait_ge(s_tz, KI * f.n + k + 1)
                    dve.scalar_tensor_tensor(silu_z[:, f.p, k, :], tanh_z[:, k, :], 1.0, fb[k % 2][:, 0:GT],
                                             ALU.add, ALU.mult).then_inc(s_sz, 1)

                def gates_of(a):
                    dve.wait_ge(s_g_mm, a.n + 1)
                    dve.tensor_tensor(gl[:], mb[1][0:R, 0:32].rearrange("p (j g) -> p j g", j=NT),
                                      gates_b[:].unsqueeze(1).broadcast_to([R, NT, 2 * NH]), ALU.add).then_inc(s_gl, 1)
                    dve.wait_ge(s_gl, a.n + 1)
                    dve.scalar_tensor_tensor(fabs[:], gl[:, :, NH:], -1.0, gl[:, :, NH:], ALU.mult,
                                             ALU.max).then_inc(s_fabs, 1)

                def log_f(a):
                    dve.wait_ge(s_fln, a.n + 1)
                    dve.scalar_tensor_tensor(logf[:], gl[:, :, NH:], 0.0, fln[:], ALU.min,
                                             ALU.subtract).then_inc(s_logf, 1)

                def a_of(a):
                    dve.wait_ge(s_f_mm, a.n + 1)
                    sums = ab[1][0:R, 0:NT * NH].rearrange("p (j h) -> p j h", j=NT)
                    dve.tensor_tensor(a_gate[:], gl[:, :, 0:NH], sums, ALU.subtract).then_inc(s_a, 1)
                    dve.tensor_copy(fsum[:], sums).then_inc(s_fsum, 1)

                def diag_of(a, j):
                    dve.wait_ge(s_a, a.n + 1)
                    dve.tensor_tensor(diag[:, j], ident[0:R, 0:R].unsqueeze(1).broadcast_to([R, NH, R]),
                                      a_gate[:, j].unsqueeze(2).broadcast_to([R, NH, R]), ALU.mult).then_inc(s_diag, 1)

                def decay(a, j):
                    n = NT * a.n + j + 1
                    dve.wait_ge(s_b_mm, n)
                    dve.tensor_reduce(minus_max[:, j, :], ab[2 * (j % 2)][0:R, 0:GT].rearrange("p (h t) -> p h t", h=NH),
                                      AX.X, ALU.max, negate=True).then_inc(s_max, 1)

                def weigh(a, j):
                    n = NT * a.n + j + 1
                    dve.wait_ge(s_dmat, NH * n)
                    dve.wait_ge(s_c_mm, n)
                    dve.tensor_tensor(cw[:, j], ab[2 * (j % 2) + 1][0:R, 0:GT].rearrange("p (h t) -> p h t", h=NH),
                                      cw[:, j], ALU.mult).then_inc(s_cw, 1)
                    dve.wait_ge(s_cw, n)
                    dve.tensor_reduce(row_sum[:, j, :], cw[:, j], AX.X, ALU.add).then_inc(s_sum, 1)

                def norm_1(a):
                    dve.wait_ge(s_max, NT * a.n + NT)
                    dve.tensor_tensor(m_d[:], minus_max[:], fsum[:], ALU.subtract).then_inc(s_md, 1)

                def norm_2(a):
                    dve.wait_ge(s_sum, NT * a.n + NT)
                    dve.wait_ge(s_expmd, a.n + 1)
                    dve.scalar_tensor_tensor(norm[:], row_sum[:], -1.0, row_sum[:], ALU.mult,
                                             ALU.max).then_inc(s_norm, 1)
                    dve.wait_ge(s_norm, 4 * a.n + 1)
                    dve.tensor_tensor(norm[:], norm[:], exp_md[:], ALU.max).then_inc(s_norm, 1)
                    dve.wait_ge(s_norm, 4 * a.n + 2)
                    dve.tensor_scalar(norm[:], norm[:], 1e-6, None, ALU.add).then_inc(s_norm, 1)
                    dve.wait_ge(s_norm, 4 * a.n + 3)
                    dve.tensor_tensor(norm2[:], norm[:], norm[:], ALU.mult).then_inc(s_norm, 1)

                def head_stats(a, j):
                    dve.wait_ge(s_o, NT * a.n + j + 1)
                    for h in range(NH):
                        dve.bn_stats(stats_h[:, j, h, :], o[:, j, h, :]).then_inc(s_sth, 1)
                    wait_apart(dve, s_sth, NT * NH * a.n + NH * j + NH)
                    for h in range(NH):
                        dve.bn_aggr(mv_h[:, j, h, :], stats_h[:, j, h, :]).then_inc(s_mvh, 1)

                def head_var(a, j):
                    dve.wait_ge(s_mvh, NT * NH * a.n + NH * j + NH)
                    if j == 0:
                        dve.wait_ge(s_norm, 4 * a.n + 4)
                    dve.scalar_tensor_tensor(var_h[:, j, :], norm2[:, j, :], 1e-6, mv_h[:, j, :, 1], ALU.mult,
                                             ALU.add).then_inc(s_varh, 1)

                def head_shift(a, j):
                    wait_apart(dve, s_rstdh, NT * a.n + j + 1)
                    dve.scalar_tensor_tensor(shift_h[:, j, :], mv_h[:, j, :, 0], -1.0, rstd_h[:, j, :],
                                             ALU.mult, ALU.mult).then_inc(s_shift, 1)

                def head_norm(a, j):
                    dve.wait_ge(s_rstdh, NT * a.n + j + 1)
                    for h in range(NH):
                        dve.tensor_scalar(o[:, j, h, :], o[:, j, h, :], mv_h[:, j, h, 0:1],
                                          rstd_h[:, j, h:h + 1], ALU.subtract, ALU.mult).then_inc(s_hn, 1)

                def state(a):
                    dve.wait_ge(s_skip, NH * a.n + NH)
                    for h in range(NH):
                        if h == 0:
                            dve.wait_ge(s_hnt_mm, a.n + 1)
                        dve.scalar_tensor_tensor(hst[:, h, :], ab[h][:, 0:GT], chan_t[:, h, 0:1], hst[:, h, :],
                                                 ALU.mult, ALU.add).then_inc(s_hmix, 1)
                        dve.wait_ge(s_hmix, NH * a.n + h + 1)
                        dve.tensor_tensor(hst[:, h, :], hst[:, h, :], silu_z[:, a.p, h, :],
                                          ALU.mult).then_inc(s_hst, 1)

                def h2_of(a):
                    for b in range(2):
                        dve.wait_ge(s_at_mm, 2 * a.n + b + 1)
                        dve.tensor_tensor(h2[:, a.p, 2 * b:2 * b + 2, :],
                                          ab[2 + b][0:R, :].rearrange("p (j d) -> p j d", j=2),
                                          h_rows[:, a.p, 2 * b:2 * b + 2, :], ALU.add).then_inc(s_h2, 1)

                def ln2_stats(m):
                    for j in range(NT):
                        if j % 2 == 0:
                            dve.wait_ge(s_h2, 2 * m.n + j // 2 + 1)
                        dve.bn_stats(stats2[:, j, :], h2[:, m.p, j, :]).then_inc(s_st2, 1)
                    for j in range(NT):
                        wait_apart(dve, s_st2, NT * m.n + j + 1)
                        dve.bn_aggr(mv2[:, j, :], stats2[:, j, :]).then_inc(s_mv2, 1)

                def xn2_of(m):
                    dve.wait_ge(s_rstd2, m.n + 1)
                    for j in range(NT):
                        dve.tensor_scalar(xn2[:, j, :], h2[:, m.p, j, :], mv2[:, j, 0:1], rstd2[:, j:j + 1],
                                          ALU.subtract, ALU.mult).then_inc(s_xn2, 1)

                def xn2_lo_of(m):
                    for c in range(KD):
                        dve.wait_ge(s_xn2t, KD * m.n + c + 1)
                        dve.tensor_tensor(xn2_lo[:, c, :], mb[c][:, 0:GT], xn2_hi[:, c, :].bitcast(f32),
                                          ALU.subtract).then_inc(s_xn2l, 1)

                def route(m):
                    dve.wait_ge(s_rt_mm, m.n + 1)
                    dve.tensor_copy(logits[:].rearrange("p j e -> p (j e)"), mb[0][0:R, 0:NT * E]).then_inc(s_lgt, 1)
                    wait_apart(dve, s_lgt, m.n + 1)
                    for j in range(NT):
                        dve.max(top[:, j, :], logits[:, j, :]).then_inc(s_top, 1)
                    for j in range(NT):
                        wait_apart(dve, s_top, NT * m.n + j + 1)
                        dve.max_index(top_i[:, j, :], top[:, j, :], logits[:, j, :]).then_inc(s_topi, 1)
                    dve.wait_ge(s_topi, NT * m.n + NT)
                    dve.tensor_copy(top_f[:], top_i[:, :, 0]).then_inc(s_topf, 1)
                    dve.wait_ge(s_topf, m.n + 1)
                    for j in range(NT):
                        dve.tensor_scalar(hot[:, bass.ds(NT * m.n + j, 1), :], iota_e[:].unsqueeze(1),
                                          top_f[:, j:j + 1], None, ALU.is_equal).then_inc(s_hot, 1)

                def score_of(m):
                    dve.wait_ge(s_ts, m.n + 1)
                    dve.tensor_scalar(score[:], tanh_s[:], 1.0, 0.5, ALU.add, ALU.mult).then_inc(s_score, 1)

                def expert_act(m, k):
                    dve.wait_ge(s_tg, KI * m.n + k + 1)
                    dve.scalar_tensor_tensor(silu_g[:, k % 2, :], tanh_g[:, k % 2, :], 1.0, mb[0][:, 0:GT],
                                             ALU.add, ALU.mult).then_inc(s_sg, 1)
                    dve.wait_ge(s_sg, KI * m.n + k + 1)
                    dve.wait_ge(s_gu_mm, 2 * KI * m.n + 2 * k + 2)
                    dve.tensor_tensor(act_t[:, k, :], silu_g[:, k % 2, :], mb[1][:, 0:GT], ALU.mult).then_inc(s_act, 1)

                def base_of(m):
                    dve.wait_ge(s_base_out, 16 * m.n + 16)
                    for b in range(2):
                        dve.wait_ge(s_ft_mm, 2 * m.n + b + 1)
                        dve.tensor_tensor(base_rows[:, 2 * b:2 * b + 2, :],
                                          mb[b][0:R, :].rearrange("p (j d) -> p j d", j=2),
                                          h2[:, m.p, 2 * b:2 * b + 2, :], ALU.add).then_inc(s_base, 1)

                def step(e, f, a, m):
                    if f and isinstance(f.n, int) and f.n == 0:
                        halve_front()
                        merge_weights()
                    if m: ln2_stats(m)
                    if f:
                        ln1_stats(f)
                        xn_of(f)
                    if a: gates_of(a)
                    if m: xn2_of(m)
                    if a: log_f(a)
                    if f: xn_lo_of(f)
                    if a:
                        a_of(a)
                        diag_of(a, 0)
                        diag_of(a, 1)
                    if m: xn2_lo_of(m)
                    if a:
                        diag_of(a, 2)
                        diag_of(a, 3)
                        decay(a, 0)
                    if f: conv_of(f, 0, (1,))
                    if a:
                        decay(a, 1)
                        weigh(a, 0)
                        weigh(a, 1)
                        decay(a, 2)
                    if m: route(m)
                    if a: decay(a, 3)
                    if m: expert_act(m, 0)
                    if f: conv_of(f, 0, (2,))
                    if a:
                        norm_1(a)
                        weigh(a, 2)
                        weigh(a, 3)
                    if m: expert_act(m, 1)
                    if a: norm_2(a)
                    if f:
                        conv_of(f, 0, (3,))
                        conv_of(f, 1, (1,))
                        conv_of(f, 1, (2, 3))
                        silu_z_of(f, 0)
                    if a:
                        head_stats(a, 0)
                        head_var(a, 0)
                    if m: expert_act(m, 2)
                    if a:
                        head_stats(a, 1)
                        head_var(a, 1)
                        head_shift(a, 0)
                    if f: silu_z_of(f, 1)
                    if m: expert_act(m, 3)
                    if a:
                        head_stats(a, 2)
                        head_var(a, 2)
                        head_shift(a, 1)
                        head_stats(a, 3)
                        head_var(a, 3)
                    if f: silu_z_of(f, 2)
                    if a: head_norm(a, 2)
                    if f: silu_z_of(f, 3)
                    if a: head_norm(a, 3)
                    if m:
                        score_of(m)
                        base_of(m)
                    if a: state(a)
                    if e: embed(e)
                    if a: h2_of(a)

                pipeline(dve, step)

            @block.tensor
            def _(pe):
                pe.wait_ge(s_const, 13)
                pe.wait_ge(s_w_emb, 3 * 16)

                def merge_weights():
                    pe.wait_ge(s_w_att, 6 * 16)
                    for h in range(NH):
                        last = pe.matmul(ab[0][:, h * 128:(h + 1) * 128], q_raw[:, h], k_raw[:, h],
                                         start=True, stop=True)
                    last.then_inc(s_prep_mm, 1)
                    for h in range(NH):
                        pe.matmul(ab[1][:, 8 * h:8 * h + 8], q_raw[:, h], g_raw[:, 0, h], start=True, stop=False)
                        pe.matmul(ab[1][:, 8 * h:8 * h + 8], k_raw[:, h], g_raw[:, 1, h], start=False, stop=True)
                    for h in range(NH):
                        last = pe.matmul(ab[1][:, 32 + 8 * h:40 + 8 * h], v_raw[:, h], g_raw[:, 2, h],
                                         start=True, stop=True)
                    last.then_inc(s_prep_mm, 1)
                    pe.wait_ge(s_prep, 14)

                def embed(f, c):
                    if c == 0:
                        pe.wait_ge(s_patch, 16 * f.n + 16)
                    wait(pe, s_sz, KI * f.n - 1 + c)
                    for k in range(KF):
                        last = pe.matmul(fb[c][:, 0:GS * N], lin_w[:, k, c * 128:(c + 1) * 128],
                                         patch[:, k, :], start=(k == 0), stop=(k == KF - 1))
                    last.then_inc(s_emb_mm, 1)

                def to_rows(dst, src, done):
                    for b in range(2):
                        for j in (2 * b, 2 * b + 1):
                            for c in range(KD):
                                last = pe.transpose(dst[b][0:R, (j % 2) * D + c * 128:(j % 2) * D + (c + 1) * 128],
                                                    src[:, c, j * R:(j + 1) * R], ident[:])
                        last.then_inc(done, 1)

                def h_rows_of(f):
                    pe.wait_ge(s_ht, KD * f.n + KD)
                    to_rows(fb, h_t[:].rearrange("p c s t -> p c (s t)"), s_h_mm)

                def to_columns(dst, src, ready, n, done, a=None):
                    for c in range(KD):
                        if a and c == 1:
                            pe.wait_ge(s_gl, a.n + 1)
                        for j in range(NT):
                            if c == 0:
                                pe.wait_ge(ready, NT * n + j + 1)
                            last = pe.transpose(dst[c][:, j * R:(j + 1) * R], src[:, j, c * 128:(c + 1) * 128],
                                                ident[0:R, 0:R])
                        last.then_inc(done, 1)

                def split_product(dst, weights, x, at):
                    n = 0
                    for w, part in ((0, 0), (1, 0), (0, 1)):
                        for c in range(KD):
                            last = pe.matmul(dst, weights[w][:, c, at:at + 128], x[part][:, c, :],
                                             start=(n == 0), stop=(n == 3 * KD - 1))
                            n += 1
                    return last

                def up(f, k):
                    if k < 2:
                        pe.wait_ge(s_xnl, KD * f.n + KD)
                    elif k < 2 + KI:
                        pe.wait_ge(s_xm, KI * f.n + k - 1)
                    else:
                        pe.wait_ge(s_sz, KI * f.n + k - KI - 1)
                    split_product(fb[k % 2][:, 0:GT], (up_hi, up_lo), (xn_hi, xn_lo), k * 128).then_inc(s_up_mm, 1)

                def q_of(a):
                    pe.wait_ge(s_xact, KI * a.n + KI)
                    for h in range(NH):
                        if h < 2:
                            wait(pe, s_att, KD * a.n)
                        else:
                            wait(pe, s_h2, 2 * a.n)
                        pe.matmul(ab[h][:, 0:GT], score_w[:, h], x_act[:, a.p, h, :],
                                  start=True, stop=True).then_inc(s_q_mm, 1)

                def xm_tile(a, h, j):
                    return xm[:, a.p, h, TS * j:TS * j + TS, :].rearrange("p s t -> p (s t)")

                def v_of(a, j):
                    pe.wait_ge(s_q, NH * a.n + j + 1)
                    for h in range(NH):
                        last = pe.matmul(ab[j][0:R, h * 128:(h + 1) * 128], xm_tile(a, h, j), v_w[:, h],
                                         start=True, stop=True)
                    last.then_inc(s_v_mm, 1)

                def gates_of(a, j):
                    if j == 0:
                        wait(pe, s_h2, 2 * a.n)
                    dst = mb[1][0:R, 8 * j:8 * j + 8]
                    for h in range(NH):
                        pe.matmul(dst, x_act[:, a.p, h, j * R:(j + 1) * R], gx_w[:, h], start=(h == 0), stop=False)
                    for h in range(NH):
                        last = pe.matmul(dst, xm_tile(a, h, j), gm_w[:, h], start=False, stop=(h == NH - 1))
                    if j == NT - 1:
                        last.then_inc(s_g_mm, 1)

                def f_sums(a):
                    pe.wait_ge(s_v, NT * a.n + 2)
                    pe.wait_ge(s_logf, a.n + 1)
                    pe.matmul(ab[1][0:R, 0:NT * NH], tri[:], logf[:].rearrange("p j h -> p (j h)"),
                              start=True, stop=True).then_inc(s_f_mm, 1)

                def scores(a, j):
                    pe.wait_ge(s_diag, NT * a.n + j + 1)
                    if j == 0:
                        pe.wait_ge(s_fsum, a.n + 1)
                    elif j == 1:
                        pe.wait_ge(s_v, NT * a.n + NT)
                    else:
                        pe.wait_ge(s_cw, NT * a.n + j - 1)
                    b = 2 * (j % 2)
                    pe.matmul(ab[b][0:R, 0:GT], ident_bf[:], mask_bf[:].unsqueeze(1).broadcast_to([R, NH, R]),
                              start=True, stop=False)
                    pe.matmul(ab[b][0:R, 0:GT], ones[0:R, 0:R], diag[:, j].rearrange("p h t -> p (h t)"),
                              start=False, stop=True).then_inc(s_b_mm, 1)
                    for h in range(NH):
                        last = pe.matmul(ab[b + 1][0:R, h * R:(h + 1) * R], q_t[:, h, j * R:(j + 1) * R],
                                         x_act[:, a.p, h, j * R:(j + 1) * R], start=True, stop=True)
                    last.then_inc(s_c_mm, 1)

                def cw_t_of(a, j):
                    pe.wait_ge(s_cw, NT * a.n + (NT if j > 1 else NT - 1))
                    for h in range(NH):
                        last = pe.transpose(ab[j][0:R, h * R:(h + 1) * R], cw[:, j, h, :], ident[0:R, 0:R])
                    last.then_inc(s_ct_mm, 1)

                def heads(a, j):
                    pe.wait_ge(s_ct, NT * a.n + j + 1)
                    for h in range(NH):
                        last = pe.matmul(ab[j][0:R, h * 128:(h + 1) * 128], cw_t[:, j, h * R:(h + 1) * R],
                                         v[:, j, h * 128:(h + 1) * 128], start=True, stop=True)
                    last.then_inc(s_pv_mm, 1)

                def heads_t(a):
                    pe.wait_ge(s_o, NT * a.n + NT)
                    for j in range(NT):
                        pe.wait_ge(s_hn_act if j < 2 else s_hn, NT * NH // 2 * a.n + NH * (j % 2 + 1))
                        for h in range(NH):
                            last = pe.transpose(ab[h][:, j * R:(j + 1) * R], o[:, j, h, :], ident[0:R, 0:R])
                    last.then_inc(s_hnt_mm, 1)

                def down(a):
                    for k in range(KI):
                        pe.wait_ge(s_hst, KI * a.n + k + 1)
                        if k == 0:
                            pe.wait_ge(s_hmix, KI * a.n + KD)
                        for c in range(KD):
                            last = pe.matmul(ab[c][:, 0:GT], down_w[:, k, c * 128:(c + 1) * 128], hst[:, k, :],
                                             start=(k == 0), stop=(k == KI - 1))
                            if k == KI - 1:
                                last.then_inc(s_wd_mm, 1)

                def att_rows(a):
                    pe.wait_ge(s_att, KD * a.n + KD)
                    to_rows(ab[2:4], att_t, s_at_mm)

                def route(m):
                    pe.wait_ge(s_xn2l, KD * m.n + KD)
                    for j in range(NT):
                        n = 0
                        for part in (xn2_hi, xn2_lo):
                            for c in range(KD):
                                last = pe.matmul(mb[0][0:R, j * E:(j + 1) * E],
                                                 part[:, c, j * R:(j + 1) * R].bitcast(f32),
                                                 route_w[:, c], start=(n == 0), stop=(n == 2 * KD - 1))
                                n += 1
                    last.then_inc(s_rt_mm, 1)

                def gate_up(m, k):
                    if k == 0:
                        pe.wait_ge(s_lgt, m.n + 1)
                    else:
                        pe.wait_ge(s_sg, KI * m.n + k)
                    for u in range(2):
                        if u and k:
                            pe.wait_ge(s_act, KI * m.n + k)
                        at = u * I + k * 128
                        split_product(mb[u][:, 0:GT], (sgu_hi, sgu_lo), (xn2_hi, xn2_lo), at).then_inc(s_gu_mm, 1)

                def shared_down(m):
                    pe.wait_ge(s_act, KI * m.n + KI)
                    for c in range(KD):
                        for k in range(KI):
                            last = pe.matmul(mb[c][:, 0:GT], sd_w[:, k, c * 128:(c + 1) * 128], act_t[:, k, :],
                                             start=(k == 0), stop=(k == KI - 1))
                        last.then_inc(s_sd_mm, 1)

                def ffn_rows(m):
                    pe.wait_ge(s_ffn, KD * m.n + KD)
                    to_rows(mb, ffn_t, s_ft_mm)

                def step(e, f, a, m):
                    if f and isinstance(f.n, int) and f.n == 0:
                        merge_weights()
                    if a:
                        q_of(a)
                        gates_of(a, 0)
                    if f: h_rows_of(f)
                    if a:
                        gates_of(a, 1)
                        v_of(a, 0)
                        gates_of(a, 2)
                        v_of(a, 1)
                        gates_of(a, 3)
                        v_of(a, 2)
                        v_of(a, 3)
                    if f: to_columns(fb, xn, s_xn, f.n, s_xnt_mm)
                    if m: to_columns(mb, xn2, s_xn2, m.n, s_xn2t_mm, a)
                    if f: up(f, 0)
                    if a: f_sums(a)
                    if f:
                        up(f, 1)
                        up(f, 2)
                    if a: scores(a, 0)
                    if f: up(f, 3)
                    if a: scores(a, 1)
                    if m: route(m)
                    if a: scores(a, 2)
                    if m: gate_up(m, 0)
                    if a: scores(a, 3)
                    if m: gate_up(m, 1)
                    if f: up(f, 4)
                    if a:
                        cw_t_of(a, 0)
                        cw_t_of(a, 1)
                        heads(a, 0)
                        heads(a, 1)
                    if m: gate_up(m, 2)
                    if a:
                        cw_t_of(a, 2)
                        cw_t_of(a, 3)
                    if f: up(f, 5)
                    if a:
                        heads(a, 2)
                        heads(a, 3)
                    if m: gate_up(m, 3)
                    if f:
                        up(f, 6)
                        up(f, 7)
                    if m: shared_down(m)
                    if e: embed(e, 0)
                    if m: ffn_rows(m)
                    if a: heads_t(a)
                    if e: embed(e, 1)
                    if a:
                        down(a)
                        att_rows(a)

                pipeline(pe, step)


def experts_phase(nc, w_exp, xs_dram, base_dram, out, hot, banks):
    f32, i32, u32, bf16 = (mybir.dt.float32, mybir.dt.int32, mybir.dt.uint32, mybir.dt.bfloat16)
    f32r = mybir.dt.float32r
    ALU, ACT, AX = mybir.AluOpType, mybir.ActivationFunctionType, mybir.AxisListType
    HALF = TILES // 2
    PART = 8

    with ExitStack() as ctx:
        def sb(name, shape, dt=f32):
            return ctx.enter_context(nc.sbuf_tensor(name, shape, dt))

        def sem(name):
            return ctx.enter_context(nc.semaphore(name))

        ident2 = sb("ident2", [128, 128])
        before = sb("before", [R, R], bf16)
        ones_bf = sb("ones_bf", [R, R], bf16)
        ones_e = sb("ones_e", [R, E])
        restart = sb("restart", [R, E, TILES])
        levels = sb("levels", [R, LEVELS])
        iota_r = sb("iota_r", [R, SLOT], bf16)
        tile_no = sb("tile_no", [R, TILES], bf16)
        row_no = sb("row_no", [R, 1])
        total = sb("total", [R, E, TILES])
        upto = sb("upto", [R, E, TILES])
        above = sb("above", [R, E, LEVELS])
        n_slots = sb("n_slots", [R, E])
        end_slot = sb("end_slot", [R, E])
        start_slot = sb("start_slot", [R, E])
        start_row = sb("start_row", [R, E, TILES])
        ended = sb("ended", [R, E])
        slot_e = sb("slot_e", [R, 1])
        iota_p = sb("iota_p", [R, 1])
        USED = SLOTS + 3
        table = sb("table", [1, USED + 1], i32)
        place = sb("place", [R, TILES, E])
        pos_f = sb("pos_f", [R, TILES])
        pos_i = sb("pos_i", [R, TILES], i32)
        slot_i = sb("slot_i", [R, TILES], i32)
        row_i = sb("row_i", [R, TILES], i32)
        slot_f = sb("slot_f", [R, TILES], bf16)
        row_f = sb("row_f", [R, TILES], bf16)
        in_slot = sb("in_slot", [R, TILES, 2, SLOTS], bf16)
        in_row = sb("in_row", [R, TILES, SLOT], bf16)
        empty = sb("empty", [128, SLOTS])
        take_f = sb("take_f", [128, SLOTS])
        put_f = sb("put_f", [128, SLOTS])
        take = sb("take", [128, SLOTS + 8], u32)
        put = sb("put", [128, SLOTS + 8], u32)
        wts = sb("wts", [128, 4, 2 * KD * I])
        wts_down = sb("wts_down", [128, 4, KI * D])
        take_i = sb("take_i", [128, 4], u32)
        put_i = sb("put_i", [128, 4], u32)
        xg = sb("xg", [128, 4, D])
        bg = sb("bg", [128, 4, D])
        w_hi = sb("w_hi", [128, 2, 2, KD * I], f32r)
        w_lo = sb("w_lo", [128, 2, 2, KD * I], f32r)
        x_hi = sb("x_hi", [128, 2, KD * SLOT], f32r)
        x_lo = sb("x_lo", [128, 2, KD * SLOT], f32r)
        tanh_e = sb("tanh_e", [128, 2, I])
        silu_e = sb("silu_e", [128, 2, I])
        act_e = sb("act_e", [128, 2, I])
        act_et = sb("act_et", [128, 2, KI, SLOT])
        rows = sb("rows", [128, 4, D])
        iota_s = sb("iota_s", [R, SLOTS], bf16)

        s_passed2 = sem("s_passed2")
        s_const2 = sem("s_const2")
        s_rank_mm = sem("s_rank_mm")
        s_tot_mm = sem("s_tot_mm")
        s_seq = sem("s_seq")
        s_table = sem("s_table")
        s_slot_e = sem("s_slot_e")
        s_slot_mm = sem("s_slot_mm")
        s_in = sem("s_in")
        s_list_mm = sem("s_list_mm")
        s_list = sem("s_list")
        s_wts = [sem(f"s_wts{i}") for i in range(4)]
        s_wts_down = [sem(f"s_wts_down{i}") for i in range(4)]
        s_take = sem("s_take")
        s_put = sem("s_put")
        s_x_in = [sem(f"s_x_in{i}") for i in range(4)]
        s_base_in = [sem(f"s_base_in{i}") for i in range(4)]
        s_xgt_mm = sem("s_xgt_mm")
        s_xgt = sem("s_xgt")
        s_ge_mm = sem("s_ge_mm")
        s_te = sem("s_te")
        s_se = sem("s_se")
        s_ae = sem("s_ae")
        s_aet_mm = sem("s_aet_mm")
        s_aet = sem("s_aet")
        s_y_mm = sem("s_y_mm")
        s_y = sem("s_y")
        s_out = sem("s_out")
        s_stored = sem("s_stored")
        s_w_hi = sem("s_w_hi")
        s_w_lo = sem("s_w_lo")
        s_x_lo = sem("s_x_lo")
        s_pad = sem("s_pad")
        CREDIT = 4

        def wait_apart(eng, semaphore, value):
            eng.wait_ge(semaphore, value)
            if not isinstance(value, int):
                eng.sem_inc(s_passed2, 1)

        def slots_in_use(eng):
            eng.wait_ge(s_table, 2)
            return eng.value_load(table[0:1, USED:USED + 1], min_val=1, max_val=SLOTS)

        def slots(eng, front, turn, last):
            used = slots_in_use(eng)
            front(0, 0)
            turn(0, 0)
            turn(1, 1)
            with eng.If(used < 3):
                last(1, 1)
            with eng.Fori(0, SLOTS // 4) as t:
                with eng.If(used > 4 * t + 2):
                    turn(4 * t + 2, 2)
                    turn(4 * t + 3, 3)
                    with eng.If(used < 4 * t + 5):
                        last(4 * t + 3, 3)
                    with eng.If(used > 4 * t + 4):
                        turn(4 * t + 4, 0)
                        turn(4 * t + 5, 1)
                        with eng.If(used < 4 * t + 7):
                            last(4 * t + 5, 1)

        with nc.Block() as block:

            @block.sync
            def _(sp):
                used = slots_in_use(sp)

                def load(dst, k, i, cols, done):
                    e = sp.value_load(table[0:1, bass.ds(k, 1)], min_val=0, max_val=E - 1)
                    sp.dma_start(dst[:, i, :].rearrange("p (a n) -> p a n", a=1),
                                 w_exp[bass.ds(e, 1), :, cols].rearrange("e p n -> p e n")).then_inc(done[i], 16)

                def load_gate_up(k, i):
                    sp.wait_ge(s_w_lo, 2 * k + 2)
                    load(wts, k, i, slice(0, 2 * KD * I), s_wts)

                def load_down(k, i):
                    sp.wait_ge(s_y_mm, k + 1)
                    load(wts_down, k, i, slice(2 * KD * I, WCOLS), s_wts_down)

                for i in range(4):
                    load_gate_up(i, i)
                    if i < 2:
                        load_down(i, i)
                with sp.Fori(0, SLOTS // 4) as t:
                    for first in (4, 6):
                        with sp.If(used + 2 > 4 * t + first):
                            for i in (first, first + 1):
                                load_gate_up(4 * t + i, i % 4)
                                load_down(4 * t + i - 2, (i - 2) % 4)

            @block.gpsimd
            def _(pool):
                pool.memset(ones_bf[:], 1.0).then_inc(s_const2, 1)
                pool.memset(ident2[:], 0.0).then_inc(s_const2, 1)
                pool.memset(before[:], 1.0).then_inc(s_const2, 1)
                pool.wait_ge(s_const2, 3)
                pool.affine_select(out=before[:], in_=before[:], compare_op=ALU.is_ge, fill=0.0,
                                   base=-1, pattern=[[1, R]], channel_multiplier=-1).then_inc(s_const2, 1)
                pool.memset(restart[:], 1.0).then_inc(s_const2, 1)
                pool.wait_ge(s_const2, 5)
                pool.memset(restart[:, :, 0:1], 0.0).then_inc(s_const2, 1)
                pool.memset(ones_e[:], 1.0).then_inc(s_const2, 1)
                for dst, pattern, base, cm in [(levels, [[SLOT, LEVELS]], 0, 0), (iota_s, [[1, SLOTS]], 0, 0),
                                               (iota_r, [[1, SLOT]], 0, 0), (tile_no, [[1, TILES]], 0, 0),
                                               (row_no, [[1, 1]], 1, 1),
                                               (iota_p, [[1, 1]], 0, 1)]:
                    pool.iota(dst[:], pattern=pattern, base=base, channel_multiplier=cm,
                              allow_small_or_imprecise_dtypes=True).then_inc(s_const2, 1)
                pool.affine_select(out=ident2[:], in_=ident2[:], compare_op=ALU.not_equal, fill=1.0,
                                   base=0, pattern=[[-1, 128]], channel_multiplier=1).then_inc(s_const2, 1)
                pool.sem_inc(s_stored, CREDIT)

                pool.memset(take[:, SLOTS:], 0).then_inc(s_pad, 1)
                pool.wait_ge(s_list, 2)
                pool.wait_ge(s_pad, 1)

                def gather(rows_of, dst, i, done):
                    pool.indirect_dma_start(dst[:, i, :], None, rows_of,
                                            bass.IndirectOffsetOnAxis(ap=take_i[:, i:i + 1], axis=0)
                                            ).then_inc(done[i], 16)

                def gather_x(k, i):
                    pool.tensor_copy(take_i[:, i:i + 1], take[:, bass.ds(k, 1)]).then_inc(s_take, 1)
                    wait_apart(pool, s_take, k + 1)
                    gather(xs_dram, xg, i, s_x_in)

                def scatter(k, i):
                    pool.wait_ge(s_y, k + 3)
                    pool.tensor_copy(put_i[:, i:i + 1], put[:, bass.ds(k, 1)]).then_inc(s_put, 1)
                    wait_apart(pool, s_put, k + 1)
                    pool.indirect_dma_start(out, bass.IndirectOffsetOnAxis(ap=put_i[:, i:i + 1], axis=0),
                                            rows[:, i, :], None, bounds_check=T - 1,
                                            oob_is_err=False).then_inc(s_out, 16)

                def stored(k):
                    pool.wait_ge(s_out, 16 * k + 16)
                    pool.sem_inc(s_stored, 1)

                def front(k, i):
                    for ahead in range(4):
                        gather_x(k + ahead, i + ahead)
                        if ahead < 3:
                            gather(base_dram, bg, i + ahead, s_base_in)

                def turn(k, i):
                    pool.wait_ge(s_xgt_mm, k + 1)
                    pool.wait_ge(s_base_in[i], 4 * (k - i) + 16)
                    gather_x(k + 4, i)
                    if not (isinstance(k, int) and k < 2):
                        stored(k - 2)
                    if not (isinstance(k, int) and k == 0):
                        scatter(k - 1, (i + 3) % 4)
                    gather(base_dram, bg, (i + 3) % 4, s_base_in)

                def last(k, i):
                    stored(k - 1)
                    scatter(k, i)
                    stored(k)

                slots(pool, front, turn, last)

            @block.vector
            def _(dve):
                step = [0]

                def seq(op):
                    step[0] += 1
                    op.then_inc(s_seq, 1)
                    dve.wait_ge(s_seq, step[0])

                dve.sem_inc(s_y, 2)
                dve.sem_inc(s_w_lo, 2 * CREDIT)
                dve.wait_ge(s_tot_mm, 1)
                for i in range(2):
                    op = dve.tensor_copy(total[:, :, i * HALF:(i + 1) * HALF],
                                         banks[2 + i][0:R, :].rearrange("p (t e) -> p e t", e=E))
                    op.then_inc(s_seq, 1)
                step[0] = 2
                dve.wait_ge(s_seq, 2)
                dve.wait_ge(s_const2, 14)
                seq(dve.tensor_tensor_scan(upto[:].rearrange("p e t -> p (e t)"),
                                           restart[:].rearrange("p e t -> p (e t)"),
                                           total[:].rearrange("p e t -> p (e t)"), 0.0, ALU.mult, ALU.add))
                seq(dve.tensor_tensor(above[:], upto[:, :, TILES - 1:TILES].broadcast_to([R, E, LEVELS]),
                                      levels[:].unsqueeze(1).broadcast_to([R, E, LEVELS]), ALU.is_gt))
                seq(dve.tensor_reduce(n_slots[:], above[:], AX.X, ALU.add))
                seq(dve.tensor_tensor_scan(end_slot[:], ones_e[:], n_slots[:], 0.0, ALU.mult, ALU.add))
                seq(dve.tensor_scalar(ended[:], end_slot[:], iota_p[:, 0:1], None, ALU.is_le))
                seq(dve.tensor_reduce(slot_e[:], ended[:], AX.X, ALU.add))
                dve.tensor_scalar(slot_e[:], slot_e[:], float(E - 1), None, ALU.min).then_inc(s_slot_e, 1)
                seq(dve.tensor_tensor(start_slot[:], end_slot[:], n_slots[:], ALU.subtract))
                dve.wait_ge(s_slot_mm, 1)
                dve.tensor_copy(table[:, 0:SLOTS + 2], banks[5][0:1, 0:SLOTS + 2]).then_inc(s_table, 1)
                dve.tensor_copy(table[:, USED:USED + 1], end_slot[0:1, E - 1:E]).then_inc(s_table, 1)
                dve.wait_ge(s_table, 2)
                seq(dve.tensor_tensor(upto[:], upto[:], total[:], ALU.subtract))
                seq(dve.scalar_tensor_tensor(start_row[:], start_slot[:].unsqueeze(2).broadcast_to([R, E, TILES]),
                                             float(SLOT), upto[:], ALU.mult, ALU.add))
                dve.wait_ge(s_rank_mm, 1)
                for i in range(2):
                    half = slice(i * HALF, (i + 1) * HALF)
                    seq(dve.tensor_tensor(place[:, half, :], banks[i][0:R, :].rearrange("p (t e) -> p t e", e=E),
                                          start_row[:, :, half].rearrange("p e t -> p t e"), ALU.add))
                seq(dve.tensor_tensor(place[:], place[:], hot[:], ALU.mult))
                seq(dve.tensor_reduce(pos_f[:], place[:], AX.X, ALU.add))
                seq(dve.tensor_copy(pos_i[:], pos_f[:]))
                seq(dve.tensor_scalar(slot_i[:], pos_i[:], SLOT.bit_length() - 1, None, ALU.arith_shift_right))
                seq(dve.tensor_scalar(row_i[:], pos_i[:], SLOT - 1, None, ALU.bitwise_and))
                seq(dve.tensor_copy(slot_f[:], slot_i[:]))
                seq(dve.tensor_copy(row_f[:], row_i[:]))
                for t in range(0, TILES, PART):
                    part = slice(t, t + PART)
                    one = in_slot[:, part, 1, :]
                    seq(dve.tensor_tensor(one, iota_s[:].unsqueeze(1).broadcast_to([R, PART, SLOTS]),
                                          slot_f[:, part].unsqueeze(2).broadcast_to([R, PART, SLOTS]), ALU.is_equal))
                    seq(dve.tensor_tensor(in_slot[:, part, 0, :], one,
                                          tile_no[:, part].unsqueeze(2).broadcast_to([R, PART, SLOTS]), ALU.mult))
                    seq(dve.tensor_scalar(one, one, row_no[:, 0:1], None, ALU.mult))
                    dve.tensor_tensor(in_row[:, part, :], iota_r[:].unsqueeze(1).broadcast_to([R, PART, SLOT]),
                                      row_f[:, part].unsqueeze(2).broadcast_to([R, PART, SLOT]),
                                      ALU.is_equal).then_inc(s_in, 1)
                dve.wait_ge(s_list_mm, 1)
                rows1 = banks[4][:, SLOTS:2 * SLOTS]
                seq(dve.tensor_copy(take_f[:], rows1))
                seq(dve.scalar_tensor_tensor(take_f[:], banks[4][:, 0:SLOTS], float(R), take_f[:], ALU.mult, ALU.add))
                seq(dve.tensor_scalar(empty[:], rows1, 0.5, NOWHERE, ALU.is_lt, ALU.mult))
                seq(dve.tensor_scalar(take_f[:], take_f[:], -1.0, 0.0, ALU.add, ALU.max))
                seq(dve.tensor_tensor(put_f[:], take_f[:], empty[:], ALU.add))
                dve.tensor_copy(take[:, 0:SLOTS], take_f[:]).then_inc(s_list, 1)
                dve.tensor_copy(put[:, 0:SLOTS], put_f[:]).then_inc(s_list, 1)

                def rows_of(k, i):
                    dve.wait_ge(s_y_mm, k + 1 + CREDIT)
                    dve.wait_ge(s_stored, k + 1)
                    dve.wait_ge(s_base_in[i], 4 * (k - i) + 16)
                    dve.scalar_tensor_tensor(rows[:, i, :], banks[i % 2][:, 0:D], 0.5, bg[:, i, :],
                                             ALU.mult, ALU.add).then_inc(s_y, 1)

                def w_lo_of(k, i, u):
                    dve.wait_ge(s_w_hi, 2 * k + u + 1)
                    dve.tensor_tensor(w_lo[:, i % 2, u, :], wts[:, i, u * KD * I:(u + 1) * KD * I],
                                      w_hi[:, i % 2, u, :].bitcast(f32), ALU.subtract).then_inc(s_w_lo, 1)

                def x_lo_of(k, i):
                    e = i % 2
                    dve.wait_ge(s_xgt, k + 1)
                    dve.tensor_tensor(x_lo[:, e, :], banks[7][:, e * D:(e + 1) * D], x_hi[:, e, :].bitcast(f32),
                                      ALU.subtract).then_inc(s_x_lo, 1)

                def front(k, i):
                    w_lo_of(k, i, 0)
                    x_lo_of(k, i)
                    w_lo_of(k, i, 1)
                    w_lo_of(k + 1, i + 1, 0)

                def turn(k, i):
                    e = i % 2
                    dve.wait_ge(s_te, k + 1)
                    dve.scalar_tensor_tensor(silu_e[:, e, :], tanh_e[:, e, :], 1.0, banks[2 + 2 * e][:, :],
                                             ALU.add, ALU.mult).then_inc(s_se, 1)
                    dve.wait_ge(s_se, k + 1)
                    dve.wait_ge(s_ge_mm, 2 * k + 2)
                    dve.tensor_tensor(act_e[:, e, :], silu_e[:, e, :], banks[3 + 2 * e][:, :],
                                      ALU.mult).then_inc(s_ae, 1)
                    x_lo_of(k + 1, (i + 1) % 4)
                    if not (isinstance(k, int) and k == 0):
                        rows_of(k - 1, (i + 3) % 4)
                    w_lo_of(k + 1, (i + 1) % 4, 1)
                    w_lo_of(k + 2, (i + 2) % 4, 0)

                slots(dve, front, turn, rows_of)

            @block.scalar
            def _(act):
                def x_of(k, i):
                    e = i % 2
                    act.wait_ge(s_xgt_mm, k + 1)
                    act.activation(x_hi[:, e, :], banks[7][:, e * D:(e + 1) * D], ACT.Copy).then_inc(s_xgt, 1)

                def w_hi_of(k, i, u):
                    if u == 0:
                        act.wait_ge(s_wts[i], 4 * (k - i) + 16)
                    act.activation(w_hi[:, i % 2, u, :], wts[:, i, u * KD * I:(u + 1) * KD * I],
                                   ACT.Copy).then_inc(s_w_hi, 1)

                def act_of(k, i):
                    act.wait_ge(s_aet_mm, k + 1)
                    act.activation(act_et[:, i % 2].rearrange("p c n -> p (c n)"), banks[6][:, :],
                                   ACT.Copy).then_inc(s_aet, 1)

                def front(k, i):
                    w_hi_of(k, i, 0)
                    x_of(k, i)
                    w_hi_of(k, i, 1)
                    w_hi_of(k + 1, i + 1, 0)

                def turn(k, i):
                    e = i % 2
                    act.wait_ge(s_ge_mm, 2 * k + 1)
                    act.activation(tanh_e[:, e, :], banks[2 + 2 * e][:, :], ACT.Tanh, scale=0.5).then_inc(s_te, 1)
                    if not (isinstance(k, int) and k == 0):
                        act_of(k - 1, (i + 3) % 4)
                    x_of(k + 1, (i + 1) % 4)
                    w_hi_of(k + 1, (i + 1) % 4, 1)
                    w_hi_of(k + 2, (i + 2) % 4, 0)

                slots(act, front, turn, act_of)

            @block.tensor
            def _(pe):
                pe.sem_inc(s_y_mm, CREDIT)
                pe.wait_ge(s_const2, 1)
                for i in range(2):
                    last = pe.matmul(banks[2 + i][0:R, :], ones_bf[:], hot[:, i * HALF:(i + 1) * HALF, :],
                                     start=True, stop=True)
                last.then_inc(s_tot_mm, 1)
                pe.wait_ge(s_const2, 14)
                for i in range(2):
                    last = pe.matmul(banks[i][0:R, :], before[:], hot[:, i * HALF:(i + 1) * HALF, :],
                                     start=True, stop=True)
                last.then_inc(s_rank_mm, 1)
                pe.wait_ge(s_slot_e, 1)
                pe.matmul(banks[5][0:1, 0:R], slot_e[:, 0:1], ident2[0:R, 0:R], start=True,
                          stop=True).then_inc(s_slot_mm, 1)
                for t in range(TILES):
                    if t % PART == 0:
                        pe.wait_ge(s_in, t // PART + 1)
                    last = pe.matmul(banks[4][:, 0:2 * SLOTS], in_row[:, t, :],
                                     in_slot[:, t].rearrange("p d n -> p (d n)"),
                                     start=(t == 0), stop=(t == TILES - 1))
                last.then_inc(s_list_mm, 1)
                pe.wait_ge(s_list, 2)

                def x_of(k, i):
                    pe.wait_ge(s_x_in[i], 4 * (k - i) + 16)
                    for c in range(KD):
                        last = pe.transpose(banks[7][:, (i % 2) * D + c * 128:(i % 2) * D + (c + 1) * 128],
                                            xg[:, i, c * 128:(c + 1) * 128], ident2[:])
                    last.then_inc(s_xgt_mm, 1)

                def gate_up(k, i, u):
                    e = i % 2
                    pe.wait_ge(s_w_lo, 2 * (k + CREDIT) + u + 1)
                    n = 0
                    for x, w in ((x_hi, w_hi), (x_hi, w_lo), (x_lo, w_hi)):
                        for c in range(KD):
                            last = pe.matmul(banks[2 + 2 * e + u][:, :], x[:, e, c * SLOT:(c + 1) * SLOT],
                                             w[:, e, u, c * I:(c + 1) * I], start=(n == 0), stop=(n == 3 * KD - 1))
                            n += 1
                    last.then_inc(s_ge_mm, 1)

                def act_t_of(k, i):
                    pe.wait_ge(s_ae, k + 1)
                    for c in range(KI):
                        last = pe.transpose(banks[6][:, c * 128:(c + 1) * 128],
                                            act_e[:, i % 2, c * 128:(c + 1) * 128], ident2[:])
                    last.then_inc(s_aet_mm, 1)

                def down(k, i):
                    pe.wait_ge(s_wts_down[i], 4 * (k - i) + 16)
                    pe.wait_ge(s_aet, k + 1)
                    pe.wait_ge(s_y, k + 1)
                    for c in range(KI):
                        last = pe.matmul(banks[i % 2][:, 0:D], act_et[:, i % 2, c, :],
                                         wts_down[:, i, c * D:(c + 1) * D], start=(c == 0), stop=(c == KI - 1))
                    last.then_inc(s_y_mm, 1)

                def turn(k, i):
                    first = isinstance(k, int) and k == 0
                    pe.wait_ge(s_x_lo, k + 1)
                    gate_up(k, i, 0)
                    if not first:
                        act_t_of(k - 1, (i + 3) % 4)
                    gate_up(k, i, 1)
                    x_of(k + 1, (i + 1) % 4)
                    if not first:
                        down(k - 1, (i + 3) % 4)

                def last(k, i):
                    act_t_of(k, i)
                    down(k, i)

                slots(pe, x_of, turn, last)


def vit_tower(nc, patches, w_lin, pos, cols, w_up, conv, chan, wq, wk, wv, wvt, w_gates, b_gates,
              w_down, w_route, w_sgu, w_sd, w_exp, out):
    xs_dram = nc.dram_tensor("xs_rows_dram", (T, D), mybir.dt.float32).ap()
    base_dram = nc.dram_tensor("base_rows_dram", (T, D), mybir.dt.float32).ap()
    with ExitStack() as ctx:
        hot = ctx.enter_context(nc.sbuf_tensor("hot", [R, TILES, E], mybir.dt.bfloat16))
        banks = [ctx.enter_context(nc.psum_tensor(f"bank{i}", [128, 512], mybir.dt.float32)) for i in range(8)]
        groups_phase(nc, patches, w_lin, pos, cols, w_up, conv, chan, wq, wk, wv, wvt, w_gates, b_gates,
                     w_down, w_route, w_sgu, w_sd, xs_dram, base_dram, hot, banks)
        experts_phase(nc, w_exp, xs_dram, base_dram, out, hot, banks)


def _block_diagonal(w, transposed=False):
    d = np.zeros((KI, 128, 128), w.dtype)
    for c in range(KI):
        for i in range(128 // PD):
            d[c, PD * i:PD * i + PD, PD * i:PD * i + PD] = w[(128 // PD) * c + i]
    return d.transpose(2, 0, 1) if transposed else d.transpose(1, 0, 2)


def _chunks(w):
    return w.reshape(-1, 128, w.shape[-1]).transpose(1, 0, 2)


def kernel(**inputs):
    import concourse.bacc as bacc
    from concourse.bass_utils import run_bass_kernel_spmd

    a = {k: np.asarray(v) for k, v in inputs.items()}
    L = "L0_"
    x = a["x"].reshape(G, GS, C, HP, P, HP, P).transpose(0, 2, 4, 6, 1, 3, 5).reshape(G, KF, 128, GS * N)
    ig, fg = a[L + "attn_W_ig"], a[L + "attn_W_fg"]
    gates = np.concatenate([ig, fg], 1).reshape(3, KI, 128, 2 * NH)
    laid = {
        "patches": x.transpose(0, 2, 1, 3).reshape(G, 128, KF * GS * N),
        "w_lin": _chunks(a[L + "tok_W_lin"].T),
        "pos": _chunks(a[L + "tok_position_embeddings"][0].T),
        "cols": _chunks(np.stack([a[L + "tok_b_lin"], a[L + "tok_class_token"][0, 0], a["cls_tok"][0, 0]], 1)),
        "w_up": _chunks(a[L + "attn_W_up"]),
        "conv": _chunks(np.concatenate([a[L + "attn_conv_w"], a[L + "attn_conv_b"][None]], 0).T),
        "chan": _chunks(np.stack([a[L + "attn_norm_w"], a[L + "attn_skip"]], 1)),
        "wq": _block_diagonal(a[L + "attn_Wq"]),
        "wk": _block_diagonal(a[L + "attn_Wk"]),
        "wv": _block_diagonal(a[L + "attn_Wv"]),
        "wvt": _block_diagonal(a[L + "attn_Wv"], True),
        "w_gates": gates.transpose(2, 0, 1, 3),
        "b_gates": np.concatenate([a[L + "attn_b_ig"], a[L + "attn_b_fg"]])[None],
        "w_down": _chunks(a[L + "attn_W_down"]),
        "w_route": _chunks(a[L + "ffn_gate_w"]),
        "w_sgu": _chunks(np.concatenate([a[L + "ffn_shared_gate_w"], a[L + "ffn_shared_up_w"]], 1)),
        "w_sd": _chunks(a[L + "ffn_shared_down_w"]),
        "w_exp": np.concatenate(
            [a[L + "ffn_routed_gate_w"].reshape(E, KD, 128, I).transpose(0, 2, 1, 3).reshape(E, 128, KD * I),
             a[L + "ffn_routed_up_w"].reshape(E, KD, 128, I).transpose(0, 2, 1, 3).reshape(E, 128, KD * I),
             a[L + "ffn_routed_down_w"].reshape(E, KI, 128, D).transpose(0, 2, 1, 3).reshape(E, 128, KI * D)], 2),
    }
    laid = {k: np.ascontiguousarray(v) for k, v in laid.items()}
    nc = bacc.Bacc("TRN2", target_bir_lowering=False, num_devices=1)
    args = [nc.dram_tensor(k, v.shape, mybir.dt.from_np(v.dtype), kind="ExternalInput").ap()
            for k, v in laid.items()]
    out = nc.dram_tensor("out", (T, D), mybir.dt.float32, kind="ExternalOutput").ap()
    vit_tower(nc, *args, out)
    r = run_bass_kernel_spmd(nc, [laid], core_ids=[0])
    return r.results[0]["out"].reshape(B, S, D)
```

```python
from contextlib import ExitStack
from collections import namedtuple

import numpy as np
import concourse.bass as bass
from concourse import mybir

B, C, HW, P = 64, 3, 96, 16
HP = HW // P
N = HP * HP
S = N + 2
F = C * P * P
D = 256
INNER, NH, PH, PD = 512, 4, 128, 4
TAPS = 4
I = 512
E = 32
T = B * S

GS = 8
G = B // GS
GT = GS * S
TS = 2
R = TS * S
NT = GS // TS
TILES = B // TS
HALF = TILES // 2
KF, KD, KI = F // 128, D // 128, INNER // 128
SLOT = 128
SLOTS = (T + E * (SLOT - 1)) // SLOT
SLOTS += -SLOTS % 4
USED = SLOTS + 3
LEVELS = T // SLOT
WCOLS = 2 * KD * I + KI * D
MASKED = -1.0e30
NOWHERE = 1.0e6

Group = namedtuple("Group", "n p")


def groups_phase(nc, patches, w_lin, pos, cols, w_up, conv, chan, wq, wk, wv, wvt, w_gates, b_gates,
                 w_down, w_route, w_sgu, w_sd, xs_dram, base_dram, hot, banks, sort, w_exp):
    f32, bf16, u32, f32r = mybir.dt.float32, mybir.dt.bfloat16, mybir.dt.uint32, mybir.dt.float32r
    ALU, ACT, AX = mybir.AluOpType, mybir.ActivationFunctionType, mybir.AxisListType
    fb, ab, mb = banks[0:2], banks[2:6], banks[6:8]

    with ExitStack() as ctx:
        def sb(name, shape, dt=f32):
            return ctx.enter_context(nc.sbuf_tensor(name, shape, dt))

        def sem(name):
            return ctx.enter_context(nc.semaphore(name))

        ident = sort.ident
        ones = sb("ones", [128, 128])
        tri = sb("tri", [R, R])
        mask = sb("mask", [R, R])
        mask_bf = sb("mask_bf", [R, R], bf16)
        ident_bf = sb("ident_bf", [R, R], bf16)
        iota_e = sb("iota_e", [R, E])
        minus_half = sb("minus_half", [R, NH])
        lin_w = sort.lin_w
        up_hi = sb("up_hi", [128, KD, 2 * INNER], f32r)
        up_lo = sb("up_lo", [128, KD, 2 * INNER], f32r)
        down_w = sort.down_w
        sgu_hi = sb("sgu_hi", [128, KD, 2 * I], f32r)
        sgu_lo = sb("sgu_lo", [128, KD, 2 * I], f32r)
        sd_w = sb("sd_w", [128, KI, D])
        route_w = sb("route_w", [128, KD, E])
        pos_t = sb("pos_t", [128, KD, N + 1])
        col_t = sb("col_t", [128, KD, 3])
        posb = sb("posb", [128, KD, N])
        conv_t = sb("conv_t", [128, KI, TAPS + 1])
        chan_t = sb("chan_t", [128, KI, 2])
        gates_b = sb("gates_b", [R, 2 * NH])
        score_w = sb("score_w", [128, KI, 128])
        v_w = sb("v_w", [128, KI, 128])
        gx_w = sb("gx_w", [128, KI, 2 * NH])
        gm_w = sb("gm_w", [128, KI, 2 * NH])

        patch = sb("patch", [128, KF, GS * N])
        h_t = sb("h_t", [128, KD, GS, S])
        h_rows = sb("h_rows", [R, 2, NT, D])
        stats1 = sb("stats1", [R, NT, 6])
        mv1 = sb("mv1", [R, NT, 2])
        rstd1 = sb("rstd1", [R, NT])
        xn = sb("xn", [R, NT, D])
        xn_hi = sb("xn_hi", [128, KD, GT], f32r)
        xn_lo = sb("xn_lo", [128, KD, GT], f32r)
        xm = sb("xm", [128, 2, KI, GS, S])
        tanh_z = sb("tanh_z", [128, KI, GT])
        silu_z = sort.silu_z
        y = sb("y", [128, KI, GS, S])
        tanh_y = sb("tanh_y", [128, KI, GT])
        x_act = sort.x_act
        q_t = sb("q_t", [128, KI, GT])
        v = sb("v", [R, NT, INNER])
        gl = sb("gl", [R, NT, 2 * NH])
        fabs = sb("fabs", [R, NT, NH])
        fexp = sb("fexp", [R, NT, NH])
        fln = sb("fln", [R, NT, NH])
        logf = sb("logf", [R, NT, NH])
        fsum = sb("fsum", [R, NT, NH])
        a_gate = sb("a_gate", [R, NT, NH])
        diag = sb("diag", [R, NT, NH, R])
        cw = sb("cw", [R, NT, NH, R])
        minus_max = sb("minus_max", [R, NT, NH])
        row_sum = sb("row_sum", [R, NT, NH])
        m_d = sb("m_d", [R, NT, NH])
        exp_md = sb("exp_md", [R, NT, NH])
        norm = sb("norm", [R, NT, NH])
        norm2 = sb("norm2", [R, NT, NH])
        cw_t = sb("cw_t", [R, NT, NH * R])
        o = sb("o", [R, NT, NH, 128])
        stats_h = sb("stats_h", [R, NT, NH, 6])
        mv_h = sb("mv_h", [R, NT, NH, 2])
        var_h = sb("var_h", [R, NT, NH])
        rstd_h = sb("rstd_h", [R, NT, NH])
        shift_h = sb("shift_h", [R, NT, NH])
        hst = sb("hst", [128, KI, GT])
        att_t = sb("att_t", [128, KD, GT])
        h2 = sb("h2", [R, 2, NT, D])
        stats2 = sb("stats2", [R, NT, 6])
        mv2 = sb("mv2", [R, NT, 2])
        rstd2 = sb("rstd2", [R, NT])
        xn2 = sb("xn2", [R, NT, D])
        xn2_hi = sb("xn2_hi", [128, KD, GT], f32r)
        xn2_lo = sb("xn2_lo", [128, KD, GT], f32r)
        logits = sb("logits", [R, NT, E])
        top = sb("top", [R, NT, 8])
        top_i = sb("top_i", [R, NT, 8], u32)
        top_f = sb("top_f", [R, NT])
        tanh_s = sb("tanh_s", [R, NT])
        score = sb("score", [R, NT])
        xs_rows = sb("xs_rows", [R, NT, D])
        tanh_g = sb("tanh_g", [128, 2, GT])
        silu_g = sb("silu_g", [128, 2, GT])
        act_t = sb("act_t", [128, KI, GT])
        ffn_t = sb("ffn_t", [128, KD, GT])
        base_rows = sb("base_rows", [R, NT, D])
        def within(buffer, pattern, at, shape):
            flat = buffer[:].rearrange(pattern)
            names = "abc"[:len(shape)]
            sizes = {c: n for c, n in zip(names[:-1], shape[:-1])}
            size = int(np.prod(shape))
            return flat[:, at:at + size].rearrange(f"p ({' '.join(names)}) -> p {' '.join(names)}", **sizes)

        up_raw = within(xm, "p a k s t -> p (a k s t)", 0, [KD, 2 * INNER])
        sgu_raw = within(silu_z, "p a k n -> p (a k n)", 0, [KD, 2 * I])
        q_raw = within(tanh_y, "p k n -> p (k n)", 0, [KI, 128])
        k_raw = within(tanh_y, "p k n -> p (k n)", KI * 128, [KI, 128])
        v_raw = within(tanh_z, "p k n -> p (k n)", 0, [KI, 128])
        g_raw = within(tanh_z, "p k n -> p (k n)", KI * 128, [3, KI, 2 * NH])

        s_w_emb = sem("s_w_emb")
        s_w_front = sem("s_w_front")
        s_w_att = sem("s_w_att")
        s_w_ffn = sem("s_w_ffn")
        s_passed = sem("s_passed")
        s_const = sem("s_const")
        s_prep_mm = sem("s_prep_mm")
        s_prep = sem("s_prep")
        s_patch = sem("s_patch")
        s_emb_mm = sem("s_emb_mm")
        s_ht = sem("s_ht")
        s_h_mm = sem("s_h_mm")
        s_hrows = sem("s_hrows")
        s_st1 = sem("s_st1")
        s_mv1 = sem("s_mv1")
        s_ve1 = sem("s_ve1")
        s_rstd1 = sem("s_rstd1")
        s_xn = sem("s_xn")
        s_xnt_mm = sem("s_xnt_mm")
        s_xnt = sem("s_xnt")
        s_xnl = sem("s_xnl")
        s_split = sem("s_split")
        s_up_mm = sem("s_up_mm")
        s_xm = sem("s_xm")
        s_tz = sem("s_tz")
        s_sz = sem("s_sz")
        s_conv = sem("s_conv")
        s_ty = sem("s_ty")
        s_tyy = sem("s_tyy")
        s_xact = sem("s_xact")
        s_q_mm = sem("s_q_mm")
        s_q = sem("s_q")
        s_v_mm = sem("s_v_mm")
        s_v = sem("s_v")
        s_g_mm = sem("s_g_mm")
        s_gl = sem("s_gl")
        s_fabs = sem("s_fabs")
        s_fexp = sem("s_fexp")
        s_fln = sem("s_fln")
        s_logf = sem("s_logf")
        s_f_mm = sem("s_f_mm")
        s_fsum = sem("s_fsum")
        s_a = sem("s_a")
        s_diag = sem("s_diag")
        s_b_mm = sem("s_b_mm")
        s_c_mm = sem("s_c_mm")
        s_max = sem("s_max")
        s_dmat = sem("s_dmat")
        s_cw = sem("s_cw")
        s_sum = sem("s_sum")
        s_md = sem("s_md")
        s_expmd = sem("s_expmd")
        s_norm = sem("s_norm")
        s_ct_mm = sem("s_ct_mm")
        s_ct = sem("s_ct")
        s_pv_mm = sem("s_pv_mm")
        s_o = sem("s_o")
        s_sth = sem("s_sth")
        s_mvh = sem("s_mvh")
        s_varh = sem("s_varh")
        s_rstdh = sem("s_rstdh")
        s_shift = sem("s_shift")
        s_hn = sem("s_hn")
        s_hn_act = sem("s_hn_act")
        s_skip = sem("s_skip")
        s_hnt_mm = sem("s_hnt_mm")
        s_hmix = sem("s_hmix")
        s_hst = sem("s_hst")
        s_wd_mm = sem("s_wd_mm")
        s_att = sem("s_att")
        s_at_mm = sem("s_at_mm")
        s_h2 = sem("s_h2")
        s_st2 = sem("s_st2")
        s_mv2 = sem("s_mv2")
        s_ve2 = sem("s_ve2")
        s_rstd2 = sem("s_rstd2")
        s_xn2 = sem("s_xn2")
        s_xn2t_mm = sem("s_xn2t_mm")
        s_xn2t = sem("s_xn2t")
        s_xn2l = sem("s_xn2l")
        s_rt_mm = sem("s_rt_mm")
        s_lgt = sem("s_lgt")
        s_top = sem("s_top")
        s_topi = sem("s_topi")
        s_topf = sem("s_topf")
        s_hot = sem("s_hot")
        s_ts = sem("s_ts")
        s_score = sem("s_score")
        s_xs = sem("s_xs")
        s_xs_out = sort.s_xs_out
        s_gu_mm = sem("s_gu_mm")
        s_tg = sem("s_tg")
        s_sg = sem("s_sg")
        s_act = sem("s_act")
        s_sd_mm = sem("s_sd_mm")
        s_ffn = sem("s_ffn")
        s_ft_mm = sem("s_ft_mm")
        s_base = sem("s_base")
        s_base_out = sort.s_base_out

        sort.borrow(ones, diag, cw, cw_t[:].rearrange("p j (h t) -> p j h t", h=NH),
                    v[:].rearrange("p j (h c) -> p j h c", h=NH), o,
                    xm[:, 0])

        CONV = KI * (TAPS - 1)

        def wait(eng, semaphore, value):
            if not isinstance(value, int) or value > 0:
                eng.wait_ge(semaphore, value)

        def wait_apart(eng, semaphore, value):
            eng.wait_ge(semaphore, value)
            if not isinstance(value, int):
                eng.sem_inc(s_passed, 1)

        def pipeline(eng, step):
            step(Group(0, 0), None, None, None)
            step(Group(1, 1), Group(0, 0), None, None)
            step(Group(2, 0), Group(1, 1), Group(0, 0), None)
            with eng.Fori(0, (G - 4) // 2) as j:
                step(Group(2 * j + 3, 1), Group(2 * j + 2, 0), Group(2 * j + 1, 1), Group(2 * j, 0))
                step(Group(2 * j + 4, 0), Group(2 * j + 3, 1), Group(2 * j + 2, 0), Group(2 * j + 1, 1))
            step(Group(G - 1, 1), Group(G - 2, 0), Group(G - 3, 1), Group(G - 4, 0))
            step(None, Group(G - 1, 1), Group(G - 2, 0), Group(G - 3, 1))
            step(None, None, Group(G - 1, 1), Group(G - 2, 0))
            step(None, None, None, Group(G - 1, 1))

        def final(e, f, a):
            return not (e or f or a)

        with nc.Block() as block:

            @block.sync
            def _(sp):
                sp.dma_start(lin_w[:], w_lin).then_inc(s_w_emb, 16)

                def load_patches(f):
                    wait(sp, s_emb_mm, KD * f.n)
                    src = patches[bass.ds(f.n, 1)].rearrange("g p (k n) -> p (g k) n", k=KF)
                    sp.dma_start(patch[:], src).then_inc(s_patch, 16)

                load_patches(Group(0, 0))
                for dst, src in [(pos_t, pos), (col_t, cols)]:
                    sp.dma_start(dst[:], src).then_inc(s_w_emb, 16)
                for dst, src in [(up_raw, w_up), (conv_t[:], conv), (chan_t[:], chan)]:
                    sp.dma_start(dst, src).then_inc(s_w_front, 16)

                def step(e, f, a, m):
                    if final(e, f, a): sort.first_loads(sp, w_exp)
                    if m is not None:
                        sp.wait_ge(s_xs, NT * m.n + NT)
                        dst = xs_dram[bass.ds(m.n * GT, GT), :].rearrange("(j p) d -> p j d", p=R)
                        sp.dma_start(dst, xs_rows[:]).then_inc(s_xs_out, 16)
                        sp.wait_ge(s_base, 2 * m.n + 2)
                        dst = base_dram[bass.ds(m.n * GT, GT), :].rearrange("(j p) d -> p j d", p=R)
                        sp.dma_start(dst, base_rows[:]).then_inc(s_base_out, 16)
                    if e is not None and not (isinstance(e.n, int) and e.n == G - 1):
                        load_patches(Group(e.n + 1, 1 - e.p))

                pipeline(sp, step)

            @block.gpsimd
            def _(pool):
                pool.sem_inc(s_xs_out, 16)
                pool.sem_inc(s_base_out, 16)
                pool.memset(ident[:], 0.0).then_inc(s_const, 1)
                pool.memset(tri[:], 1.0).then_inc(s_const, 1)
                pool.memset(mask[:], 0.0).then_inc(s_const, 1)
                pool.memset(ones[:], 1.0).then_inc(s_const, 1)
                pool.memset(minus_half[:], -0.5).then_inc(s_const, 1)
                pool.iota(iota_e[:], pattern=[[1, E]], base=0, channel_multiplier=0,
                          allow_small_or_imprecise_dtypes=True).then_inc(s_const, 1)
                pool.wait_ge(s_const, 6)
                pool.affine_select(out=ident[:], in_=ident[:], compare_op=ALU.not_equal, fill=1.0,
                                   base=0, pattern=[[-1, 128]], channel_multiplier=1).then_inc(s_const, 1)
                pool.affine_select(out=tri[:], in_=tri[:], compare_op=ALU.is_ge, fill=0.0,
                                   base=0, pattern=[[1, R]], channel_multiplier=-1).then_inc(s_const, 1)
                pool.affine_select(out=mask[:], in_=mask[:], compare_op=ALU.is_ge, fill=MASKED,
                                   base=0, pattern=[[-1, R]], channel_multiplier=1).then_inc(s_const, 1)
                pool.wait_ge(s_const, 9)
                pool.affine_select(out=tri[:, S:R], in_=tri[:, S:R], compare_op=ALU.is_ge, fill=0.0,
                                   base=-S, pattern=[[0, S]], channel_multiplier=1).then_inc(s_const, 1)
                pool.affine_select(out=mask[:, 0:S], in_=mask[:, 0:S], compare_op=ALU.is_ge, fill=MASKED,
                                   base=S - 1, pattern=[[0, S]], channel_multiplier=-1).then_inc(s_const, 1)
                pool.wait_ge(s_const, 11)
                pool.tensor_copy(mask_bf[:], mask[:]).then_inc(s_const, 1)
                pool.tensor_copy(ident_bf[:], ident[0:R, 0:R]).then_inc(s_const, 1)

                def rstd1_of(f):
                    wait_apart(pool, s_mv1, NT * f.n + NT)
                    pool.tensor_scalar(rstd1[:], mv1[:, :, 1], 1e-5, None, ALU.add).then_inc(s_ve1, 1)
                    pool.wait_ge(s_ve1, f.n + 1)
                    pool.tensor_tensor(rstd1[:], rstd1[:], minus_half[:], ALU.pow).then_inc(s_rstd1, 1)

                def rstd2_of(m):
                    wait_apart(pool, s_mv2, NT * m.n + NT)
                    pool.tensor_scalar(rstd2[:], mv2[:, :, 1], 1e-5, None, ALU.add).then_inc(s_ve2, 1)
                    pool.wait_ge(s_ve2, m.n + 1)
                    pool.tensor_tensor(rstd2[:], rstd2[:], minus_half[:], ALU.pow).then_inc(s_rstd2, 1)

                def skip_of(a):
                    wait(pool, s_wd_mm, KD * a.n)
                    wait_apart(pool, s_xact, KI * a.n + KI)
                    for h in range(NH):
                        pool.tensor_scalar(hst[:, h, :], x_act[:, a.p, h, :], chan_t[:, h, 1:2], None,
                                           ALU.mult).then_inc(s_skip, 1)

                def x_act_of(f, pair):
                    for k in (2 * pair, 2 * pair + 1):
                        pool.wait_ge(s_ty, KI * f.n + k + 1)
                        half = y[:, k].rearrange("p s t -> p (s t)")
                        pool.tensor_tensor(tanh_y[:, k, :], tanh_y[:, k, :], half, ALU.mult).then_inc(s_tyy, 1)
                        pool.wait_ge(s_tyy, KI * f.n + k + 1)
                        pool.tensor_tensor(x_act[:, f.p, k, :], tanh_y[:, k, :], half, ALU.add).then_inc(s_xact, 1)

                def rstd_h_of(a, j):
                    pool.wait_ge(s_varh, NT * a.n + j + 1)
                    pool.tensor_tensor(rstd_h[:, j, :], var_h[:, j, :], minus_half[:],
                                       ALU.pow).then_inc(s_rstdh, 1)

                def step(e, f, a, m):
                    if m: rstd2_of(m)
                    if final(e, f, a): sort.constants(pool)
                    if f: rstd1_of(f)
                    if a: skip_of(a)
                    if f: x_act_of(f, 0)
                    if a:
                        rstd_h_of(a, 0)
                        rstd_h_of(a, 1)
                        rstd_h_of(a, 2)
                        rstd_h_of(a, 3)
                    if f: x_act_of(f, 1)

                pipeline(pool, step)

            @block.scalar
            def _(act):
                bias = b_gates.partition_broadcast(R)
                act.wait_ge(s_w_emb, 3 * 16)
                for dst, src in [(q_raw, wq), (k_raw, wk), (v_raw, wv), (v_w[:], wvt), (g_raw, w_gates),
                                 (gates_b[:], bias)]:
                    act.dma_start(dst, src).then_inc(s_w_att, 16)
                for dst, src in [(down_w[:], w_down), (route_w[:], w_route), (sgu_raw, w_sgu), (sd_w[:], w_sd)]:
                    act.dma_start(dst, src).then_inc(s_w_ffn, 16)

                def copy(dst, src):
                    return act.activation(dst, src, ACT.Copy)

                def split_weights():
                    act.wait_ge(s_prep, 8)
                    copy(up_hi[:], up_raw).then_inc(s_split, 1)
                    act.wait_ge(s_prep, 9)
                    copy(sgu_hi[:], sgu_raw).then_inc(s_split, 1)
                    act.wait_ge(s_prep_mm, 2)

                def h_rows_of(f):
                    for b in range(2):
                        act.wait_ge(s_h_mm, 2 * f.n + b + 1)
                        copy(h_rows[:, f.p, 2 * b:2 * b + 2, :].rearrange("p j d -> p (j d)"),
                             fb[b][0:R, :]).then_inc(s_hrows, 1)

                def xn_t_of(f):
                    for c in range(KD):
                        act.wait_ge(s_xnt_mm, KD * f.n + c + 1)
                        copy(xn_hi[:, c, :], fb[c][:, 0:GT]).then_inc(s_xnt, 1)

                def xm_of(f, k):
                    act.wait_ge(s_up_mm, 2 * KI * f.n + k + 1)
                    if k == 0:
                        wait(act, s_xact, KI * f.n)
                    act.activation(y[:, k].rearrange("p s t -> p (s t)"), fb[k % 2][:, 0:GT], ACT.Identity,
                                   bias=conv_t[:, k, TAPS:TAPS + 1], scale=conv_t[:, k, TAPS - 1:TAPS])
                    copy(xm[:, f.p, k].rearrange("p s t -> p (s t)"), fb[k % 2][:, 0:GT]).then_inc(s_xm, 1)

                def tanh_z_of(f, k):
                    act.wait_ge(s_up_mm, 2 * KI * f.n + KI + k + 1)
                    act.activation(tanh_z[:, k, :], fb[k % 2][:, 0:GT], ACT.Tanh).then_inc(s_tz, 1)

                def tanh_y_of(f, pair):
                    act.wait_ge(s_conv, CONV * f.n + CONV // 2 * (pair + 1))
                    for k in (2 * pair, 2 * pair + 1):
                        act.activation(tanh_y[:, k, :], y[:, k].rearrange("p s t -> p (s t)"),
                                       ACT.Tanh).then_inc(s_ty, 1)

                def q_of(a):
                    for h in range(NH):
                        act.wait_ge(s_q_mm, NH * a.n + h + 1)
                        act.activation(q_t[:, h, :], ab[h][:, 0:GT], ACT.Copy,
                                       scale=float(INNER // NH) ** -0.5).then_inc(s_q, 1)

                def v_of(a, j):
                    act.wait_ge(s_v_mm, NT * a.n + j + 1)
                    copy(v[:, j, :], ab[j][0:R, :]).then_inc(s_v, 1)

                def log_f(a):
                    act.wait_ge(s_fabs, a.n + 1)
                    act.activation(fexp[:], fabs[:], ACT.Exp, scale=-1.0).then_inc(s_fexp, 1)
                    act.wait_ge(s_fexp, a.n + 1)
                    act.activation(fln[:], fexp[:], ACT.Ln, bias=1.0).then_inc(s_fln, 1)

                def decay(a, j):
                    act.wait_ge(s_max, NT * a.n + j + 1)
                    for h in range(NH):
                        act.activation(cw[:, j, h, :], ab[2 * (j % 2)][0:R, h * R:(h + 1) * R], ACT.Exp,
                                       bias=minus_max[:, j, h:h + 1]).then_inc(s_dmat, 1)

                def exp_m_d(a):
                    act.wait_ge(s_md, a.n + 1)
                    act.activation(exp_md[:], m_d[:], ACT.Exp).then_inc(s_expmd, 1)

                def cw_t_of(a, j):
                    act.wait_ge(s_ct_mm, NT * a.n + j + 1)
                    copy(cw_t[:, j, :], ab[j][0:R, 0:GT]).then_inc(s_ct, 1)

                def o_of(a, j):
                    act.wait_ge(s_pv_mm, NT * a.n + j + 1)
                    copy(o[:, j].rearrange("p h d -> p (h d)"), ab[j][0:R, :]).then_inc(s_o, 1)

                def head_norm(a, j):
                    act.wait_ge(s_shift, 2 * a.n + j + 1)
                    for h in range(NH):
                        act.activation(o[:, j, h, :], o[:, j, h, :], ACT.Identity, bias=shift_h[:, j, h:h + 1],
                                       scale=rstd_h[:, j, h:h + 1]).then_inc(s_hn_act, 1)

                def att_t_of(a):
                    for c in range(KD):
                        act.wait_ge(s_wd_mm, KD * a.n + c + 1)
                        copy(att_t[:, c, :], ab[c][:, 0:GT]).then_inc(s_att, 1)

                def xn2_t_of(m):
                    for c in range(KD):
                        act.wait_ge(s_xn2t_mm, KD * m.n + c + 1)
                        copy(xn2_hi[:, c, :], mb[c][:, 0:GT]).then_inc(s_xn2t, 1)

                def tanh_score(m):
                    act.wait_ge(s_top, NT * m.n + NT)
                    act.activation(tanh_s[:], top[:, :, 0], ACT.Tanh, scale=0.5).then_inc(s_ts, 1)

                def score_rows(m):
                    act.wait_ge(s_score, m.n + 1)
                    act.wait_ge(s_xs_out, 16 * m.n + 16)
                    for j in range(NT):
                        act.activation(xs_rows[:, j, :], xn2[:, j, :], ACT.Copy,
                                       scale=score[:, j:j + 1]).then_inc(s_xs, 1)

                def tanh_g_of(m, k):
                    act.wait_ge(s_gu_mm, 2 * KI * m.n + 2 * k + 1)
                    act.activation(tanh_g[:, k % 2, :], mb[0][:, 0:GT], ACT.Tanh).then_inc(s_tg, 1)

                def ffn_t_of(m):
                    for c in range(KD):
                        act.wait_ge(s_sd_mm, KD * m.n + c + 1)
                        copy(ffn_t[:, c, :], mb[c][:, 0:GT]).then_inc(s_ffn, 1)

                def step(e, f, a, m):
                    if f and isinstance(f.n, int) and f.n == 0:
                        split_weights()
                    if a: q_of(a)
                    if f: h_rows_of(f)
                    if a:
                        v_of(a, 0)
                        v_of(a, 1)
                        log_f(a)
                        v_of(a, 2)
                        v_of(a, 3)
                    if f: xn_t_of(f)
                    if m: xn2_t_of(m)
                    if f:
                        xm_of(f, 0)
                        xm_of(f, 1)
                        xm_of(f, 2)
                    if a:
                        decay(a, 0)
                        decay(a, 1)
                    if f: xm_of(f, 3)
                    if a: decay(a, 2)
                    if m:
                        tanh_score(m)
                        tanh_g_of(m, 0)
                    if a: decay(a, 3)
                    if m: tanh_g_of(m, 1)
                    if a:
                        exp_m_d(a)
                        cw_t_of(a, 0)
                        cw_t_of(a, 1)
                    if f:
                        tanh_y_of(f, 0)
                        tanh_z_of(f, 0)
                    if a:
                        o_of(a, 0)
                        o_of(a, 1)
                    if m: tanh_g_of(m, 2)
                    if a:
                        cw_t_of(a, 2)
                        cw_t_of(a, 3)
                    if f:
                        tanh_y_of(f, 1)
                        tanh_z_of(f, 1)
                    if a:
                        o_of(a, 2)
                        o_of(a, 3)
                    if m: tanh_g_of(m, 3)
                    if a: head_norm(a, 0)
                    if f: tanh_z_of(f, 2)
                    if a: head_norm(a, 1)
                    if f: tanh_z_of(f, 3)
                    if m:
                        ffn_t_of(m)
                        score_rows(m)
                    if a: att_t_of(a)

                pipeline(act, step)

            @block.vector
            def _(dve):
                dve.wait_ge(s_w_emb, 3 * 16)
                for c in range(KD):
                    dve.tensor_scalar(posb[:, c, :], pos_t[:, c, 1:], col_t[:, c, 0:1], None,
                                      ALU.add).then_inc(s_prep, 1)
                    dve.tensor_copy(h_t[:, c, :, 0], col_t[:, c, 2:3].broadcast_to([128, GS])).then_inc(s_prep, 1)
                    dve.tensor_scalar(h_t[:, c, :, 1], pos_t[:, c, 0:1].broadcast_to([128, GS]),
                                      col_t[:, c, 1:2], None, ALU.add).then_inc(s_prep, 1)
                dve.wait_ge(s_prep, 6)

                def halve_front():
                    dve.wait_ge(s_w_front, 3 * 16)
                    dve.tensor_scalar(conv_t[:], conv_t[:], 0.5, None, ALU.mult).then_inc(s_prep, 1)
                    dve.tensor_scalar(up_raw[:, :, INNER:], up_raw[:, :, INNER:], 0.5, None, ALU.mult).then_inc(s_prep, 1)
                    dve.wait_ge(s_w_ffn, 4 * 16)
                    dve.tensor_scalar(sgu_raw[:, :, 0:I], sgu_raw[:, :, 0:I], 0.5, None, ALU.mult).then_inc(s_prep, 1)
                    dve.wait_ge(s_split, 1)
                    dve.tensor_tensor(up_lo[:], up_raw, up_hi[:].bitcast(f32), ALU.subtract).then_inc(s_prep, 1)
                    dve.wait_ge(s_split, 2)
                    dve.tensor_tensor(sgu_lo[:], sgu_raw, sgu_hi[:].bitcast(f32), ALU.subtract).then_inc(s_prep, 1)

                def merge_weights():
                    dve.wait_ge(s_prep_mm, 1)
                    dve.tensor_copy(score_w[:].rearrange("p h d -> p (h d)"), ab[0][:, :]).then_inc(s_prep, 1)
                    dve.wait_ge(s_prep_mm, 2)
                    dve.tensor_copy(gx_w[:].rearrange("p h g -> p (h g)"), ab[1][:, 0:32]).then_inc(s_prep, 1)
                    dve.tensor_copy(gm_w[:].rearrange("p h g -> p (h g)"), ab[1][:, 32:64]).then_inc(s_prep, 1)

                def embed(f):
                    for c in range(KD):
                        dve.wait_ge(s_emb_mm, KD * f.n + c + 1)
                        dve.tensor_tensor(h_t[:, c, :, 2:],
                                          fb[c][:, 0:GS * N].rearrange("p (s n) -> p s n", n=N),
                                          posb[:, c].unsqueeze(1).broadcast_to([128, GS, N]),
                                          ALU.add).then_inc(s_ht, 1)

                def ln1_stats(f):
                    for j in range(NT):
                        if j % 2 == 0:
                            dve.wait_ge(s_hrows, 2 * f.n + j // 2 + 1)
                        dve.bn_stats(stats1[:, j, :], h_rows[:, f.p, j, :]).then_inc(s_st1, 1)
                    for j in range(NT):
                        wait_apart(dve, s_st1, NT * f.n + j + 1)
                        dve.bn_aggr(mv1[:, j, :], stats1[:, j, :]).then_inc(s_mv1, 1)

                def xn_of(f):
                    dve.wait_ge(s_rstd1, f.n + 1)
                    for j in range(NT):
                        dve.tensor_scalar(xn[:, j, :], h_rows[:, f.p, j, :], mv1[:, j, 0:1], rstd1[:, j:j + 1],
                                          ALU.subtract, ALU.mult).then_inc(s_xn, 1)

                def xn_lo_of(f):
                    for c in range(KD):
                        dve.wait_ge(s_xnt, KD * f.n + c + 1)
                        dve.tensor_tensor(xn_lo[:, c, :], fb[c][:, 0:GT], xn_hi[:, c, :].bitcast(f32),
                                          ALU.subtract).then_inc(s_xnl, 1)

                def conv_of(f, pair, lags):
                    for lag in lags:
                        for e in range(2):
                            k = 2 * pair + e
                            w = conv_t[:, k, TAPS - 1 - lag:TAPS - lag]
                            if lag == 1:
                                dve.wait_ge(s_xm, KI * f.n + k + 1)
                            else:
                                dve.wait_ge(s_conv, CONV * f.n + CONV // 2 * pair + 2 * (lag - 2) + e + 1)
                            dve.scalar_tensor_tensor(y[:, k, :, lag:], xm[:, f.p, k, :, 0:S - lag], w,
                                                     y[:, k, :, lag:], ALU.mult, ALU.add).then_inc(s_conv, 1)

                def silu_z_of(f, k):
                    dve.wait_ge(s_tz, KI * f.n + k + 1)
                    dve.scalar_tensor_tensor(silu_z[:, f.p, k, :], tanh_z[:, k, :], 1.0, fb[k % 2][:, 0:GT],
                                             ALU.add, ALU.mult).then_inc(s_sz, 1)

                def gates_of(a):
                    dve.wait_ge(s_g_mm, a.n + 1)
                    dve.tensor_tensor(gl[:], mb[1][0:R, 0:32].rearrange("p (j g) -> p j g", j=NT),
                                      gates_b[:].unsqueeze(1).broadcast_to([R, NT, 2 * NH]), ALU.add).then_inc(s_gl, 1)
                    dve.wait_ge(s_gl, a.n + 1)
                    dve.scalar_tensor_tensor(fabs[:], gl[:, :, NH:], -1.0, gl[:, :, NH:], ALU.mult,
                                             ALU.max).then_inc(s_fabs, 1)

                def log_f(a):
                    dve.wait_ge(s_fln, a.n + 1)
                    dve.scalar_tensor_tensor(logf[:], gl[:, :, NH:], 0.0, fln[:], ALU.min,
                                             ALU.subtract).then_inc(s_logf, 1)

                def a_of(a):
                    dve.wait_ge(s_f_mm, a.n + 1)
                    sums = ab[1][0:R, 0:NT * NH].rearrange("p (j h) -> p j h", j=NT)
                    dve.tensor_tensor(a_gate[:], gl[:, :, 0:NH], sums, ALU.subtract).then_inc(s_a, 1)
                    dve.tensor_copy(fsum[:], sums).then_inc(s_fsum, 1)

                def diag_of(a, j):
                    dve.wait_ge(s_a, a.n + 1)
                    dve.tensor_tensor(diag[:, j], ident[0:R, 0:R].unsqueeze(1).broadcast_to([R, NH, R]),
                                      a_gate[:, j].unsqueeze(2).broadcast_to([R, NH, R]), ALU.mult).then_inc(s_diag, 1)

                def decay(a, j):
                    n = NT * a.n + j + 1
                    dve.wait_ge(s_b_mm, n)
                    dve.tensor_reduce(minus_max[:, j, :], ab[2 * (j % 2)][0:R, 0:GT].rearrange("p (h t) -> p h t", h=NH),
                                      AX.X, ALU.max, negate=True).then_inc(s_max, 1)

                def weigh(a, j):
                    n = NT * a.n + j + 1
                    dve.wait_ge(s_dmat, NH * n)
                    dve.wait_ge(s_c_mm, n)
                    dve.tensor_tensor(cw[:, j], ab[2 * (j % 2) + 1][0:R, 0:GT].rearrange("p (h t) -> p h t", h=NH),
                                      cw[:, j], ALU.mult).then_inc(s_cw, 1)
                    dve.wait_ge(s_cw, n)
                    dve.tensor_reduce(row_sum[:, j, :], cw[:, j], AX.X, ALU.add).then_inc(s_sum, 1)

                def norm_1(a):
                    dve.wait_ge(s_max, NT * a.n + NT)
                    dve.tensor_tensor(m_d[:], minus_max[:], fsum[:], ALU.subtract).then_inc(s_md, 1)

                def norm_2(a):
                    dve.wait_ge(s_sum, NT * a.n + NT)
                    dve.wait_ge(s_expmd, a.n + 1)
                    dve.scalar_tensor_tensor(norm[:], row_sum[:], -1.0, row_sum[:], ALU.mult,
                                             ALU.max).then_inc(s_norm, 1)
                    dve.wait_ge(s_norm, 4 * a.n + 1)
                    dve.tensor_tensor(norm[:], norm[:], exp_md[:], ALU.max).then_inc(s_norm, 1)
                    dve.wait_ge(s_norm, 4 * a.n + 2)
                    dve.tensor_scalar(norm[:], norm[:], 1e-6, None, ALU.add).then_inc(s_norm, 1)
                    dve.wait_ge(s_norm, 4 * a.n + 3)
                    dve.tensor_tensor(norm2[:], norm[:], norm[:], ALU.mult).then_inc(s_norm, 1)

                def head_stats(a, j):
                    dve.wait_ge(s_o, NT * a.n + j + 1)
                    for h in range(NH):
                        dve.bn_stats(stats_h[:, j, h, :], o[:, j, h, :]).then_inc(s_sth, 1)
                    wait_apart(dve, s_sth, NT * NH * a.n + NH * j + NH)
                    for h in range(NH):
                        dve.bn_aggr(mv_h[:, j, h, :], stats_h[:, j, h, :]).then_inc(s_mvh, 1)

                def head_var(a, j):
                    dve.wait_ge(s_mvh, NT * NH * a.n + NH * j + NH)
                    if j == 0:
                        dve.wait_ge(s_norm, 4 * a.n + 4)
                    dve.scalar_tensor_tensor(var_h[:, j, :], norm2[:, j, :], 1e-6, mv_h[:, j, :, 1], ALU.mult,
                                             ALU.add).then_inc(s_varh, 1)

                def head_shift(a, j):
                    wait_apart(dve, s_rstdh, NT * a.n + j + 1)
                    dve.scalar_tensor_tensor(shift_h[:, j, :], mv_h[:, j, :, 0], -1.0, rstd_h[:, j, :],
                                             ALU.mult, ALU.mult).then_inc(s_shift, 1)

                def head_norm(a, j):
                    dve.wait_ge(s_rstdh, NT * a.n + j + 1)
                    for h in range(NH):
                        dve.tensor_scalar(o[:, j, h, :], o[:, j, h, :], mv_h[:, j, h, 0:1],
                                          rstd_h[:, j, h:h + 1], ALU.subtract, ALU.mult).then_inc(s_hn, 1)

                def state(a):
                    dve.wait_ge(s_skip, NH * a.n + NH)
                    for h in range(NH):
                        if h == 0:
                            dve.wait_ge(s_hnt_mm, a.n + 1)
                        dve.scalar_tensor_tensor(hst[:, h, :], ab[h][:, 0:GT], chan_t[:, h, 0:1], hst[:, h, :],
                                                 ALU.mult, ALU.add).then_inc(s_hmix, 1)
                        dve.wait_ge(s_hmix, NH * a.n + h + 1)
                        dve.tensor_tensor(hst[:, h, :], hst[:, h, :], silu_z[:, a.p, h, :],
                                          ALU.mult).then_inc(s_hst, 1)

                def h2_of(a):
                    for b in range(2):
                        dve.wait_ge(s_at_mm, 2 * a.n + b + 1)
                        dve.tensor_tensor(h2[:, a.p, 2 * b:2 * b + 2, :],
                                          ab[2 + b][0:R, :].rearrange("p (j d) -> p j d", j=2),
                                          h_rows[:, a.p, 2 * b:2 * b + 2, :], ALU.add).then_inc(s_h2, 1)

                def ln2_stats(m):
                    for j in range(NT):
                        if j % 2 == 0:
                            dve.wait_ge(s_h2, 2 * m.n + j // 2 + 1)
                        dve.bn_stats(stats2[:, j, :], h2[:, m.p, j, :]).then_inc(s_st2, 1)
                    for j in range(NT):
                        wait_apart(dve, s_st2, NT * m.n + j + 1)
                        dve.bn_aggr(mv2[:, j, :], stats2[:, j, :]).then_inc(s_mv2, 1)

                def xn2_of(m):
                    dve.wait_ge(s_rstd2, m.n + 1)
                    for j in range(NT):
                        dve.tensor_scalar(xn2[:, j, :], h2[:, m.p, j, :], mv2[:, j, 0:1], rstd2[:, j:j + 1],
                                          ALU.subtract, ALU.mult).then_inc(s_xn2, 1)

                def xn2_lo_of(m):
                    for c in range(KD):
                        dve.wait_ge(s_xn2t, KD * m.n + c + 1)
                        dve.tensor_tensor(xn2_lo[:, c, :], mb[c][:, 0:GT], xn2_hi[:, c, :].bitcast(f32),
                                          ALU.subtract).then_inc(s_xn2l, 1)

                def route(m):
                    dve.wait_ge(s_rt_mm, m.n + 1)
                    dve.tensor_copy(logits[:].rearrange("p j e -> p (j e)"), mb[0][0:R, 0:NT * E]).then_inc(s_lgt, 1)
                    wait_apart(dve, s_lgt, m.n + 1)
                    for j in range(NT):
                        dve.max(top[:, j, :], logits[:, j, :]).then_inc(s_top, 1)
                    for j in range(NT):
                        wait_apart(dve, s_top, NT * m.n + j + 1)
                        dve.max_index(top_i[:, j, :], top[:, j, :], logits[:, j, :]).then_inc(s_topi, 1)
                    dve.wait_ge(s_topi, NT * m.n + NT)
                    dve.tensor_copy(top_f[:], top_i[:, :, 0]).then_inc(s_topf, 1)
                    dve.wait_ge(s_topf, m.n + 1)
                    for j in range(NT):
                        dve.tensor_scalar(hot[:, bass.ds(NT * m.n + j, 1), :], iota_e[:].unsqueeze(1),
                                          top_f[:, j:j + 1], None, ALU.is_equal).then_inc(s_hot, 1)

                def score_of(m):
                    dve.wait_ge(s_ts, m.n + 1)
                    dve.tensor_scalar(score[:], tanh_s[:], 1.0, 0.5, ALU.add, ALU.mult).then_inc(s_score, 1)

                def expert_act(m, k):
                    dve.wait_ge(s_tg, KI * m.n + k + 1)
                    dve.scalar_tensor_tensor(silu_g[:, k % 2, :], tanh_g[:, k % 2, :], 1.0, mb[0][:, 0:GT],
                                             ALU.add, ALU.mult).then_inc(s_sg, 1)
                    dve.wait_ge(s_sg, KI * m.n + k + 1)
                    dve.wait_ge(s_gu_mm, 2 * KI * m.n + 2 * k + 2)
                    dve.tensor_tensor(act_t[:, k, :], silu_g[:, k % 2, :], mb[1][:, 0:GT], ALU.mult).then_inc(s_act, 1)

                def base_of(m):
                    dve.wait_ge(s_base_out, 16 * m.n + 16)
                    for b in range(2):
                        dve.wait_ge(s_ft_mm, 2 * m.n + b + 1)
                        dve.tensor_tensor(base_rows[:, 2 * b:2 * b + 2, :],
                                          mb[b][0:R, :].rearrange("p (j d) -> p j d", j=2),
                                          h2[:, m.p, 2 * b:2 * b + 2, :], ALU.add).then_inc(s_base, 1)

                def step(e, f, a, m):
                    if f and isinstance(f.n, int) and f.n == 0:
                        halve_front()
                        merge_weights()
                    if m: ln2_stats(m)
                    if f:
                        ln1_stats(f)
                        xn_of(f)
                    if a: gates_of(a)
                    if m: xn2_of(m)
                    if a: log_f(a)
                    if f: xn_lo_of(f)
                    if a:
                        a_of(a)
                        diag_of(a, 0)
                        diag_of(a, 1)
                    if m: xn2_lo_of(m)
                    if a:
                        diag_of(a, 2)
                        diag_of(a, 3)
                        decay(a, 0)
                    if f: conv_of(f, 0, (1,))
                    if a:
                        decay(a, 1)
                        weigh(a, 0)
                        weigh(a, 1)
                        decay(a, 2)
                    if m: route(m)
                    if a: decay(a, 3)
                    if m: expert_act(m, 0)
                    if final(e, f, a):
                        sort.sum_tiles(dve)
                        sort.count_slots(dve)
                    if f: conv_of(f, 0, (2,))
                    if a:
                        norm_1(a)
                        weigh(a, 2)
                        weigh(a, 3)
                    if m: expert_act(m, 1)
                    if final(e, f, a):
                        sort.first_rows(dve)
                    if a: norm_2(a)
                    if f:
                        conv_of(f, 0, (3,))
                        conv_of(f, 1, (1,))
                        conv_of(f, 1, (2, 3))
                        silu_z_of(f, 0)
                    if a:
                        head_stats(a, 0)
                        head_var(a, 0)
                    if m: expert_act(m, 2)
                    if final(e, f, a):
                        sort.add_ranks(dve)
                    if a:
                        head_stats(a, 1)
                        head_var(a, 1)
                        head_shift(a, 0)
                    if f: silu_z_of(f, 1)
                    if m: expert_act(m, 3)
                    if final(e, f, a): sort.split_place(dve)
                    if a:
                        head_stats(a, 2)
                        head_var(a, 2)
                        head_shift(a, 1)
                        head_stats(a, 3)
                        head_var(a, 3)
                    if f: silu_z_of(f, 2)
                    if a: head_norm(a, 2)
                    if f: silu_z_of(f, 3)
                    if a: head_norm(a, 3)
                    if m:
                        score_of(m)
                        base_of(m)
                    if a: state(a)
                    if e: embed(e)
                    if a: h2_of(a)

                pipeline(dve, step)

            @block.tensor
            def _(pe):
                pe.wait_ge(s_const, 13)
                pe.wait_ge(s_w_emb, 3 * 16)

                def merge_weights():
                    pe.wait_ge(s_w_att, 6 * 16)
                    for h in range(NH):
                        last = pe.matmul(ab[0][:, h * 128:(h + 1) * 128], q_raw[:, h], k_raw[:, h],
                                         start=True, stop=True)
                    last.then_inc(s_prep_mm, 1)
                    for h in range(NH):
                        pe.matmul(ab[1][:, 8 * h:8 * h + 8], q_raw[:, h], g_raw[:, 0, h], start=True, stop=False)
                        pe.matmul(ab[1][:, 8 * h:8 * h + 8], k_raw[:, h], g_raw[:, 1, h], start=False, stop=True)
                    for h in range(NH):
                        last = pe.matmul(ab[1][:, 32 + 8 * h:40 + 8 * h], v_raw[:, h], g_raw[:, 2, h],
                                         start=True, stop=True)
                    last.then_inc(s_prep_mm, 1)
                    pe.wait_ge(s_prep, 14)

                def embed(f, c):
                    if c == 0:
                        pe.wait_ge(s_patch, 16 * f.n + 16)
                    wait(pe, s_sz, KI * f.n - 1 + c)
                    for k in range(KF):
                        last = pe.matmul(fb[c][:, 0:GS * N], lin_w[:, k, c * 128:(c + 1) * 128],
                                         patch[:, k, :], start=(k == 0), stop=(k == KF - 1))
                    last.then_inc(s_emb_mm, 1)

                def to_rows(dst, src, done):
                    for b in range(2):
                        for j in (2 * b, 2 * b + 1):
                            for c in range(KD):
                                last = pe.transpose(dst[b][0:R, (j % 2) * D + c * 128:(j % 2) * D + (c + 1) * 128],
                                                    src[:, c, j * R:(j + 1) * R], ident[:])
                        last.then_inc(done, 1)

                def h_rows_of(f):
                    pe.wait_ge(s_ht, KD * f.n + KD)
                    to_rows(fb, h_t[:].rearrange("p c s t -> p c (s t)"), s_h_mm)

                def to_columns(dst, src, ready, n, done, a=None):
                    for c in range(KD):
                        if a and c == 1:
                            pe.wait_ge(s_gl, a.n + 1)
                        for j in range(NT):
                            if c == 0:
                                pe.wait_ge(ready, NT * n + j + 1)
                            last = pe.transpose(dst[c][:, j * R:(j + 1) * R], src[:, j, c * 128:(c + 1) * 128],
                                                ident[0:R, 0:R])
                        last.then_inc(done, 1)

                def split_product(dst, weights, x, at):
                    n = 0
                    for w, part in ((0, 0), (1, 0), (0, 1)):
                        for c in range(KD):
                            last = pe.matmul(dst, weights[w][:, c, at:at + 128], x[part][:, c, :],
                                             start=(n == 0), stop=(n == 3 * KD - 1))
                            n += 1
                    return last

                def up(f, k):
                    if k < 2:
                        pe.wait_ge(s_xnl, KD * f.n + KD)
                    elif k < 2 + KI:
                        pe.wait_ge(s_xm, KI * f.n + k - 1)
                    else:
                        pe.wait_ge(s_sz, KI * f.n + k - KI - 1)
                    split_product(fb[k % 2][:, 0:GT], (up_hi, up_lo), (xn_hi, xn_lo), k * 128).then_inc(s_up_mm, 1)

                def q_of(a):
                    pe.wait_ge(s_xact, KI * a.n + KI)
                    for h in range(NH):
                        if h < 2:
                            wait(pe, s_att, KD * a.n)
                        else:
                            wait(pe, s_h2, 2 * a.n)
                        pe.matmul(ab[h][:, 0:GT], score_w[:, h], x_act[:, a.p, h, :],
                                  start=True, stop=True).then_inc(s_q_mm, 1)

                def xm_tile(a, h, j):
                    return xm[:, a.p, h, TS * j:TS * j + TS, :].rearrange("p s t -> p (s t)")

                def v_of(a, j):
                    pe.wait_ge(s_q, NH * a.n + j + 1)
                    for h in range(NH):
                        last = pe.matmul(ab[j][0:R, h * 128:(h + 1) * 128], xm_tile(a, h, j), v_w[:, h],
                                         start=True, stop=True)
                    last.then_inc(s_v_mm, 1)

                def gates_of(a, j):
                    if j == 0:
                        wait(pe, s_h2, 2 * a.n)
                    dst = mb[1][0:R, 8 * j:8 * j + 8]
                    for h in range(NH):
                        pe.matmul(dst, x_act[:, a.p, h, j * R:(j + 1) * R], gx_w[:, h], start=(h == 0), stop=False)
                    for h in range(NH):
                        last = pe.matmul(dst, xm_tile(a, h, j), gm_w[:, h], start=False, stop=(h == NH - 1))
                    if j == NT - 1:
                        last.then_inc(s_g_mm, 1)

                def f_sums(a):
                    pe.wait_ge(s_v, NT * a.n + 2)
                    pe.wait_ge(s_logf, a.n + 1)
                    pe.matmul(ab[1][0:R, 0:NT * NH], tri[:], logf[:].rearrange("p j h -> p (j h)"),
                              start=True, stop=True).then_inc(s_f_mm, 1)

                def scores(a, j):
                    pe.wait_ge(s_diag, NT * a.n + j + 1)
                    if j == 0:
                        pe.wait_ge(s_fsum, a.n + 1)
                    elif j == 1:
                        pe.wait_ge(s_v, NT * a.n + NT)
                    else:
                        pe.wait_ge(s_cw, NT * a.n + j - 1)
                    b = 2 * (j % 2)
                    pe.matmul(ab[b][0:R, 0:GT], ident_bf[:], mask_bf[:].unsqueeze(1).broadcast_to([R, NH, R]),
                              start=True, stop=False)
                    pe.matmul(ab[b][0:R, 0:GT], ones[0:R, 0:R], diag[:, j].rearrange("p h t -> p (h t)"),
                              start=False, stop=True).then_inc(s_b_mm, 1)
                    for h in range(NH):
                        last = pe.matmul(ab[b + 1][0:R, h * R:(h + 1) * R], q_t[:, h, j * R:(j + 1) * R],
                                         x_act[:, a.p, h, j * R:(j + 1) * R], start=True, stop=True)
                    last.then_inc(s_c_mm, 1)

                def cw_t_of(a, j):
                    pe.wait_ge(s_cw, NT * a.n + (NT if j > 1 else NT - 1))
                    for h in range(NH):
                        last = pe.transpose(ab[j][0:R, h * R:(h + 1) * R], cw[:, j, h, :], ident[0:R, 0:R])
                    last.then_inc(s_ct_mm, 1)

                def heads(a, j):
                    pe.wait_ge(s_ct, NT * a.n + j + 1)
                    for h in range(NH):
                        last = pe.matmul(ab[j][0:R, h * 128:(h + 1) * 128], cw_t[:, j, h * R:(h + 1) * R],
                                         v[:, j, h * 128:(h + 1) * 128], start=True, stop=True)
                    last.then_inc(s_pv_mm, 1)

                def heads_t(a):
                    pe.wait_ge(s_o, NT * a.n + NT)
                    for j in range(NT):
                        pe.wait_ge(s_hn_act if j < 2 else s_hn, NT * NH // 2 * a.n + NH * (j % 2 + 1))
                        for h in range(NH):
                            last = pe.transpose(ab[h][:, j * R:(j + 1) * R], o[:, j, h, :], ident[0:R, 0:R])
                    last.then_inc(s_hnt_mm, 1)

                def down(a):
                    for k in range(KI):
                        pe.wait_ge(s_hst, KI * a.n + k + 1)
                        if k == 0:
                            pe.wait_ge(s_hmix, KI * a.n + KD)
                        for c in range(KD):
                            last = pe.matmul(ab[c][:, 0:GT], down_w[:, k, c * 128:(c + 1) * 128], hst[:, k, :],
                                             start=(k == 0), stop=(k == KI - 1))
                            if k == KI - 1:
                                last.then_inc(s_wd_mm, 1)

                def att_rows(a):
                    pe.wait_ge(s_att, KD * a.n + KD)
                    to_rows(ab[2:4], att_t, s_at_mm)

                def route(m):
                    pe.wait_ge(s_xn2l, KD * m.n + KD)
                    for j in range(NT):
                        n = 0
                        for part in (xn2_hi, xn2_lo):
                            for c in range(KD):
                                last = pe.matmul(mb[0][0:R, j * E:(j + 1) * E],
                                                 part[:, c, j * R:(j + 1) * R].bitcast(f32),
                                                 route_w[:, c], start=(n == 0), stop=(n == 2 * KD - 1))
                                n += 1
                    last.then_inc(s_rt_mm, 1)

                def gate_up(m, k):
                    if k == 0:
                        pe.wait_ge(s_lgt, m.n + 1)
                    else:
                        pe.wait_ge(s_sg, KI * m.n + k)
                    for u in range(2):
                        if u and k:
                            pe.wait_ge(s_act, KI * m.n + k)
                        at = u * I + k * 128
                        split_product(mb[u][:, 0:GT], (sgu_hi, sgu_lo), (xn2_hi, xn2_lo), at).then_inc(s_gu_mm, 1)

                def shared_down(m):
                    pe.wait_ge(s_act, KI * m.n + KI)
                    for c in range(KD):
                        for k in range(KI):
                            last = pe.matmul(mb[c][:, 0:GT], sd_w[:, k, c * 128:(c + 1) * 128], act_t[:, k, :],
                                             start=(k == 0), stop=(k == KI - 1))
                        last.then_inc(s_sd_mm, 1)

                def ffn_rows(m):
                    pe.wait_ge(s_ffn, KD * m.n + KD)
                    to_rows(mb, ffn_t, s_ft_mm)

                def step(e, f, a, m):
                    if f and isinstance(f.n, int) and f.n == 0:
                        merge_weights()
                    if a:
                        q_of(a)
                        gates_of(a, 0)
                    if f: h_rows_of(f)
                    if a:
                        gates_of(a, 1)
                        v_of(a, 0)
                        gates_of(a, 2)
                        v_of(a, 1)
                        gates_of(a, 3)
                        v_of(a, 2)
                        v_of(a, 3)
                    if f: to_columns(fb, xn, s_xn, f.n, s_xnt_mm)
                    if m: to_columns(mb, xn2, s_xn2, m.n, s_xn2t_mm, a)
                    if f: up(f, 0)
                    if a: f_sums(a)
                    if f:
                        up(f, 1)
                        up(f, 2)
                    if a: scores(a, 0)
                    if f: up(f, 3)
                    if a: scores(a, 1)
                    if m: route(m)
                    if a: scores(a, 2)
                    if m: gate_up(m, 0)
                    if final(e, f, a): sort.count(pe, s_hot)
                    if a: scores(a, 3)
                    if m: gate_up(m, 1)
                    if final(e, f, a): sort.slot_table(pe)
                    if f: up(f, 4)
                    if a:
                        cw_t_of(a, 0)
                        cw_t_of(a, 1)
                        heads(a, 0)
                        heads(a, 1)
                    if m: gate_up(m, 2)
                    if a:
                        cw_t_of(a, 2)
                        cw_t_of(a, 3)
                    if f: up(f, 5)
                    if a:
                        heads(a, 2)
                        heads(a, 3)
                    if m: gate_up(m, 3)
                    if f:
                        up(f, 6)
                        up(f, 7)
                    if m: shared_down(m)
                    if e: embed(e, 0)
                    if m: ffn_rows(m)
                    if a: heads_t(a)
                    if e: embed(e, 1)
                    if a:
                        down(a)
                        att_rows(a)

                pipeline(pe, step)


class Sort:

    def __init__(self, ctx, nc, hot, banks):
        f32, i32, bf16 = (mybir.dt.float32, mybir.dt.int32, mybir.dt.bfloat16)
        self.hot, self.banks = hot, banks
        self.steps = 0

        def sb(name, shape, dt=f32):
            return ctx.enter_context(nc.sbuf_tensor(name, shape, dt))

        def sem(name):
            return ctx.enter_context(nc.semaphore(name))

        self.ident = sb("ident", [128, 128])
        self.x_act = sb("x_act", [128, 2, KI, GT])
        self.silu_z = sb("silu_z", [128, 2, KI, GT])
        self.down_w = sb("down_w", [128, KI, D])
        self.lin_w = sb("lin_w", [128, KF, D])
        assert KD * I <= KI * GT and KF >= KI
        self.wts = [b[:].rearrange("p a k t -> p (a k t)")[:, 0:2 * KD * I] for b in (self.x_act, self.silu_z)]
        self.wts_down = [w[:, 0:KI, :].rearrange("p k d -> p (k d)") for w in (self.down_w, self.lin_w)]
        self.s_wts = [sem(f"s_wts{i}") for i in range(4)]
        self.s_wts_down = [sem(f"s_wts_down{i}") for i in range(4)]
        self.before = sb("before", [R, R], bf16)
        self.ones_bf = sb("ones_bf", [R, R], bf16)
        self.levels = sb("levels", [R, LEVELS])
        self.iota_r = sb("iota_r", [R, SLOT], bf16)
        self.tile_no = sb("tile_no", [R, TILES], bf16)
        self.row_no = sb("row_no", [R, 1])
        self.n_slots = sb("n_slots", [R, E])
        self.end_slot = sb("end_slot", [R, E])
        self.start_slot = sb("start_slot", [R, E])
        self.ended = sb("ended", [R, E])
        self.slot_e = sb("slot_e", [R, 1])
        self.iota_p = sb("iota_p", [R, 1])
        self.table = sb("table", [1, USED + 1], i32)
        self.pos_f = sb("pos_f", [R, TILES])
        self.pos_i = sb("pos_i", [R, TILES], i32)
        self.slot_i = sb("slot_i", [R, TILES], i32)
        self.row_i = sb("row_i", [R, TILES], i32)
        self.slot_f = sb("slot_f", [R, TILES], bf16)
        self.row_f = sb("row_f", [R, TILES], bf16)
        self.iota_s = sb("iota_s", [R, SLOTS], bf16)
        self.s_xs_out = sem("s_xs_out")
        self.s_base_out = sem("s_base_out")
        self.s_const2 = sem("s_const2")
        self.s_rank_mm = sem("s_rank_mm")
        self.s_tot_mm = sem("s_tot_mm")
        self.s_seq = sem("s_seq")
        self.s_table = sem("s_table")
        self.s_slot_e = sem("s_slot_e")
        self.s_slot_mm = sem("s_slot_mm")

    def borrow(self, ones, restart, total, upto, start_row, place, above):
        def view(buffer, size=E * TILES):
            return buffer[0:R].rearrange("p a b c -> p (a b c)")[:, 0:size]

        self.ones_e = ones[0:R, 0:E]
        self.restart = view(restart).rearrange("p (e t) -> p e t", e=E)
        self.total = view(total).rearrange("p (e t) -> p e t", e=E)
        self.upto = view(upto).rearrange("p (e t) -> p e t", e=E)
        self.start_row = view(start_row).rearrange("p (e t) -> p e t", e=E)
        self.above = view(above, E * LEVELS).rearrange("p (e l) -> p e l", e=E)
        self.place = view(place).rearrange("p (t e) -> p t e", e=E)

    def in_order(self, dve):
        def seq(op):
            self.steps += 1
            op.then_inc(self.s_seq, 1)
            dve.wait_ge(self.s_seq, self.steps)
        return seq

    def load(self, sp, w_exp, k, dst, at, done):
        e = sp.value_load(self.table[0:1, bass.ds(k, 1)], min_val=0, max_val=E - 1)
        sp.dma_start(dst.rearrange("p (a n) -> p a n", a=1),
                     w_exp[bass.ds(e, 1), :, at:at + dst.shape[-1]].rearrange("e p n -> p e n")).then_inc(done, 16)

    def first_loads(self, sp, w_exp):
        sp.wait_ge(self.s_table, 2)
        for i in range(2):
            self.load(sp, w_exp, i, self.wts[i], 0, self.s_wts[i])
            self.load(sp, w_exp, i, self.wts_down[i], 2 * KD * I, self.s_wts_down[i])

    def constants(self, pool):
        ALU = mybir.AluOpType
        pool.memset(self.ones_bf[:], 1.0).then_inc(self.s_const2, 1)
        pool.memset(self.before[:], 1.0).then_inc(self.s_const2, 1)
        pool.wait_ge(self.s_const2, 2)
        pool.affine_select(out=self.before[:], in_=self.before[:], compare_op=ALU.is_ge, fill=0.0,
                           base=-1, pattern=[[1, R]], channel_multiplier=-1).then_inc(self.s_const2, 1)
        pool.memset(self.restart[:], 1.0).then_inc(self.s_const2, 1)
        pool.wait_ge(self.s_const2, 4)
        pool.memset(self.restart[:, :, 0:1], 0.0).then_inc(self.s_const2, 1)
        for dst, pattern, base, cm in [(self.levels, [[SLOT, LEVELS]], 0, 0), (self.iota_s, [[1, SLOTS]], 0, 0),
                                       (self.iota_r, [[1, SLOT]], 0, 0), (self.tile_no, [[1, TILES]], 0, 0),
                                       (self.row_no, [[1, 1]], 1, 1),
                                       (self.iota_p, [[1, 1]], 0, 1)]:
            pool.iota(dst[:], pattern=pattern, base=base, channel_multiplier=cm,
                      allow_small_or_imprecise_dtypes=True).then_inc(self.s_const2, 1)

    def sum_tiles(self, dve):
        ALU, AX, seq = mybir.AluOpType, mybir.AxisListType, self.in_order(dve)
        dve.wait_ge(self.s_tot_mm, 1)
        for i in range(2):
            op = dve.tensor_copy(self.total[:, :, i * HALF:(i + 1) * HALF],
                                 self.banks[2 + i][0:R, :].rearrange("p (t e) -> p e t", e=E))
            op.then_inc(self.s_seq, 1)
        self.steps += 2
        dve.wait_ge(self.s_seq, self.steps)
        dve.wait_ge(self.s_const2, 11)
        seq(dve.tensor_tensor_scan(self.upto[:].rearrange("p e t -> p (e t)"),
                                   self.restart[:].rearrange("p e t -> p (e t)"),
                                   self.total[:].rearrange("p e t -> p (e t)"), 0.0, ALU.mult, ALU.add))

    def count_slots(self, dve):
        ALU, AX, seq = mybir.AluOpType, mybir.AxisListType, self.in_order(dve)
        seq(dve.tensor_tensor(self.above[:], self.upto[:, :, TILES - 1:TILES].broadcast_to([R, E, LEVELS]),
                              self.levels[:].unsqueeze(1).broadcast_to([R, E, LEVELS]), ALU.is_gt))
        seq(dve.tensor_reduce(self.n_slots[:], self.above[:], AX.X, ALU.add))
        seq(dve.tensor_tensor_scan(self.end_slot[:], self.ones_e, self.n_slots[:], 0.0, ALU.mult, ALU.add))
        seq(dve.tensor_scalar(self.ended[:], self.end_slot[:], self.iota_p[:, 0:1], None, ALU.is_le))
        seq(dve.tensor_reduce(self.slot_e[:], self.ended[:], AX.X, ALU.add))
        dve.tensor_scalar(self.slot_e[:], self.slot_e[:], float(E - 1), None, ALU.min).then_inc(self.s_slot_e, 1)
        seq(dve.tensor_tensor(self.start_slot[:], self.end_slot[:], self.n_slots[:], ALU.subtract))
        dve.wait_ge(self.s_slot_mm, 1)
        dve.tensor_copy(self.table[:, 0:SLOTS + 2], self.banks[5][0:1, 0:SLOTS + 2]).then_inc(self.s_table, 1)
        dve.tensor_copy(self.table[:, USED:USED + 1], self.end_slot[0:1, E - 1:E]).then_inc(self.s_table, 1)
        dve.wait_ge(self.s_table, 2)

    def first_rows(self, dve):
        ALU, AX, seq = mybir.AluOpType, mybir.AxisListType, self.in_order(dve)
        seq(dve.tensor_tensor(self.upto[:], self.upto[:], self.total[:], ALU.subtract))
        seq(dve.scalar_tensor_tensor(self.start_row[:], self.start_slot[:].unsqueeze(2).broadcast_to([R, E, TILES]),
                                     float(SLOT), self.upto[:], ALU.mult, ALU.add))

    def add_ranks(self, dve):
        ALU, AX, seq = mybir.AluOpType, mybir.AxisListType, self.in_order(dve)
        dve.wait_ge(self.s_rank_mm, 1)
        for i in range(2):
            half = slice(i * HALF, (i + 1) * HALF)
            seq(dve.tensor_tensor(self.place[:, half, :], self.banks[i][0:R, :].rearrange("p (t e) -> p t e", e=E),
                                  self.start_row[:, :, half].rearrange("p e t -> p t e"), ALU.add))

    def split_place(self, dve):
        ALU, AX, seq = mybir.AluOpType, mybir.AxisListType, self.in_order(dve)
        seq(dve.tensor_tensor(self.place[:], self.place[:], self.hot[:], ALU.mult))
        seq(dve.tensor_reduce(self.pos_f[:], self.place[:], AX.X, ALU.add))
        seq(dve.tensor_copy(self.pos_i[:], self.pos_f[:]))
        seq(dve.tensor_scalar(self.slot_i[:], self.pos_i[:], SLOT.bit_length() - 1, None, ALU.arith_shift_right))
        seq(dve.tensor_scalar(self.row_i[:], self.pos_i[:], SLOT - 1, None, ALU.bitwise_and))
        seq(dve.tensor_copy(self.slot_f[:], self.slot_i[:]))
        seq(dve.tensor_copy(self.row_f[:], self.row_i[:]))

    def count(self, pe, s_hot):
        pe.wait_ge(s_hot, TILES)
        pe.wait_ge(self.s_const2, 1)
        for i in range(2):
            last = pe.matmul(self.banks[2 + i][0:R, :], self.ones_bf[:], self.hot[:, i * HALF:(i + 1) * HALF, :],
                             start=True, stop=True)
        last.then_inc(self.s_tot_mm, 1)
        pe.wait_ge(self.s_const2, 11)
        for i in range(2):
            last = pe.matmul(self.banks[i][0:R, :], self.before[:], self.hot[:, i * HALF:(i + 1) * HALF, :],
                             start=True, stop=True)
        last.then_inc(self.s_rank_mm, 1)

    def slot_table(self, pe):
        pe.wait_ge(self.s_slot_e, 1)
        pe.matmul(self.banks[5][0:1, 0:R], self.slot_e[:, 0:1], self.ident[0:R, 0:R], start=True,
                  stop=True).then_inc(self.s_slot_mm, 1)


def experts_phase(nc, w_exp, xs_dram, base_dram, out, sort, banks):
    f32, i32, u32, bf16 = (mybir.dt.float32, mybir.dt.int32, mybir.dt.uint32, mybir.dt.bfloat16)
    f32r = mybir.dt.float32r
    ALU, ACT, AX = mybir.AluOpType, mybir.ActivationFunctionType, mybir.AxisListType
    PART = 8

    with ExitStack() as ctx:
        def sb(name, shape, dt=f32):
            return ctx.enter_context(nc.sbuf_tensor(name, shape, dt))

        def sem(name):
            return ctx.enter_context(nc.semaphore(name))

        one = sb("one", [R, TILES, SLOTS], bf16)
        in_slot = sb("in_slot", [R, TILES, 2, SLOTS], bf16)
        in_row = sb("in_row", [R, TILES, SLOT], bf16)
        empty = sb("empty", [128, SLOTS])
        take_f = sb("take_f", [128, SLOTS])
        put_f = sb("put_f", [128, SLOTS])
        take = sb("take", [128, SLOTS + 8], u32)
        put = sb("put", [128, SLOTS + 8], u32)
        wts23 = sb("wts23", [128, 2, 2 * KD * I])
        wts_down23 = sb("wts_down23", [128, 2, KI * D])
        wts = sort.wts + [wts23[:, i, :] for i in range(2)]
        wts_down = sort.wts_down + [wts_down23[:, i, :] for i in range(2)]
        take_i = sb("take_i", [128, 4], u32)
        put_i = sb("put_i", [128, 4], u32)
        xg = sb("xg", [128, 4, D])
        bg = sb("bg", [128, 4, D])
        w_hi = sb("w_hi", [128, 2, 2, KD * I], f32r)
        w_lo = sb("w_lo", [128, 2, 2, KD * I], f32r)
        x_hi = sb("x_hi", [128, 2, KD * SLOT], f32r)
        x_lo = sb("x_lo", [128, 2, KD * SLOT], f32r)
        tanh_e = sb("tanh_e", [128, 2, I])
        silu_e = sb("silu_e", [128, 2, I])
        act_e = sb("act_e", [128, 2, I])
        act_et = sb("act_et", [128, 2, KI, SLOT])
        rows = sb("rows", [128, 4, D])

        s_passed2 = sem("s_passed2")
        s_one = sem("s_one")
        s_tiles_in = sem("s_tiles_in")
        s_rows_in = sem("s_rows_in")
        s_in = sem("s_in")
        s_list_mm = sem("s_list_mm")
        s_list = sem("s_list")
        s_wts, s_wts_down = sort.s_wts, sort.s_wts_down
        s_take = sem("s_take")
        s_put = sem("s_put")
        s_x_in = [sem(f"s_x_in{i}") for i in range(4)]
        s_base_in = [sem(f"s_base_in{i}") for i in range(4)]
        s_xgt_mm = sem("s_xgt_mm")
        s_xgt = sem("s_xgt")
        s_ge_mm = sem("s_ge_mm")
        s_te = sem("s_te")
        s_se = sem("s_se")
        s_ae = sem("s_ae")
        s_aet_mm = sem("s_aet_mm")
        s_aet = sem("s_aet")
        s_y_mm = sem("s_y_mm")
        s_y = sem("s_y")
        s_out = sem("s_out")
        s_stored = sem("s_stored")
        s_w_hi = sem("s_w_hi")
        s_w_lo = sem("s_w_lo")
        s_x_lo = sem("s_x_lo")
        s_pad = sem("s_pad")
        CREDIT = 4

        def wait_apart(eng, semaphore, value):
            eng.wait_ge(semaphore, value)
            if not isinstance(value, int):
                eng.sem_inc(s_passed2, 1)

        def slots_in_use(eng):
            eng.wait_ge(sort.s_table, 2)
            return eng.value_load(sort.table[0:1, USED:USED + 1], min_val=1, max_val=SLOTS)

        def slots(eng, front, turn, last):
            used = slots_in_use(eng)
            front(0, 0)
            turn(0, 0)
            turn(1, 1)
            with eng.If(used < 3):
                last(1, 1)
            with eng.Fori(0, SLOTS // 4) as t:
                with eng.If(used > 4 * t + 2):
                    turn(4 * t + 2, 2)
                    turn(4 * t + 3, 3)
                    with eng.If(used < 4 * t + 5):
                        last(4 * t + 3, 3)
                    with eng.If(used > 4 * t + 4):
                        turn(4 * t + 4, 0)
                        turn(4 * t + 5, 1)
                        with eng.If(used < 4 * t + 7):
                            last(4 * t + 5, 1)

        with nc.Block() as block:

            @block.sync
            def _(sp):
                used = slots_in_use(sp)

                def load_gate_up(k, i):
                    sp.wait_ge(s_w_lo, 2 * k + 2)
                    sort.load(sp, w_exp, k, wts[i], 0, s_wts[i])

                def load_down(k, i):
                    sp.wait_ge(s_y_mm, k + 1)
                    sort.load(sp, w_exp, k, wts_down[i], 2 * KD * I, s_wts_down[i])

                for i in (2, 3):
                    load_gate_up(i, i)
                with sp.Fori(0, SLOTS // 4) as t:
                    for first in (4, 6):
                        with sp.If(used + 2 > 4 * t + first):
                            for i in (first, first + 1):
                                load_down(4 * t + i - 2, (i - 2) % 4)
                                load_gate_up(4 * t + i, i % 4)

            @block.gpsimd
            def _(pool):
                pool.sem_inc(s_stored, CREDIT)

                pool.memset(take[:, SLOTS:], 0).then_inc(s_pad, 1)
                for t in range(0, TILES, PART):
                    part = slice(t, t + PART)
                    pool.wait_ge(s_one, t // PART + 1)
                    pool.tensor_tensor(in_slot[:, part, 0, :], one[:, part, :],
                                       sort.tile_no[:, part].unsqueeze(2).broadcast_to([R, PART, SLOTS]),
                                       ALU.mult).then_inc(s_tiles_in, 1)
                pool.wait_ge(sort.s_xs_out, 16 * G + 16)
                pool.wait_ge(sort.s_base_out, 16 * G + 16)
                pool.wait_ge(s_list, 2)
                pool.wait_ge(s_pad, 1)

                def gather(rows_of, dst, i, done):
                    pool.indirect_dma_start(dst[:, i, :], None, rows_of,
                                            bass.IndirectOffsetOnAxis(ap=take_i[:, i:i + 1], axis=0)
                                            ).then_inc(done[i], 16)

                def gather_x(k, i):
                    pool.tensor_copy(take_i[:, i:i + 1], take[:, bass.ds(k, 1)]).then_inc(s_take, 1)
                    wait_apart(pool, s_take, k + 1)
                    gather(xs_dram, xg, i, s_x_in)

                def scatter(k, i):
                    pool.wait_ge(s_y, k + 3)
                    pool.tensor_copy(put_i[:, i:i + 1], put[:, bass.ds(k, 1)]).then_inc(s_put, 1)
                    wait_apart(pool, s_put, k + 1)
                    pool.indirect_dma_start(out, bass.IndirectOffsetOnAxis(ap=put_i[:, i:i + 1], axis=0),
                                            rows[:, i, :], None, bounds_check=T - 1,
                                            oob_is_err=False).then_inc(s_out, 16)

                def stored(k):
                    pool.wait_ge(s_out, 16 * k + 16)
                    pool.sem_inc(s_stored, 1)

                def front(k, i):
                    for ahead in range(4):
                        gather_x(k + ahead, i + ahead)
                        if ahead < 3:
                            gather(base_dram, bg, i + ahead, s_base_in)

                def turn(k, i):
                    pool.wait_ge(s_xgt_mm, k + 1)
                    pool.wait_ge(s_base_in[i], 4 * (k - i) + 16)
                    gather_x(k + 4, i)
                    if not (isinstance(k, int) and k < 2):
                        stored(k - 2)
                    if not (isinstance(k, int) and k == 0):
                        scatter(k - 1, (i + 3) % 4)
                    gather(base_dram, bg, (i + 3) % 4, s_base_in)

                def last(k, i):
                    stored(k - 1)
                    scatter(k, i)
                    stored(k)

                slots(pool, front, turn, last)

            @block.vector
            def _(dve):
                seq = sort.in_order(dve)
                dve.sem_inc(s_y, 2)
                dve.sem_inc(s_w_lo, 2 * CREDIT)
                for t in range(0, TILES, PART):
                    part = slice(t, t + PART)
                    dve.tensor_tensor(one[:, part, :], sort.iota_s[:].unsqueeze(1).broadcast_to([R, PART, SLOTS]),
                                      sort.slot_f[:, part].unsqueeze(2).broadcast_to([R, PART, SLOTS]),
                                      ALU.is_equal).then_inc(s_one, 1)
                    dve.tensor_tensor(in_row[:, part, :], sort.iota_r[:].unsqueeze(1).broadcast_to([R, PART, SLOT]),
                                      sort.row_f[:, part].unsqueeze(2).broadcast_to([R, PART, SLOT]),
                                      ALU.is_equal).then_inc(s_in, 1)
                dve.wait_ge(s_list_mm, 1)
                rows1 = banks[4][:, SLOTS:2 * SLOTS]
                seq(dve.tensor_copy(take_f[:], rows1))
                seq(dve.scalar_tensor_tensor(take_f[:], banks[4][:, 0:SLOTS], float(R), take_f[:], ALU.mult, ALU.add))
                seq(dve.tensor_scalar(empty[:], rows1, 0.5, NOWHERE, ALU.is_lt, ALU.mult))
                seq(dve.tensor_scalar(take_f[:], take_f[:], -1.0, 0.0, ALU.add, ALU.max))
                seq(dve.tensor_tensor(put_f[:], take_f[:], empty[:], ALU.add))
                dve.tensor_copy(take[:, 0:SLOTS], take_f[:]).then_inc(s_list, 1)
                dve.tensor_copy(put[:, 0:SLOTS], put_f[:]).then_inc(s_list, 1)

                def rows_of(k, i):
                    dve.wait_ge(s_y_mm, k + 1 + CREDIT)
                    dve.wait_ge(s_stored, k + 1)
                    dve.wait_ge(s_base_in[i], 4 * (k - i) + 16)
                    dve.scalar_tensor_tensor(rows[:, i, :], banks[i % 2][:, 0:D], 0.5, bg[:, i, :],
                                             ALU.mult, ALU.add).then_inc(s_y, 1)

                def w_lo_of(k, i, u):
                    dve.wait_ge(s_w_hi, 2 * k + u + 1)
                    dve.tensor_tensor(w_lo[:, i % 2, u, :], wts[i][:, u * KD * I:(u + 1) * KD * I],
                                      w_hi[:, i % 2, u, :].bitcast(f32), ALU.subtract).then_inc(s_w_lo, 1)

                def x_lo_of(k, i):
                    e = i % 2
                    dve.wait_ge(s_xgt, k + 1)
                    dve.tensor_tensor(x_lo[:, e, :], banks[7][:, e * D:(e + 1) * D], x_hi[:, e, :].bitcast(f32),
                                      ALU.subtract).then_inc(s_x_lo, 1)

                def front(k, i):
                    w_lo_of(k, i, 0)
                    x_lo_of(k, i)
                    w_lo_of(k, i, 1)
                    w_lo_of(k + 1, i + 1, 0)

                def turn(k, i):
                    e = i % 2
                    dve.wait_ge(s_te, k + 1)
                    dve.scalar_tensor_tensor(silu_e[:, e, :], tanh_e[:, e, :], 1.0, banks[2 + 2 * e][:, :],
                                             ALU.add, ALU.mult).then_inc(s_se, 1)
                    dve.wait_ge(s_se, k + 1)
                    dve.wait_ge(s_ge_mm, 2 * k + 2)
                    dve.tensor_tensor(act_e[:, e, :], silu_e[:, e, :], banks[3 + 2 * e][:, :],
                                      ALU.mult).then_inc(s_ae, 1)
                    x_lo_of(k + 1, (i + 1) % 4)
                    if not (isinstance(k, int) and k == 0):
                        rows_of(k - 1, (i + 3) % 4)
                    w_lo_of(k + 1, (i + 1) % 4, 1)
                    w_lo_of(k + 2, (i + 2) % 4, 0)

                slots(dve, front, turn, rows_of)

            @block.scalar
            def _(act):
                for t in range(0, TILES, PART):
                    part = slice(t, t + PART)
                    act.wait_ge(s_one, t // PART + 1)
                    act.activation(in_slot[:, part, 1, :], one[:, part, :], ACT.Copy,
                                   scale=sort.row_no[:, 0:1]).then_inc(s_rows_in, 1)

                def x_of(k, i):
                    e = i % 2
                    act.wait_ge(s_xgt_mm, k + 1)
                    act.activation(x_hi[:, e, :], banks[7][:, e * D:(e + 1) * D], ACT.Copy).then_inc(s_xgt, 1)

                def w_hi_of(k, i, u):
                    if u == 0:
                        act.wait_ge(s_wts[i], 4 * (k - i) + 16)
                    act.activation(w_hi[:, i % 2, u, :], wts[i][:, u * KD * I:(u + 1) * KD * I],
                                   ACT.Copy).then_inc(s_w_hi, 1)

                def act_of(k, i):
                    act.wait_ge(s_aet_mm, k + 1)
                    act.activation(act_et[:, i % 2].rearrange("p c n -> p (c n)"), banks[6][:, :],
                                   ACT.Copy).then_inc(s_aet, 1)

                def front(k, i):
                    w_hi_of(k, i, 0)
                    x_of(k, i)
                    w_hi_of(k, i, 1)
                    w_hi_of(k + 1, i + 1, 0)

                def turn(k, i):
                    e = i % 2
                    act.wait_ge(s_ge_mm, 2 * k + 1)
                    act.activation(tanh_e[:, e, :], banks[2 + 2 * e][:, :], ACT.Tanh, scale=0.5).then_inc(s_te, 1)
                    if not (isinstance(k, int) and k == 0):
                        act_of(k - 1, (i + 3) % 4)
                    x_of(k + 1, (i + 1) % 4)
                    w_hi_of(k + 1, (i + 1) % 4, 1)
                    w_hi_of(k + 2, (i + 2) % 4, 0)

                slots(act, front, turn, act_of)

            @block.tensor
            def _(pe):
                pe.sem_inc(s_y_mm, CREDIT)
                for t in range(TILES):
                    if t % PART == 0:
                        pe.wait_ge(s_in, t // PART + 1)
                        pe.wait_ge(s_tiles_in, t // PART + 1)
                        pe.wait_ge(s_rows_in, t // PART + 1)
                    last = pe.matmul(banks[4][:, 0:2 * SLOTS], in_row[:, t, :],
                                     in_slot[:, t].rearrange("p d n -> p (d n)"),
                                     start=(t == 0), stop=(t == TILES - 1))
                last.then_inc(s_list_mm, 1)
                pe.wait_ge(s_list, 2)

                def x_of(k, i):
                    pe.wait_ge(s_x_in[i], 4 * (k - i) + 16)
                    for c in range(KD):
                        last = pe.transpose(banks[7][:, (i % 2) * D + c * 128:(i % 2) * D + (c + 1) * 128],
                                            xg[:, i, c * 128:(c + 1) * 128], sort.ident[:])
                    last.then_inc(s_xgt_mm, 1)

                def gate_up(k, i, u):
                    e = i % 2
                    pe.wait_ge(s_w_lo, 2 * (k + CREDIT) + u + 1)
                    n = 0
                    for x, w in ((x_hi, w_hi), (x_hi, w_lo), (x_lo, w_hi)):
                        for c in range(KD):
                            last = pe.matmul(banks[2 + 2 * e + u][:, :], x[:, e, c * SLOT:(c + 1) * SLOT],
                                             w[:, e, u, c * I:(c + 1) * I], start=(n == 0), stop=(n == 3 * KD - 1))
                            n += 1
                    last.then_inc(s_ge_mm, 1)

                def act_t_of(k, i):
                    pe.wait_ge(s_ae, k + 1)
                    for c in range(KI):
                        last = pe.transpose(banks[6][:, c * 128:(c + 1) * 128],
                                            act_e[:, i % 2, c * 128:(c + 1) * 128], sort.ident[:])
                    last.then_inc(s_aet_mm, 1)

                def down(k, i):
                    pe.wait_ge(s_wts_down[i], 4 * (k - i) + 16)
                    pe.wait_ge(s_aet, k + 1)
                    pe.wait_ge(s_y, k + 1)
                    for c in range(KI):
                        last = pe.matmul(banks[i % 2][:, 0:D], act_et[:, i % 2, c, :],
                                         wts_down[i][:, c * D:(c + 1) * D], start=(c == 0), stop=(c == KI - 1))
                    last.then_inc(s_y_mm, 1)

                def turn(k, i):
                    first = isinstance(k, int) and k == 0
                    pe.wait_ge(s_x_lo, k + 1)
                    gate_up(k, i, 0)
                    if not first:
                        act_t_of(k - 1, (i + 3) % 4)
                    gate_up(k, i, 1)
                    x_of(k + 1, (i + 1) % 4)
                    if not first:
                        down(k - 1, (i + 3) % 4)

                def last(k, i):
                    act_t_of(k, i)
                    down(k, i)

                slots(pe, x_of, turn, last)


def vit_tower(nc, patches, w_lin, pos, cols, w_up, conv, chan, wq, wk, wv, wvt, w_gates, b_gates,
              w_down, w_route, w_sgu, w_sd, w_exp, out):
    xs_dram = nc.dram_tensor("xs_rows_dram", (T, D), mybir.dt.float32).ap()
    base_dram = nc.dram_tensor("base_rows_dram", (T, D), mybir.dt.float32).ap()
    with ExitStack() as ctx:
        hot = ctx.enter_context(nc.sbuf_tensor("hot", [R, TILES, E], mybir.dt.bfloat16))
        banks = [ctx.enter_context(nc.psum_tensor(f"bank{i}", [128, 512], mybir.dt.float32)) for i in range(8)]
        sort = Sort(ctx, nc, hot, banks)
        groups_phase(nc, patches, w_lin, pos, cols, w_up, conv, chan, wq, wk, wv, wvt, w_gates, b_gates,
                     w_down, w_route, w_sgu, w_sd, xs_dram, base_dram, hot, banks, sort, w_exp)
        experts_phase(nc, w_exp, xs_dram, base_dram, out, sort, banks)


def _block_diagonal(w, transposed=False):
    d = np.zeros((KI, 128, 128), w.dtype)
    for c in range(KI):
        for i in range(128 // PD):
            d[c, PD * i:PD * i + PD, PD * i:PD * i + PD] = w[(128 // PD) * c + i]
    return d.transpose(2, 0, 1) if transposed else d.transpose(1, 0, 2)


def _chunks(w):
    return w.reshape(-1, 128, w.shape[-1]).transpose(1, 0, 2)


def kernel(**inputs):
    import concourse.bacc as bacc
    from concourse.bass_utils import run_bass_kernel_spmd

    a = {k: np.asarray(v) for k, v in inputs.items()}
    L = "L0_"
    x = a["x"].reshape(G, GS, C, HP, P, HP, P).transpose(0, 2, 4, 6, 1, 3, 5).reshape(G, KF, 128, GS * N)
    ig, fg = a[L + "attn_W_ig"], a[L + "attn_W_fg"]
    gates = np.concatenate([ig, fg], 1).reshape(3, KI, 128, 2 * NH)
    laid = {
        "patches": x.transpose(0, 2, 1, 3).reshape(G, 128, KF * GS * N),
        "w_lin": _chunks(a[L + "tok_W_lin"].T),
        "pos": _chunks(a[L + "tok_position_embeddings"][0].T),
        "cols": _chunks(np.stack([a[L + "tok_b_lin"], a[L + "tok_class_token"][0, 0], a["cls_tok"][0, 0]], 1)),
        "w_up": _chunks(a[L + "attn_W_up"]),
        "conv": _chunks(np.concatenate([a[L + "attn_conv_w"], a[L + "attn_conv_b"][None]], 0).T),
        "chan": _chunks(np.stack([a[L + "attn_norm_w"], a[L + "attn_skip"]], 1)),
        "wq": _block_diagonal(a[L + "attn_Wq"]),
        "wk": _block_diagonal(a[L + "attn_Wk"]),
        "wv": _block_diagonal(a[L + "attn_Wv"]),
        "wvt": _block_diagonal(a[L + "attn_Wv"], True),
        "w_gates": gates.transpose(2, 0, 1, 3),
        "b_gates": np.concatenate([a[L + "attn_b_ig"], a[L + "attn_b_fg"]])[None],
        "w_down": _chunks(a[L + "attn_W_down"]),
        "w_route": _chunks(a[L + "ffn_gate_w"]),
        "w_sgu": _chunks(np.concatenate([a[L + "ffn_shared_gate_w"], a[L + "ffn_shared_up_w"]], 1)),
        "w_sd": _chunks(a[L + "ffn_shared_down_w"]),
        "w_exp": np.concatenate(
            [a[L + "ffn_routed_gate_w"].reshape(E, KD, 128, I).transpose(0, 2, 1, 3).reshape(E, 128, KD * I),
             a[L + "ffn_routed_up_w"].reshape(E, KD, 128, I).transpose(0, 2, 1, 3).reshape(E, 128, KD * I),
             a[L + "ffn_routed_down_w"].reshape(E, KI, 128, D).transpose(0, 2, 1, 3).reshape(E, 128, KI * D)], 2),
    }
    laid = {k: np.ascontiguousarray(v) for k, v in laid.items()}
    nc = bacc.Bacc("TRN2", target_bir_lowering=False, num_devices=1)
    args = [nc.dram_tensor(k, v.shape, mybir.dt.from_np(v.dtype), kind="ExternalInput").ap()
            for k, v in laid.items()]
    out = nc.dram_tensor("out", (T, D), mybir.dt.float32, kind="ExternalOutput").ap()
    vit_tower(nc, *args, out)
    r = run_bass_kernel_spmd(nc, [laid], core_ids=[0])
    return r.results[0]["out"].reshape(B, S, D)
```
